# Optimizing a Trainium2 kernel written in Bass

```python
import numpy as np
import jax
import jax.numpy as jnp

def _softmax(x, axis=-1):
    return jax.nn.softmax(x, axis=axis)

def _gelu(x):
    return jax.nn.gelu(x, approximate=True)

def _silu(x):
    return jax.nn.silu(x)

def _sigmoid(x):
    return jax.nn.sigmoid(x)

def _layernorm(x, axis=-1, eps=1e-05):
    m = jnp.mean(x, axis=axis, keepdims=True)
    v = jnp.var(x, axis=axis, keepdims=True)
    return (x - m) / jnp.sqrt(v + eps)

def _scatter_add(tgt, idx, src, axis=0):
    return tgt.at[idx].add(src)

def _segment_sum(src, seg, n):
    return jax.ops.segment_sum(src, seg, n)
kernel_name = 'mk_adj_resnorm_d4_adj_r2_35c449'

def setup_inputs(seed: int=0):
    np.random.seed(seed)
    _w = jnp.asarray

    def _rec_inputs():
        import jax
        import jax.numpy as jnp
        _gk = jax.random.key(seed)
        x = -0.0003929 + 0.9999 * jax.random.normal(jax.random.fold_in(_gk, 1), (64, 128, 128), jnp.float32)
        _a = jax.random.bernoulli(jax.random.fold_in(_gk, 2), 0.03125, (128, 128))
        _a = jnp.logical_or(_a, jnp.swapaxes(_a, -1, -2))
        _a = jnp.logical_or(_a, jnp.eye(128, dtype=bool))
        _af = _a.astype(jnp.float32)
        _af = _af * jax.random.uniform(jax.random.fold_in(_gk, 3), (128, 128), jnp.float32, 0.05, 1)
        adj = _af
        return (x, adj)
    x, adj = _rec_inputs()

    def _L0_gnn_setup():
        import jax, jax.numpy as jnp
        import numpy as np
        EPS = 1e-05

        def _batchnorm(x, gamma, beta):
            mu = jnp.mean(x, axis=0)
            var = jnp.var(x, axis=0)
            return (x - mu) * jax.lax.rsqrt(var + EPS) * gamma + beta
        key = jax.random.key(seed)
        ks = jax.random.split(key, 4)
        b, n, d, h, o = (32, 1024, 128, 256, 128)
        features = jax.random.normal(ks[0], (b, n, d), dtype=jnp.float32)
        A = jax.random.uniform(ks[1], (n, n), dtype=jnp.float32)
        lim1 = float(np.sqrt(6.0 / (d + h)))
        W1 = jax.random.uniform(ks[2], (h, d), minval=-lim1, maxval=lim1, dtype=jnp.float32)
        b1 = jnp.zeros((h,), jnp.float32)
        lim2 = float(np.sqrt(6.0 / (h + o)))
        W2 = jax.random.uniform(ks[3], (o, h), minval=-lim2, maxval=lim2, dtype=jnp.float32)
        b2 = jnp.zeros((o,), jnp.float32)
        g1 = jnp.ones((h,), jnp.float32)
        be1 = jnp.zeros((h,), jnp.float32)
        g2 = jnp.ones((o,), jnp.float32)
        be2 = jnp.zeros((o,), jnp.float32)
        return {'features': features, 'A': A, 'W1': W1, 'b1': b1, 'g1': g1, 'be1': be1, 'W2': W2, 'b2': b2, 'g2': g2, 'be2': be2}
    _L0_gnn_all = _L0_gnn_setup()
    _L0_gnn_in = {k: v for k, v in _L0_gnn_all.items() if k in ('W1', 'b1', 'g1', 'be1', 'W2', 'b2', 'g2', 'be2')}
    del _L0_gnn_all

    def _L1_gnn_setup():
        import jax, jax.numpy as jnp
        import numpy as np
        B, J, F_IN, F_OUT = (8192, 17, 128, 128)
        key = jax.random.key(seed)
        k1, k2, k3, k4 = jax.random.split(key, 4)
        gain = 1.414
        bound = gain * np.sqrt(6.0 / (F_IN + F_OUT))
        W = jax.random.uniform(k2, (3, F_IN, F_OUT), dtype=jnp.float32, minval=-bound, maxval=bound)
        stdv = 1.0 / np.sqrt(F_OUT)
        bias = jax.random.uniform(k4, (F_OUT,), dtype=jnp.float32, minval=-stdv, maxval=stdv)
        return {'x': jax.random.normal(k1, (B, J, F_IN), dtype=jnp.float32), 'W': W, 'adj': jax.random.uniform(k3, (J, J), dtype=jnp.float32), 'bias': bias}
    _L1_gnn_all = _L1_gnn_setup()
    _L1_gnn_in = {k: v for k, v in _L1_gnn_all.items() if k in ('W', 'bias')}
    del _L1_gnn_all

    def _L2_gnn_setup():
        import jax, jax.numpy as jnp
        import numpy as np
        B, T, D, H = (64, 1024, 128, 128)
        MAX_SKIP = 4

        def _lstm_last(Wih, Whh, bih, bhh, xs):
            N, _, Hd = xs.shape
            bias = bih + bhh

            def step(carry, x_t):
                h, c = carry
                g = x_t @ Wih.T + h @ Whh.T + bias
                i, f, gg, o = jnp.split(g, 4, axis=-1)
                c = jax.nn.sigmoid(f) * c + jax.nn.sigmoid(i) * jnp.tanh(gg)
                h = jax.nn.sigmoid(o) * jnp.tanh(c)
                return ((h, c), None)
            init = (jnp.zeros((N, Hd), xs.dtype), jnp.zeros((N, Hd), xs.dtype))
            (h_last, _), _ = jax.lax.scan(step, init, jnp.swapaxes(xs, 0, 1))
            return h_last
        key = jax.random.key(seed)
        ks = jax.random.split(key, 8)
        s = 0.05
        x = jax.random.normal(ks[0], (B, T, D), jnp.float32)
        adj = jax.random.uniform(ks[1], (T, T), jnp.float32) / T
        Wg0 = jax.random.normal(ks[2], (D, H), jnp.float32) * s
        bg0 = jnp.zeros((H,), jnp.float32)
        Wg1 = jax.random.normal(ks[3], (H, H), jnp.float32) * s
        bg1 = jnp.zeros((H,), jnp.float32)
        Wih = jax.random.normal(ks[4], (MAX_SKIP, 4 * H, H), jnp.float32) * s
        Whh = jax.random.normal(ks[5], (MAX_SKIP, 4 * H, H), jnp.float32) * s
        bih = jax.random.normal(ks[6], (MAX_SKIP, 4 * H), jnp.float32) * s
        bhh = jax.random.normal(ks[7], (MAX_SKIP, 4 * H), jnp.float32) * s
        return dict(x=x, adj=adj, Wg0=Wg0, bg0=bg0, Wg1=Wg1, bg1=bg1, Wih=Wih, Whh=Whh, bih=bih, bhh=bhh)
    _L2_gnn_all = _L2_gnn_setup()
    _L2_gnn_in = {k: v for k, v in _L2_gnn_all.items() if k in ('Wg0', 'bg0', 'Wg1', 'bg1', 'Wih', 'Whh', 'bih', 'bhh')}
    del _L2_gnn_all

    def _L3_gnn_setup():
        import jax, jax.numpy as jnp
        import numpy as np
        BT, N, D, HEADS, E = (512, 64, 128, 4, 256)
        LRELU_SLOPE = 0.2
        EPS = 1e-08
        key = jax.random.key(seed)
        ks = jax.random.split(key, 8)
        d = D
        return {'H': jax.random.normal(ks[0], (BT, N, d), jnp.float32), 'W_lin': jax.random.normal(ks[1], (d, d), jnp.float32) / np.sqrt(d).astype(np.float32), 'W_val': jax.random.normal(ks[2], (d, d), jnp.float32) / np.sqrt(d).astype(np.float32), 'a': jax.random.normal(ks[3], (HEADS, d // HEADS), jnp.float32), 'W_out': jax.random.normal(ks[4], (d, d), jnp.float32) / np.sqrt(d).astype(np.float32), 'A0': jax.random.uniform(ks[5], (N, N), jnp.float32), 'src': jax.random.randint(ks[6], (E,), 0, N, jnp.int32), 'dst': jax.random.randint(ks[7], (E,), 0, N, jnp.int32)}
    _L3_gnn_all = _L3_gnn_setup()
    _L3_gnn_in = {k: v for k, v in _L3_gnn_all.items() if k in ('W_lin', 'W_val', 'a', 'W_out', 'src', 'dst')}
    del _L3_gnn_all
    return {'x': x, 'adj': adj, 'L0_gnn_W1': _L0_gnn_in['W1'], 'L0_gnn_b1': _L0_gnn_in['b1'], 'L0_gnn_g1': _L0_gnn_in['g1'], 'L0_gnn_be1': _L0_gnn_in['be1'], 'L0_gnn_W2': _L0_gnn_in['W2'], 'L0_gnn_b2': _L0_gnn_in['b2'], 'L0_gnn_g2': _L0_gnn_in['g2'], 'L0_gnn_be2': _L0_gnn_in['be2'], 'L1_gnn_W': _L1_gnn_in['W'], 'L1_gnn_bias': _L1_gnn_in['bias'], 'L2_gnn_Wg0': _L2_gnn_in['Wg0'], 'L2_gnn_bg0': _L2_gnn_in['bg0'], 'L2_gnn_Wg1': _L2_gnn_in['Wg1'], 'L2_gnn_bg1': _L2_gnn_in['bg1'], 'L2_gnn_Wih': _L2_gnn_in['Wih'], 'L2_gnn_Whh': _L2_gnn_in['Whh'], 'L2_gnn_bih': _L2_gnn_in['bih'], 'L2_gnn_bhh': _L2_gnn_in['bhh'], 'L3_gnn_W_lin': _L3_gnn_in['W_lin'], 'L3_gnn_W_val': _L3_gnn_in['W_val'], 'L3_gnn_a': _L3_gnn_in['a'], 'L3_gnn_W_out': _L3_gnn_in['W_out'], 'L3_gnn_src': _L3_gnn_in['src'], 'L3_gnn_dst': _L3_gnn_in['dst']}

def reference(x, adj, L0_gnn_W1, L0_gnn_b1, L0_gnn_g1, L0_gnn_be1, L0_gnn_W2, L0_gnn_b2, L0_gnn_g2, L0_gnn_be2, L1_gnn_W, L1_gnn_bias, L2_gnn_Wg0, L2_gnn_bg0, L2_gnn_Wg1, L2_gnn_bg1, L2_gnn_Wih, L2_gnn_Whh, L2_gnn_bih, L2_gnn_bhh, L3_gnn_W_lin, L3_gnn_W_val, L3_gnn_a, L3_gnn_W_out, L3_gnn_src, L3_gnn_dst):
    import jax
    import jax.numpy as jnp

    def _L0_gnn_ref(features, A, W1, b1, g1, be1, W2, b2, g2, be2):
        import jax, jax.numpy as jnp
        import numpy as np
        EPS = 1e-05

        def _batchnorm(x, gamma, beta):
            mu = jnp.mean(x, axis=0)
            var = jnp.var(x, axis=0)
            return (x - mu) * jax.lax.rsqrt(var + EPS) * gamma + beta
        b, n, d = features.shape
        A_norm = A + jnp.eye(n, dtype=A.dtype)
        deg = jnp.sum(A_norm, axis=0) + jnp.sum(A_norm, axis=1) - jnp.diagonal(A_norm)
        dinv = jax.lax.rsqrt(deg)
        A_hat = A_norm * dinv[:, None] * dinv[None, :]
        agg = jnp.einsum('nm,bmd->bnd', A_hat, features)
        x = agg.reshape(-1, d)
        h = jax.nn.relu(_batchnorm(x @ W1.T + b1, g1, be1))
        out = h @ W2.T + b2
        out = _batchnorm(out, g2, be2)
        return out.reshape(b, n, -1)

    def _L1_gnn_ref(x, W, adj, bias):
        import jax, jax.numpy as jnp
        import numpy as np
        B, J, F_IN, F_OUT = (8192, 17, 128, 128)
        adj_0 = jnp.diag(jnp.diagonal(adj))
        adj_1 = jnp.triu(adj, k=1)
        adj_2 = jnp.tril(adj, k=-1)
        h = jnp.einsum('bjf,kfo->kbjo', x, W)
        out = jnp.einsum('ij,bjo->bio', adj_0, h[0]) + jnp.einsum('ij,bjo->bio', adj_1, h[1]) + jnp.einsum('ij,bjo->bio', adj_2, h[2])
        return out + bias[None, None, :]

    def _L2_gnn_ref(x, adj, Wg0, bg0, Wg1, bg1, Wih, Whh, bih, bhh):
        import jax, jax.numpy as jnp
        import numpy as np
        B, T, D, H = (64, 1024, 128, 128)
        MAX_SKIP = 4

        def _lstm_last(Wih, Whh, bih, bhh, xs):
            N, _, Hd = xs.shape
            bias = bih + bhh

            def step(carry, x_t):
                h, c = carry
                g = x_t @ Wih.T + h @ Whh.T + bias
                i, f, gg, o = jnp.split(g, 4, axis=-1)
                c = jax.nn.sigmoid(f) * c + jax.nn.sigmoid(i) * jnp.tanh(gg)
                h = jax.nn.sigmoid(o) * jnp.tanh(c)
                return ((h, c), None)
            init = (jnp.zeros((N, Hd), xs.dtype), jnp.zeros((N, Hd), xs.dtype))
            (h_last, _), _ = jax.lax.scan(step, init, jnp.swapaxes(xs, 0, 1))
            return h_last
        h = jax.nn.relu(jnp.einsum('ts,bsh->bth', adj, x @ Wg0 + bg0))
        h = jax.nn.relu(jnp.einsum('ts,bsh->bth', adj, h @ Wg1 + bg1))
        Bv, Tv, Hd = h.shape
        for p in range(1, MAX_SKIP + 1):
            nw = Tv // p
            wins = h[:, :nw * p, :].reshape(Bv * nw, p, Hd)
            last = _lstm_last(Wih[p - 1], Whh[p - 1], bih[p - 1], bhh[p - 1], wins)
            idx = jnp.arange(nw) * p + (p - 1)
            h = h.at[:, idx, :].set(last.reshape(Bv, nw, Hd))
        return h

    def _L3_gnn_ref(H, W_lin, W_val, a, W_out, A0, src, dst):
        import jax, jax.numpy as jnp
        import numpy as np
        BT, N, D, HEADS, E = (512, 64, 128, 4, 256)
        LRELU_SLOPE = 0.2
        EPS = 1e-08
        bt, n, d = H.shape
        h, dh = a.shape
        Xq = (H @ W_lin.T).reshape(bt, n, h, dh)
        Xv = (H @ W_val.T).reshape(bt, n, h, dh)
        Qs = Xq[:, src]
        Kt = Xq[:, dst]
        e = jnp.einsum('behd,hd->beh', jax.nn.leaky_relu(Qs + Kt, LRELU_SLOPE), a)
        e = e + jnp.log(A0[src, dst] + EPS)[None, :, None]
        e_t = e.transpose(1, 0, 2)
        m = jax.ops.segment_max(e_t, src, num_segments=n)
        ex = jnp.exp(e_t - m[src])
        denom = jax.ops.segment_sum(ex, src, num_segments=n)
        attn = ex / denom[src]
        Vt = Xv[:, dst].transpose(1, 0, 2, 3)
        Y = jax.ops.segment_sum(attn[..., None] * Vt, src, num_segments=n)
        Y = Y.transpose(1, 0, 2, 3).reshape(bt, n, d)
        return Y @ W_out.T
    x = _layernorm(x + _L0_gnn_ref(x, adj, L0_gnn_W1, L0_gnn_b1, L0_gnn_g1, L0_gnn_be1, L0_gnn_W2, L0_gnn_b2, L0_gnn_g2, L0_gnn_be2), axis=-1)
    x = _layernorm(x + _L1_gnn_ref(x, L1_gnn_W, adj, L1_gnn_bias), axis=-1)
    x = _layernorm(x + _L2_gnn_ref(x, adj, L2_gnn_Wg0, L2_gnn_bg0, L2_gnn_Wg1, L2_gnn_bg1, L2_gnn_Wih, L2_gnn_Whh, L2_gnn_bih, L2_gnn_bhh), axis=-1)
    x = _layernorm(x + _L3_gnn_ref(x, L3_gnn_W_lin, L3_gnn_W_val, L3_gnn_a, L3_gnn_W_out, adj, L3_gnn_src, L3_gnn_dst), axis=-1)
    return x

_drawn_inputs = setup_inputs


def setup_inputs(seed=0):
    import zlib

    import numpy as np

    out = dict(_drawn_inputs(seed))
    spreads = {'L0_gnn_b1': (0.0, 0.8),
     'L0_gnn_g1': (1.0, 0.2),
     'L0_gnn_be1': (0.0, 0.1),
     'L0_gnn_b2': (0.0, 0.8),
     'L0_gnn_g2': (1.0, 0.2),
     'L0_gnn_be2': (0.0, 0.1),
     'L2_gnn_bg0': (0.0, 0.1),
     'L2_gnn_bg1': (0.0, 0.356)}
    factors = {'L1_gnn_bias': 2.801, 'L2_gnn_Whh': 8.0, 'L2_gnn_bih': 2.677}
    for name, (base, spread) in spreads.items():
        noise = np.random.default_rng([zlib.crc32(name.encode()), seed]).standard_normal(out[name].shape)
        drawn = base * np.exp(spread * noise) if base else spread * noise
        out[name] = jnp.asarray(drawn.astype(out[name].dtype))
    for name, factor in factors.items():
        out[name] = (out[name] * factor).astype(out[name].dtype)
    return out
```

```python
from contextlib import ExitStack

import concourse.bass as bass
from concourse import mybir

ALU = mybir.AluOpType
ACT = mybir.ActivationFunctionType
AX = mybir.AxisListType
F32 = mybir.dt.float32
F32R = mybir.dt.float32r
I32 = mybir.dt.int32

P = 128
NB = 64
TB = 4
TC = TB * P
NT = NB // TB
NE = 256
EC = NE // P
HEADS = 4
HD = P // HEADS
BH = TB * HEADS
SKIPS = 4
EPS = 1e-5
LOG_EPS = 1e-8
SLOPE = 0.2
FAR = -3.0e38
LT = 4
ds = bass.ds

V_B1, V_G1, V_BE1, V_B2, V_G2, V_BE2, V_BG0, V_BG1, V_A, V_BIH, V_BHH, V_ALL = 0, 2, 4, 6, 7, 8, 9, 10, 11, 12, 28, 44


def pipeline(eng, n, stages):
    depth = len(stages)
    peel = (depth + 2) // 2 * 2

    def step(t):
        for d, stage in enumerate(stages):
            if 0 <= t - d < n:
                stage(t - d, (t - d) % 2, (t - d) // 2)

    for t in range(peel):
        step(t)
    with eng.Fori(peel // 2, n // 2) as pair:
        for u in range(2):
            for d, stage in enumerate(stages):
                stage(2 * pair + (u - d), (u - d) % 2, pair + (u - d) // 2)
    for t in range(n, n + depth - 1):
        step(t)


def late(t):
    return not isinstance(t, int) or t >= 2


def tile_of(ap, t):
    return ap[:, ds(t * TC, TC)]


class Scope:

    def __init__(self, nc):
        self.nc, self.ctx, self.n = nc, ExitStack(), 0

    def __enter__(self):
        self.ctx.__enter__()
        return self

    def __exit__(self, *e):
        return self.ctx.__exit__(*e)

    def sb(self, name, shape, dt=F32):
        return self.ctx.enter_context(self.nc.sbuf_tensor(name, shape, dt))

    def ps(self, name, shape=(P, TC)):
        return self.ctx.enter_context(self.nc.psum_tensor(name, list(shape), F32))

    def sem(self, name):
        return self.ctx.enter_context(self.nc.semaphore(name))


class Chain:

    def __init__(self, eng, sem):
        self.eng, self.sem, self.n = eng, sem, 0

    def __call__(self, ins):
        self.n += 1
        ins.then_inc(self.sem, 1)
        self.eng.wait_ge(self.sem, self.n)


class Norm:

    def __init__(self, sc, name, eps):
        self.st = sc.sb(name + "_st", [P, 2, TB, 6])
        self.mv = sc.sb(name + "_mv", [P, 2, TB, 2])
        self.spare = sc.sb(name + "_spare", [P, 1])
        self.sd = sc.sb(name + "_sd", [P, 2, TB])
        self.rs = sc.sb(name + "_rs", [P, 2, TB])
        self.eps = eps
        self.stats_done = sc.sem(name + "_stats_done")
        self.var_done = sc.sem(name + "_var_done")
        self.sd_done = sc.sem(name + "_sd_done")
        self.rs_done = sc.sem(name + "_rs_done")

    def stats(self, dve, z, t, s):
        for b in range(TB):
            dve.bn_stats(self.st[:, s, b, :], z[:, b, :]).then_inc(self.stats_done, 1)
        dve.wait_ge(self.stats_done, TB * t + TB)
        dve.memset(self.spare[:, :], 0.0)
        for b in range(TB):
            dve.bn_aggr(self.mv[:, s, b, :], self.st[:, s, b, :]).then_inc(self.var_done, 1)

    def root(self, act, t, s):
        act.wait_ge(self.var_done, TB * t + TB)
        act.activation(self.sd[:, s, :], self.mv[:, s, :, 1], ACT.Sqrt, bias=self.eps).then_inc(self.sd_done, 1)

    def apply(self, dve, z, out, t, s, done):
        dve.wait_ge(self.sd_done, t + 1)
        dve.reciprocal(self.rs[:, s, :], self.sd[:, s, :]).then_inc(self.rs_done, 1)
        dve.wait_ge(self.rs_done, t + 1)
        for b in range(TB):
            ins = dve.tensor_scalar(out[:, b, :], z[:, b, :], self.mv[:, s, b, 0:1], self.rs[:, s, b:b + 1],
                                    ALU.subtract, ALU.mult)
            ins.then_inc(done, 1)


def adj_resnorm_kernel(nc, x, adj, W1, b1, g1, be1, W2, b2, g2, be2, W3, bias3, Wg0, bg0, Wg1, bg1,
                       Wih, Whh, bih, bhh, W_lin, W_val, a, W_out, src, dst, out):
    x_tiles = x.rearrange("(t b) n d -> n t b d", b=TB)
    out_tiles = out.rearrange("(t b) n d -> n t b d", b=TB)
    score_rows = nc.dram_tensor("score_rows", [NT, BH, NE], F32, kind="Internal").ap()

    with Scope(nc) as top:
        sb = top.sb
        eps = sb("eps", [P, 1])
        log_eps = sb("log_eps", [P, 1])
        ident = sb("ident", [P, P])
        vec = sb("vec", [P, V_ALL])
        lstm_b = sb("lstm_b", [P, SKIPS * 4])
        adjT = sb("adjT", [P, P])
        hatT = sb("hatT", [P, P])
        splitT = sb("splitT", [P, 3, P])
        W1T = sb("W1T", [P, 2 * P])
        W2T = sb("W2T", [P, 2, P])
        W3s = sb("W3s", [P, 3, P])
        bias3_all = sb("bias3_all", [P, P])
        Wg0s = sb("Wg0s", [P, P])
        Wg1s = sb("Wg1s", [P, P])
        B0 = sb("B0", [P, P])
        B1 = sb("B1", [P, P])
        WQV = sb("WQV", [P, 2 * P])
        WoT = sb("WoT", [P, P])
        a_heads = sb("a_heads", [P, TB, BH])
        srcdstT = sb("srcdstT", [P, NE], F32R)
        dstT = sb("dstT", [P, NE], F32R)
        src1h = sb("src1h", [P, EC, P])
        same = sb("same", [P, EC, NE])
        last_of = sb("last_of", [P, EC, NE])
        restart = sb("restart", [P, NE])
        log_adj = sb("log_adj", [P, NE])
        XS = sb("XS", [P, NB, P])
        WT_hi = sb("WT_hi", [P, 2 * SKIPS - 1, 4 * P], F32R)
        WT_lo = sb("WT_lo", [P, 2 * SKIPS - 1, 4 * P], F32R)

        with Scope(nc) as sc:
            A_sb = sc.sb("A_sb", [P, P])
            A_norm = sc.sb("A_norm", [P, P])
            scaled = sc.sb("scaled", [P, P])
            diag_p = sc.sb("diag_p", [P, P])
            deg = sc.sb("deg", [P, 8])
            ones = sc.sb("ones", [P, P])
            vrows = sc.sb("vrows", [V_ALL, P])
            W1n = sc.sb("W1n", [P, 2, P])
            W2n = sc.sb("W2n", [P, 2 * P])
            Wn = sc.sb("Wn", [P, 2 * SKIPS - 1, 4, P])
            Wlin_n = sc.sb("Wlin_n", [P, P])
            Wval_n = sc.sb("Wval_n", [P, P])
            Wout_n = sc.sb("Wout_n", [P, P])
            idx_row_i = sc.sb("idx_row_i", [P, 2, NE], I32)
            idx_col_i = sc.sb("idx_col_i", [P, 2, EC], I32)
            idx_row = sc.sb("idx_row", [P, 2, NE])
            idx_col = sc.sb("idx_col", [P, EC, 2])
            iota_i = sc.sb("iota_i", [P, NE], I32)
            iota_row = sc.sb("iota_row", [P, NE])
            iota_ci = sc.sb("iota_ci", [P, EC], I32)
            iota_col = sc.sb("iota_col", [P, EC])
            key_row = sc.sb("key_row", [P, NE])
            key_col = sc.sb("key_col", [P, EC])
            junk = sc.sb("junk", [P, NE])
            rank = sc.sb("rank", [P, EC])
            perm = sc.sb("perm", [P, EC, NE])
            spread = sc.sb("spread", [P, 2, EC, P])
            srow = sc.sb("srow", [P, 2, NE])
            scol = sc.sb("scol", [P, EC, 2])
            dst1h = sc.sb("dst1h", [P, EC, P])
            srcT = sc.sb("srcT", [P, NE])
            ends = sc.sb("ends", [P, EC])
            is_last = sc.sb("is_last", [P, EC])
            picked = sc.sb("picked", [P, EC])
            logs = sc.sb("logs", [P, EC])
            log_spread = sc.sb("log_spread", [P, EC, P])
            adj_in, vec_in, idx_in, w_in, lw_in = (sc.sem(n) for n in ("adj_in", "vec_in", "idx_in", "w_in", "lw_in"))
            ident_ok, iota_ok, adjT_ps, adjT_sb, split_ok = (sc.sem(n) for n in ("ident_ok", "iota_ok", "adjT_ps", "adjT_sb", "split_ok"))
            norm_ok, col_ps, deg_ok, deg_root, scaled_ok, hat_ps = (sc.sem(n) for n in ("norm_ok", "col_ps", "deg_ok", "deg_root", "scaled_ok", "hat_ps"))
            vec_ps, vec_ok, row_ps, w_ps, w_used, lw_ps, lw_used = (sc.sem(n) for n in ("vec_ps", "vec_ok", "row_ps", "w_ps", "w_used", "lw_ps", "lw_used"))
            perm_ok, sorted_ps, sorted_ok, picked_ps, picked_ok, log_ok, spread_ok, logrow_ps = (
                sc.sem(n) for n in ("perm_ok", "sorted_ps", "sorted_ok", "picked_ps", "picked_ok", "log_ok", "spread_ok", "logrow_ps"))
            dve_chain, pool_chain = sc.sem("dve_chain"), sc.sem("pool_chain")
            pLW = [sc.ps(f"pLW{i}") for i in range(2)]
            pW = [sc.ps(f"pW{i}") for i in range(2)]
            pA = sc.ps("pA")
            pV = sc.ps("pV")
            pI = sc.ps("pI")
            pL = sc.ps("pL")
            turned = [(W1n[:, 0, :], W1T[:, 0:P]), (W1n[:, 1, :], W1T[:, P:2 * P]),
                      (W2n[:, 0:P], W2T[:, 0, :]), (W2n[:, P:2 * P], W2T[:, 1, :]),
                      (Wlin_n[:, :], WQV[:, 0:P]), (Wval_n[:, :], WQV[:, P:2 * P]), (Wout_n[:, :], WoT[:, :])]
            N_VEC, N_W = 11, 8

            with nc.Block() as block:
                @block.sync
                def _(sp):
                    sp.dma_start(A_sb[:, :], adj).then_inc(adj_in, 16)
                    for i, v in enumerate((src, dst)):
                        sp.dma_start(idx_col_i[:, i, :], v.rearrange("(c p) -> p c", p=P), allow_slow_non_contiguous=True).then_inc(idx_in, 16)
                        sp.dma_start(idx_row_i[:, i, :], v.rearrange("(o e) -> o e", o=1).broadcast_to([P, NE])).then_inc(idx_in, 16)
                    sp.dma_start(Wn[:, 0:SKIPS, :, :], Wih.rearrange("p (g r) d -> r p g d", r=P)).then_inc(lw_in, 16)
                    sp.dma_start(Wn[:, SKIPS:, :, :], Whh[1:SKIPS].rearrange("p (g r) d -> r p g d", r=P)).then_inc(lw_in, 16)

                @block.scalar
                def _(act):
                    for v, at, k in ((b1, V_B1, 2), (g1, V_G1, 2), (be1, V_BE1, 2), (b2, V_B2, 1), (g2, V_G2, 1),
                                     (be2, V_BE2, 1), (bg0, V_BG0, 1), (bg1, V_BG1, 1)):
                        act.dma_start(vrows[at:at + k, :], v.rearrange("(k p) -> k p", p=P)).then_inc(vec_in, 16)
                    act.dma_start(vrows[V_A:V_A + 1, :], a.rearrange("h d -> (h d)").rearrange("(k p) -> k p", p=P)).then_inc(vec_in, 16)
                    act.dma_start(vrows[V_BIH:V_BIH + 16, :], bih.rearrange("s (g p) -> (s g) p", p=P)).then_inc(vec_in, 16)
                    act.dma_start(vrows[V_BHH:V_BHH + 16, :], bhh.rearrange("s (g p) -> (s g) p", p=P)).then_inc(vec_in, 16)
                    act.wait_ge(deg_ok, 1)
                    act.activation(deg[:, 5:6], deg[:, 4:5], ACT.Sqrt).then_inc(deg_root, 1)
                    act.wait_ge(picked_ok, 1)
                    act.activation(logs[:, :], picked[:, :], ACT.Ln, bias=log_eps[:, 0:1]).then_inc(log_ok, 1)

                @block.gpsimd
                def _(pool):
                    link = Chain(pool, pool_chain)
                    link(pool.memset(ident[:, :], 0.0))
                    pool.affine_select(out=ident[:, :], in_=ident[:, :], compare_op=ALU.not_equal, fill=1.0,
                                       base=0, pattern=[[-1, P]], channel_multiplier=1).then_inc(ident_ok, 1)
                    pool.iota(iota_i[:, :], pattern=[[1, NE]], base=0, channel_multiplier=0).then_inc(iota_ok, 1)
                    pool.iota(iota_ci[:, :], pattern=[[P, EC]], base=0, channel_multiplier=1).then_inc(iota_ok, 1)
                    pool.dma_start(W1n[:, :, :], W1.rearrange("(k p) d -> p k d", p=P)).then_inc(w_in, 16)
                    pool.dma_start(W2n[:, :], W2).then_inc(w_in, 16)
                    pool.dma_start(Wlin_n[:, :], W_lin).then_inc(w_in, 16)
                    pool.dma_start(Wval_n[:, :], W_val).then_inc(w_in, 16)
                    pool.dma_start(Wout_n[:, :], W_out).then_inc(w_in, 16)
                    pool.dma_start(W3s[:, :, :], W3.rearrange("k f o -> f k o")).then_inc(w_in, 16)
                    pool.dma_start(Wg0s[:, :], Wg0).then_inc(w_in, 16)
                    pool.dma_start(Wg1s[:, :], Wg1).then_inc(w_in, 16)
                    pool.dma_start(bias3_all[:, :], bias3.rearrange("(o e) -> o e", o=1).broadcast_to([P, P])).then_inc(w_in, 16)
                    pool.wait_ge(adjT_sb, 1)
                    for k, (op, base, mult, step) in enumerate(((ALU.is_equal, 0, 1, -1), (ALU.is_gt, 0, 1, -1), (ALU.is_gt, 0, -1, 1))):
                        pool.affine_select(out=splitT[:, k, :], in_=adjT[:, :], compare_op=op, fill=0.0,
                                           base=base, pattern=[[step, P]], channel_multiplier=mult).then_inc(split_ok, 1)
                    pool.wait_ge(split_ok, 3)
                    pool.wait_ge(w_in, 16 * 9)

                @block.vector
                def _(dve):
                    link = Chain(dve, dve_chain)
                    dve.memset(eps[:, :], EPS)
                    dve.memset(log_eps[:, :], LOG_EPS)
                    link(dve.memset(ones[:, :], 1.0))
                    dve.wait_ge(adj_in, 16)
                    dve.wait_ge(ident_ok, 1)
                    link(dve.tensor_tensor(A_norm[:, :], A_sb[:, :], ident[:, :], ALU.add))
                    link(dve.tensor_reduce(deg[:, 0:1], A_norm[:, :], AX.X, ALU.add))
                    link(dve.tensor_tensor(diag_p[:, :], A_norm[:, :], ident[:, :], ALU.mult))
                    dve.tensor_reduce(deg[:, 1:2], diag_p[:, :], AX.X, ALU.add).then_inc(norm_ok, 1)
                    dve.wait_ge(norm_ok, 1)
                    dve.wait_ge(adjT_ps, 1)
                    dve.tensor_copy(adjT[:, :], pA[:, 0:P]).then_inc(adjT_sb, 1)
                    link(dve.tensor_tensor(deg[:, 2:3], deg[:, 0:1], deg[:, 1:2], ALU.subtract))
                    dve.wait_ge(col_ps, 1)
                    link(dve.tensor_tensor(deg[:, 3:4], deg[:, 2:3], pL[:, 0:1], ALU.add))
                    dve.reciprocal(deg[:, 4:5], deg[:, 3:4]).then_inc(deg_ok, 1)
                    dve.wait_ge(vec_ps, 1)
                    link(dve.tensor_copy(vec[:, :], pV[:, 0:V_ALL]))
                    link(dve.tensor_tensor(lstm_b[:, :], vec[:, V_BIH:V_BHH], vec[:, V_BHH:V_ALL], ALU.add))
                    link(dve.memset(a_heads[:, :, :], 0.0))
                    for u in range(TB):
                        for h in range(HEADS):
                            rows = slice(HD * h, HD * h + HD)
                            dve.tensor_copy(a_heads[rows, u, HEADS * u + h:HEADS * u + h + 1], vec[rows, V_A:V_A + 1])
                    dve.wait_ge(deg_root, 1)
                    dve.tensor_scalar(scaled[:, :], A_norm[:, :], deg[:, 5:6], None, ALU.mult).then_inc(scaled_ok, 1)
                    for i, (_, to) in enumerate(turned):
                        dve.wait_ge(w_ps, i + 1)
                        dve.tensor_copy(to, pW[i % 2][:, 0:P]).then_inc(w_used, 1)
                    for i in range(2 * SKIPS - 1):
                        dve.wait_ge(lw_ps, i + 1)
                        link(dve.tensor_copy(WT_hi[:, i, :], pLW[i % 2][:, :]))
                        dve.tensor_tensor(WT_lo[:, i, :], pLW[i % 2][:, :], WT_hi[:, i, :].bitcast(F32),
                                          ALU.subtract).then_inc(lw_used, 1)
                    dve.wait_ge(hat_ps, 1)
                    dve.tensor_scalar(hatT[:, :], pA[:, P:2 * P], deg[:, 5:6], None, ALU.mult)
                    dve.wait_ge(row_ps, 1)
                    dve.tensor_scalar(B0[:, :], pL[:, 2 * P:3 * P], vec[:, V_BG0:V_BG0 + 1], None, ALU.mult)
                    dve.tensor_scalar(B1[:, :], pL[:, 2 * P:3 * P], vec[:, V_BG1:V_BG1 + 1], None, ALU.mult)
                    dve.wait_ge(idx_in, 64)
                    dve.wait_ge(iota_ok, 2)
                    dve.tensor_copy(iota_row[:, :], iota_i[:, :])
                    dve.tensor_copy(iota_col[:, :], iota_ci[:, :])
                    for i in range(2):
                        dve.tensor_copy(idx_row[:, i, :], idx_row_i[:, i, :])
                        link(dve.tensor_copy(idx_col[:, :, i], idx_col_i[:, i, :]))
                    dve.scalar_tensor_tensor(out=key_row[:, :], in0=idx_row[:, 0, :], scalar=float(NE),
                                             in1=iota_row[:, :], op0=ALU.mult, op1=ALU.add)
                    link(dve.scalar_tensor_tensor(out=key_col[:, :], in0=idx_col[:, :, 0], scalar=float(NE),
                                                  in1=iota_col[:, :], op0=ALU.mult, op1=ALU.add))
                    for c in range(EC):
                        link(dve.tensor_scalar(junk[:, :], key_row[:, :], key_col[:, c:c + 1], None, ALU.is_lt))
                        link(dve.tensor_reduce(rank[:, c:c + 1], junk[:, :], AX.X, ALU.add))
                        link(dve.tensor_scalar(perm[:, c, :], iota_row[:, :], rank[:, c:c + 1], None, ALU.is_equal))
                        for i in range(2):
                            link(dve.tensor_scalar(spread[:, i, c, :], ones[:, :], idx_col[:, c, i:i + 1], None, ALU.mult))
                    dve.engine_nop().then_inc(perm_ok, 1)
                    dve.wait_ge(sorted_ps, 1)
                    link(dve.tensor_copy(srow[:, :, :], pI[:, :].rearrange("p (i e) -> p i e", i=2)))
                    link(dve.tensor_copy(scol[:, :, :], pV[:, P:P + 2 * EC].rearrange("p (c i) -> p c i", i=2)))
                    link(dve.tensor_scalar(srcT[:, :], srow[:, 0, :], iota_col[:, 0:1], None, ALU.is_equal))
                    link(dve.tensor_scalar(dstT[:, :], srow[:, 1, :], iota_col[:, 0:1], None, ALU.is_equal))
                    link(dve.tensor_tensor(srcdstT[:, :], srcT[:, :], dstT[:, :].bitcast(F32), ALU.add))
                    for c in range(EC):
                        dve.tensor_scalar(src1h[:, c, :], iota_row[:, 0:P], scol[:, c, 0:1], None, ALU.is_equal)
                        dve.tensor_scalar(dst1h[:, c, :], iota_row[:, 0:P], scol[:, c, 1:2], None, ALU.is_equal)
                        link(dve.tensor_scalar(same[:, c, :], srow[:, 0, :], scol[:, c, 0:1], None, ALU.is_equal))
                        link(dve.tensor_scalar(junk[:, :], srow[:, 0, :], scol[:, c, 0:1], None, ALU.is_le))
                        link(dve.tensor_reduce(ends[:, c:c + 1], junk[:, :], AX.X, ALU.add))
                        link(dve.scalar_tensor_tensor(out=is_last[:, c:c + 1], in0=ends[:, c:c + 1], scalar=-1.0,
                                                      in1=iota_col[:, c:c + 1], op0=ALU.add, op1=ALU.is_equal))
                        link(dve.tensor_scalar(last_of[:, c, :], same[:, c, :], is_last[:, c:c + 1], None, ALU.mult))
                    dve.memset(restart[:, 0:1], 0.0)
                    link(dve.tensor_tensor(junk[:, 1:NE], srow[:, 0, 1:NE], srow[:, 0, 0:NE - 1], ALU.not_equal))
                    link(dve.tensor_scalar(restart[:, 1:NE], junk[:, 1:NE], FAR, None, ALU.mult))
                    dve.engine_nop().then_inc(sorted_ok, 1)
                    dve.wait_ge(picked_ps, 1)
                    for c in range(EC):
                        link(dve.tensor_tensor(dst1h[:, c, :], dst1h[:, c, :], pL[:, P * c:P * c + P], ALU.mult))
                        link(dve.tensor_reduce(picked[:, c:c + 1], dst1h[:, c, :], AX.X, ALU.add))
                    dve.engine_nop().then_inc(picked_ok, 1)
                    dve.wait_ge(log_ok, 1)
                    for c in range(EC):
                        link(dve.tensor_scalar(log_spread[:, c, :], ones[:, :], logs[:, c:c + 1], None, ALU.mult))
                    dve.engine_nop().then_inc(spread_ok, 1)
                    dve.wait_ge(logrow_ps, 1)
                    link(dve.tensor_copy(log_adj[:, :], pI[:, 0:NE]))

                @block.tensor
                def _(pe):
                    pe.wait_ge(ident_ok, 1)
                    pe.wait_ge(adj_in, 16)
                    pe.transpose(pA[:, 0:P], A_sb[:, :], ident[:, :]).then_inc(adjT_ps, 1)
                    pe.wait_ge(norm_ok, 1)
                    pe.matmul(pL[:, 0:1], A_norm[:, :], ones[:, 0:1], start=True, stop=True).then_inc(col_ps, 1)
                    pe.wait_ge(vec_in, 16 * N_VEC)
                    pe.transpose(pV[:, 0:V_ALL], vrows[:, :], ident[0:V_ALL, 0:V_ALL]).then_inc(vec_ps, 1)
                    pe.wait_ge(w_in, 16 * 9)
                    for i, (w, _) in enumerate(turned):
                        if i >= 2:
                            pe.wait_ge(w_used, i - 1)
                        pe.transpose(pW[i % 2][:, 0:P], w, ident[:, :]).then_inc(w_ps, 1)
                    pe.wait_ge(lw_in, 32)
                    for i in range(2 * SKIPS - 1):
                        if i >= 2:
                            pe.wait_ge(lw_used, i - 1)
                        for g in range(4):
                            ins = pe.transpose(pLW[i % 2][:, P * g:P * g + P], Wn[:, i, g, :], ident[:, :])
                        ins.then_inc(lw_ps, 1)
                    pe.wait_ge(scaled_ok, 1)
                    pe.transpose(pA[:, P:2 * P], scaled[:, :], ident[:, :]).then_inc(hat_ps, 1)
                    pe.wait_ge(adjT_sb, 1)
                    pe.matmul(pL[:, 2 * P:3 * P], ones[:, :], adjT[:, :], start=True, stop=True).then_inc(row_ps, 1)
                    pe.wait_ge(perm_ok, 1)
                    for i in range(2):
                        for c in range(EC):
                            pe.matmul(pI[:, NE * i:NE * i + NE], spread[:, i, c, :], perm[:, c, :],
                                      start=(c == 0), stop=(c == EC - 1))
                    for r in range(EC):
                        for c in range(EC):
                            ins = pe.matmul(pV[:, P + 2 * r:P + 2 * r + 2], perm[:, c, P * r:P * r + P], idx_col[:, c, :],
                                            start=(c == 0), stop=(c == EC - 1))
                    ins.then_inc(sorted_ps, 1)
                    pe.wait_ge(sorted_ok, 1)
                    for c in range(EC):
                        ins = pe.matmul(pL[:, P * c:P * c + P], srcT[:, P * c:P * c + P], A_sb[:, :], start=True, stop=True)
                    ins.then_inc(picked_ps, 1)
                    pe.wait_ge(spread_ok, 1)
                    for c in range(EC):
                        ins = pe.matmul(pI[:, P * c:P * c + P], log_spread[:, c, :], ident[:, :], start=True, stop=True)
                    ins.then_inc(logrow_ps, 1)

        with Scope(nc) as l0:
            OP = l0.sb("OP", [P, NB * P])
            st1 = l0.sb("st1", [P, 2, NT, 6])
            st2 = l0.sb("st2", [P, NT, 6])
            mv1 = l0.sb("mv1", [P, 2, 2])
            mv2 = l0.sb("mv2", [P, 2])
            aff1 = l0.sb("aff1", [P, 2, 4])
            aff2 = l0.sb("aff2", [P, 4])
            hidden_scope = Scope(nc)
            hidden_scope.__enter__()
            HP = hidden_scope.sb("HP", [P, 2, NB * P])

            def batchnorm(dve, act_sem, dve_sem, link, st, mv, aff, gamma, beta, k):
                link(dve.bn_aggr(mv, st))
                dve.engine_nop().then_inc(dve_sem, 1)
                dve.wait_ge(act_sem, k + 1)
                link(dve.reciprocal(aff[:, 1:2], aff[:, 0:1]))
                link(dve.tensor_tensor(aff[:, 2:3], gamma, aff[:, 1:2], ALU.mult))
                link(dve.tensor_tensor(aff[:, 1:2], mv[:, 0:1], aff[:, 2:3], ALU.mult))
                link(dve.tensor_tensor(aff[:, 3:4], beta, aff[:, 1:2], ALU.subtract))

            with Scope(nc) as sc:
                xs = sc.sb("xs_a", [P, 2, TB, P])
                agg = sc.sb("agg", [P, 2, TC])
                pMix = [sc.ps(f"pMix{i}") for i in range(2)]
                pHid = [[sc.ps(f"pHid{i}{k}") for k in range(2)] for i in range(2)]
                x_in = [sc.sem(f"x_in_a{i}") for i in range(2)]
                mix_done, agg_done, hid_done, hp_done, stat_done, var_done, root_done, chain = (
                    sc.sem(n) for n in ("mix_done", "agg_done", "hid_done", "hp_done", "stat_done", "var_done_a", "root_done_a", "chain_a"))
                with nc.Block() as block:
                    @block.sync
                    def _(sp):
                        def load(t, s, j):
                            if late(t):
                                sp.wait_ge(mix_done, t - 1)
                            sp.dma_start(xs[:, s, :, :], x_tiles[:, ds(t, 1), :, :].rearrange("n o b d -> n (o b) d")).then_inc(x_in[s], 16)
                        pipeline(sp, NT, [load])

                    @block.tensor
                    def _(pe):
                        def mix(t, s, j):
                            pe.wait_ge(x_in[s], 16 * j + 16)
                            if late(t):
                                pe.wait_ge(agg_done, t - 1)
                            for b in range(TB):
                                ins = pe.matmul(pMix[s][:, P * b:P * b + P], xs[:, s, b, :], hatT[:, :], start=True, stop=True)
                            ins.then_inc(mix_done, 1)

                        def hidden(t, s, j):
                            pe.wait_ge(agg_done, t + 1)
                            if late(t):
                                pe.wait_ge(hp_done, 2 * t - 2)
                            for k in range(2):
                                pe.matmul(pHid[s][k][:, :], W1T[:, P * k:P * k + P], agg[:, s, :], start=True, stop=True).then_inc(hid_done, 1)
                        pipeline(pe, NT, [mix, hidden])

                    @block.scalar
                    def _(act):
                        def copy_mix(t, s, j):
                            act.wait_ge(mix_done, t + 1)
                            if late(t):
                                act.wait_ge(hid_done, 2 * t - 2)
                            act.copy(agg[:, s, :], pMix[s][:, :]).then_inc(agg_done, 1)

                        def copy_hidden(t, s, j):
                            for k in range(2):
                                act.wait_ge(hid_done, 2 * t + k + 1)
                                act.activation(HP[:, k, ds(t * TC, TC)], pHid[s][k][:, :], ACT.Identity,
                                               bias=vec[:, V_B1 + k:V_B1 + k + 1]).then_inc(hp_done, 1)
                        pipeline(act, NT, [copy_mix, copy_hidden])
                        for k in range(2):
                            act.wait_ge(var_done, k + 1)
                            act.activation(aff1[:, k, 0:1], mv1[:, k, 1:2], ACT.Sqrt, bias=eps[:, 0:1]).then_inc(root_done, 1)

                    @block.vector
                    def _(dve):
                        def stats(t, s, j):
                            for k in range(2):
                                dve.wait_ge(hp_done, 2 * t + k + 1)
                                dve.bn_stats(st1[:, k, ds(t, 1), :].rearrange("p o s -> p (o s)"), HP[:, k, ds(t * TC, TC)]).then_inc(stat_done, 1)
                        pipeline(dve, NT, [stats])
                        dve.wait_ge(stat_done, 2 * NT)
                        link = Chain(dve, chain)
                        for k in range(2):
                            batchnorm(dve, root_done, var_done, link, st1[:, k, :, :], mv1[:, k, :], aff1[:, k, :],
                                      vec[:, V_G1 + k:V_G1 + k + 1], vec[:, V_BE1 + k:V_BE1 + k + 1], k)

            with Scope(nc) as sc:
                hr = sc.sb("hr", [P, 2, 2, TC])
                pOut = [sc.ps(f"pOut_b{i}") for i in range(2)]
                relu_done, out_done, op_done, stat_done, var_done, root_done, chain = (
                    sc.sem(n) for n in ("relu_done", "out_done_b", "op_done", "stat_done_b", "var_done_b", "root_done_b", "chain_b"))
                with nc.Block() as block:
                    @block.scalar
                    def _(act):
                        def relu(t, s, j):
                            if late(t):
                                act.wait_ge(out_done, t - 1)
                            for k in range(2):
                                act.activation(hr[:, s, k, :], HP[:, k, ds(t * TC, TC)], ACT.Relu, scale=aff1[:, k, 2:3],
                                               bias=aff1[:, k, 3:4]).then_inc(relu_done, 1)
                        pipeline(act, NT, [relu])
                        act.wait_ge(var_done, 1)
                        act.activation(aff2[:, 0:1], mv2[:, 1:2], ACT.Sqrt, bias=eps[:, 0:1]).then_inc(root_done, 1)

                    @block.tensor
                    def _(pe):
                        def second(t, s, j):
                            if late(t):
                                pe.wait_ge(op_done, t - 1)
                            for k in range(2):
                                pe.wait_ge(relu_done, 2 * t + k + 1)
                                ins = pe.matmul(pOut[s][:, :], W2T[:, k, :], hr[:, s, k, :], start=(k == 0), stop=(k == 1))
                            ins.then_inc(out_done, 1)
                        pipeline(pe, NT, [second])

                    @block.vector
                    def _(dve):
                        def copy(t, s, j):
                            dve.wait_ge(out_done, t + 1)
                            dve.tensor_scalar(tile_of(OP, t), pOut[s][:, :], vec[:, V_B2:V_B2 + 1], None, ALU.add).then_inc(op_done, 1)

                        def stats(t, s, j):
                            dve.wait_ge(op_done, t + 1)
                            dve.bn_stats(st2[:, ds(t, 1), :].rearrange("p o s -> p (o s)"), tile_of(OP, t)).then_inc(stat_done, 1)
                        pipeline(dve, NT, [copy, stats])
                        dve.wait_ge(stat_done, NT)
                        batchnorm(dve, root_done, var_done, Chain(dve, chain), st2[:, :, :], mv2[:, :], aff2[:, :],
                                  vec[:, V_G2:V_G2 + 1], vec[:, V_BE2:V_BE2 + 1], 0)

            hidden_scope.__exit__(None, None, None)

            with Scope(nc) as sc:
                xs = sc.sb("xs_c", [P, 2, TB, P])
                yT = sc.sb("yT_c", [P, 2, TC])
                z0 = sc.sb("z0", [P, 2, TB, P])
                x1 = sc.sb("x1", [P, 2, TB, P])
                x1b = sc.sb("x1b", [P, 2, TB, P])
                mixed = sc.sb("mixed", [P, 2, 3, TB, P])
                z1 = sc.sb("z1", [P, 2, TB, P])
                n0, n1 = Norm(sc, "n0", eps[:, 0:1]), Norm(sc, "n1", eps[:, 0:1])
                pTr = [sc.ps(f"pTr{i}") for i in range(2)]
                pMx = [sc.ps(f"pMx{i}") for i in range(4)]
                pO = [sc.ps(f"pO_c{i}") for i in range(2)]
                x_in = [sc.sem(f"x_in_c{i}") for i in range(2)]
                y_done, tr_done, z0_done, x1_done, xb_done, mx_done, mixed_done, prod_done, z1_done, x2_done = (
                    sc.sem(n) for n in ("y_done", "tr_done", "z0_done", "x1_done", "xb_done", "mx_done", "mixed_done", "prod_done", "z1_done", "x2_done"))
                with nc.Block() as block:
                    @block.sync
                    def _(sp):
                        def load(t, s, j):
                            if late(t):
                                sp.wait_ge(z0_done, t - 1)
                            sp.dma_start(xs[:, s, :, :], x_tiles[:, ds(t, 1), :, :].rearrange("n o b d -> n (o b) d")).then_inc(x_in[s], 16)
                        pipeline(sp, NT, [load])

                    @block.gpsimd
                    def _(pool):
                        def add_bias(t, s, j):
                            pool.wait_ge(x1_done, TB * t + TB)
                            if late(t):
                                pool.wait_ge(z1_done, t - 1)
                            pool.tensor_tensor(x1b[:, s, :, :], x1[:, s, :, :],
                                               bias3_all[:, :].unsqueeze(1).broadcast_to([P, TB, P]), ALU.add).then_inc(xb_done, 1)
                        pipeline(pool, NT, [add_bias])

                    @block.tensor
                    def _(pe):
                        def turn(t, s, j):
                            pe.wait_ge(y_done, t + 1)
                            if late(t):
                                pe.wait_ge(z0_done, t - 1)
                            for b in range(TB):
                                ins = pe.transpose(pTr[s][:, P * b:P * b + P], yT[:, s, P * b:P * b + P], ident[:, :])
                            ins.then_inc(tr_done, 1)

                        def mix(t, s, j):
                            for b in range(TB):
                                pe.wait_ge(x1_done, TB * t + b + 1)
                                if late(t):
                                    pe.wait_ge(mixed_done, TB * t + b - 3)
                                elif t:
                                    pe.wait_ge(mixed_done, b + 1)
                                pe.matmul(pMx[b][:, 0:3 * P], x1[:, s, b, :], splitT[:, :, :], start=True, stop=True).then_inc(mx_done, 1)

                        def product(t, s, j):
                            if late(t):
                                pe.wait_ge(z1_done, t - 1)
                            for b in range(TB):
                                pe.wait_ge(mixed_done, TB * t + b + 1)
                                for k in range(3):
                                    ins = pe.matmul(pO[s][:, P * b:P * b + P], mixed[:, s, k, b, :], W3s[:, k, :], start=(k == 0), stop=(k == 2))
                            ins.then_inc(prod_done, 1)
                        pipeline(pe, NT, [turn, mix, product])

                    @block.scalar
                    def _(act):
                        def norm_y(t, s, j):
                            if late(t):
                                act.wait_ge(tr_done, t - 1)
                            act.activation(yT[:, s, :], tile_of(OP, t), ACT.Identity, scale=aff2[:, 2:3], bias=aff2[:, 3:4]).then_inc(y_done, 1)

                        def root0(t, s, j):
                            n0.root(act, t, s)

                        def copy_mixed(t, s, j):
                            for b in range(TB):
                                act.wait_ge(mx_done, TB * t + b + 1)
                                if late(t) and b == 0:
                                    act.wait_ge(prod_done, t - 1)
                                act.copy(mixed[:, s, :, b, :], pMx[b][:, 0:3 * P].rearrange("p (k i) -> p k i", k=3)).then_inc(mixed_done, 1)

                        def root1(t, s, j):
                            n1.root(act, t, s)

                        def first(t, s, j):
                            norm_y(t, s, j)
                            root0(t, s, j)
                        pipeline(act, NT, [first, copy_mixed, root1])

                    @block.vector
                    def _(dve):
                        def end0(t, s, j):
                            dve.wait_ge(tr_done, t + 1)
                            dve.wait_ge(x_in[s], 16 * j + 16)
                            dve.tensor_tensor(z0[:, s, :, :], pTr[s][:, :].rearrange("p (b d) -> p b d", b=TB), xs[:, s, :, :], ALU.add).then_inc(z0_done, 1)
                            dve.wait_ge(z0_done, t + 1)
                            n0.stats(dve, z0[:, s, :, :], t, s)
                            if late(t):
                                dve.wait_ge(mx_done, TB * t - TB)
                                dve.wait_ge(xb_done, t - 1)
                            n0.apply(dve, z0[:, s, :, :], x1[:, s, :, :], t, s, x1_done)

                        def end1(t, s, j):
                            dve.wait_ge(prod_done, t + 1)
                            dve.wait_ge(xb_done, t + 1)
                            dve.tensor_tensor(z1[:, s, :, :], pO[s][:, :].rearrange("p (b d) -> p b d", b=TB), x1b[:, s, :, :], ALU.add).then_inc(z1_done, 1)
                            dve.wait_ge(z1_done, t + 1)
                            n1.stats(dve, z1[:, s, :, :], t, s)
                            n1.apply(dve, z1[:, s, :, :], XS[:, ds(t * TB, TB), :], t, s, x2_done)

                        pipeline(dve, NT, [end0, lambda t, s, j: None, end1])

        with Scope(nc) as l2:
            H_hi = l2.sb("H_hi", [P, NB, P], F32R)
            H_lo = l2.sb("H_lo", [P, NB, P], F32R)

            with Scope(nc) as sc:
                xc = sc.sb("xc", [P, 2, TB, P])
                ag = sc.sb("ag", [P, 2, TC])
                h1p = sc.sb("h1p", [P, 2, TB, P])
                h1 = sc.sb("h1", [P, 2, TB, P])
                gs = sc.sb("gs", [P, 2, TB, P])
                h2p = sc.sb("h2p", [P, 2, TB, P])
                h2 = sc.sb("h2", [P, 2, TB, P])
                pAg = [sc.ps(f"pAg{i}") for i in range(2)]
                pH1 = [sc.ps(f"pH1{i}") for i in range(2)]
                pG = [sc.ps(f"pG{i}") for i in range(2)]
                pH2 = [sc.ps(f"pH2{i}") for i in range(2)]
                c_done, a_done, ag_done, g0_done, h1p_done, h1_done, g1_done, gs_done, m2_done, h2p_done, hi_done, h2_done, lo_done = (
                    sc.sem(n) for n in ("c_done", "a_done", "ag_done", "g0_done", "h1p_done", "h1_done", "g1_done", "gs_done",
                                        "m2_done", "h2p_done", "hi_done_d", "h2_done", "lo_done_d"))
                with nc.Block() as block:
                    @block.gpsimd
                    def _(pool):
                        def fetch(t, s, j):
                            if late(t):
                                pool.wait_ge(a_done, t - 1)
                            pool.tensor_copy(xc[:, s, :, :], XS[:, ds(t * TB, TB), :]).then_inc(c_done, 1)

                        def low(t, s, j):
                            pool.wait_ge(h2_done, t + 1)
                            pool.wait_ge(hi_done, t + 1)
                            pool.tensor_tensor(H_lo[:, ds(t * TB, TB), :], h2[:, s, :, :], H_hi[:, ds(t * TB, TB), :].bitcast(F32), ALU.subtract).then_inc(lo_done, 1)
                        pipeline(pool, NT, [fetch, lambda t, s, j: None, lambda t, s, j: None, low])

                    @block.tensor
                    def _(pe):
                        def mix1(t, s, j):
                            pe.wait_ge(c_done, t + 1)
                            if late(t):
                                pe.wait_ge(ag_done, t - 1)
                            for b in range(TB):
                                ins = pe.matmul(pAg[s][:, P * b:P * b + P], xc[:, s, b, :], adjT[:, :], start=True, stop=True)
                            ins.then_inc(a_done, 1)

                        def prod1(t, s, j):
                            pe.wait_ge(ag_done, t + 1)
                            if late(t):
                                pe.wait_ge(h1p_done, t - 1)
                            pe.matmul(pH1[s][:, :], Wg0s[:, :], ag[:, s, :], start=True, stop=True).then_inc(g0_done, 1)

                        def prod2(t, s, j):
                            pe.wait_ge(h1_done, t + 1)
                            if late(t):
                                pe.wait_ge(gs_done, t - 1)
                            for b in range(TB):
                                ins = pe.matmul(pG[s][:, P * b:P * b + P], h1[:, s, b, :], Wg1s[:, :], start=True, stop=True)
                            ins.then_inc(g1_done, 1)

                        def mix2(t, s, j):
                            pe.wait_ge(gs_done, t + 1)
                            if late(t):
                                pe.wait_ge(h2p_done, t - 1)
                            for b in range(TB):
                                ins = pe.matmul(pH2[s][:, P * b:P * b + P], gs[:, s, b, :], adjT[:, :], start=True, stop=True)
                            ins.then_inc(m2_done, 1)
                        pipeline(pe, NT, [mix1, prod1, prod2, mix2])

                    @block.scalar
                    def _(act):
                        def c1(t, s, j):
                            act.wait_ge(a_done, t + 1)
                            if late(t):
                                act.wait_ge(g0_done, t - 1)
                            act.copy(ag[:, s, :], pAg[s][:, :]).then_inc(ag_done, 1)

                        def r1(t, s, j):
                            act.wait_ge(h1p_done, t + 1)
                            if late(t):
                                act.wait_ge(g1_done, t - 1)
                            act.activation(h1[:, s, :, :], h1p[:, s, :, :], ACT.Relu).then_inc(h1_done, 1)

                        def c2(t, s, j):
                            act.wait_ge(g1_done, t + 1)
                            if late(t):
                                act.wait_ge(m2_done, t - 1)
                            act.copy(gs[:, s, :, :], pG[s][:, :].rearrange("p (b d) -> p b d", b=TB)).then_inc(gs_done, 1)

                        def r2(t, s, j):
                            act.wait_ge(h2p_done, t + 1)
                            if late(t):
                                act.wait_ge(lo_done, t - 1)
                            act.activation(h2[:, s, :, :], h2p[:, s, :, :], ACT.Relu).then_inc(h2_done, 1)
                        pipeline(act, NT, [c1, r1, c2, r2])

                    @block.vector
                    def _(dve):
                        def a1(t, s, j):
                            dve.wait_ge(g0_done, t + 1)
                            if late(t):
                                dve.wait_ge(h1_done, t - 1)
                            dve.tensor_tensor(h1p[:, s, :, :], pH1[s][:, :].rearrange("p (b d) -> p b d", b=TB),
                                              B0[:, :].unsqueeze(1).broadcast_to([P, TB, P]), ALU.add).then_inc(h1p_done, 1)

                        def a2(t, s, j):
                            dve.wait_ge(m2_done, t + 1)
                            if late(t):
                                dve.wait_ge(h2_done, t - 1)
                            dve.tensor_tensor(h2p[:, s, :, :], pH2[s][:, :].rearrange("p (b d) -> p b d", b=TB),
                                              B1[:, :].unsqueeze(1).broadcast_to([P, TB, P]), ALU.add).then_inc(h2p_done, 1)
                            dve.wait_ge(h2p_done, t + 1)
                            dve.tensor_scalar(H_hi[:, ds(t * TB, TB), :], h2p[:, s, :, :], 0.0, None, ALU.max).then_inc(hi_done, 1)
                        pipeline(dve, NT, [lambda t, s, j: None, a1, lambda t, s, j: None, a2])

            with Scope(nc) as sc:
                S_c = sc.sb("S_c", [P, LT, TC])
                S_hi = sc.sb("S_hi", [P, LT, TC], F32R)
                S_lo = sc.sb("S_lo", [P, LT, TC], F32R)
                G = sc.sb("G", [P, 2, 4, TC])
                fc = sc.sb("fc", [P, TC])
                ig = sc.sb("ig", [P, TC])
                tc_ = sc.sb("tc_", [P, 2, TC])
                hf = sc.sb("hf", [P, 2, TC])
                pG = [[sc.ps(f"pG{i}{g}") for g in range(4)] for i in range(2)]
                gate_ps, gate_sb, cell_done, tanh_done, h_done, hi_done, lo_done, fc_done, ig_done = (
                    sc.sem(n) for n in ("gate_ps", "gate_sb", "cell_done", "tanh_done", "h_done", "hi_done", "lo_done", "fc_done", "ig_done"))
                FIRST, LATER = (0, 2, 3), (1, 0, 2, 3)
                NW = [P // p for p in range(1, SKIPS + 1)]
                TBS = [4, 8, 8, 16]
                GROUPS = [NB // (tb * LT) for tb in TBS]

                class Count:

                    def __init__(self, n, g, l):
                        self.n, self.g, self.l = n, g, l

                def steps(visit, eng):
                    n = g = l = 0
                    for pi in range(SKIPS):
                        p = pi + 1
                        per_n = LT * p
                        per_l = LT * (p - 1)
                        per_g = LT * 3 + per_l * 4

                        def group(it, n0, g0, l0):
                            dn = dg = dl = 0
                            for step in range(p):
                                for k in range(LT):
                                    visit(pi, step, it, k, Count(n0 + dn, g0 + dg, l0 + dl), dn)
                                    dn += 1
                                    dg += 3 if step == 0 else 4
                                    dl += step > 0
                        if pi == 0:
                            group(0, n, g, l)
                            with eng.Fori(1, GROUPS[0]) as it:
                                group(it, n + per_n * it, g + per_g * it, l)
                        elif GROUPS[pi] > 1:
                            with eng.Fori(0, GROUPS[pi]) as it:
                                group(it, n + per_n * it, g + per_g * it, l + per_l * it)
                        else:
                            group(0, n, g, l)
                        n += per_n * GROUPS[pi]
                        g += per_g * GROUPS[pi]
                        l += per_l * GROUPS[pi]

                def windows(Hx, pi, step, it, k):
                    tb, p = TBS[pi], pi + 1
                    return Hx[:, ds((it * LT + k) * tb, tb), step:step + p * (NW[pi] - 1) + 1:p]

                def cols(ap, pi):
                    n = TBS[pi] * NW[pi]
                    return ap[:, 0:n]

                def grid(ap, pi):
                    return cols(ap, pi).rearrange("p (b w) -> p b w", b=TBS[pi])

                def gates(step):
                    return LATER if step else FIRST

                with nc.Block() as block:
                    @block.tensor
                    def _(pe):
                        def visit(pi, step, it, k, c, dn):
                            s = dn % 2
                            early = isinstance(c.n, int) and c.n < 2
                            if not early:
                                pe.wait_ge(gate_sb, c.g - gates_at(pi, dn, 1))
                            if pi > 0 and step == 0:
                                pe.wait_ge(lo_done, c.n - LT + 1)
                            if step > 0:
                                pe.wait_ge(lo_done, c.n - LT + 1)
                            for g in gates(step):
                                bank = pG[s][g][:, 0:TBS[pi] * NW[pi]]
                                wx = slice(P * g, P * g + P)
                                parts = [(WT_hi[:, pi, wx], windows(H_hi, pi, step, it, k)),
                                         (WT_hi[:, pi, wx], windows(H_lo, pi, step, it, k)),
                                         (WT_lo[:, pi, wx], windows(H_hi, pi, step, it, k))]
                                if step:
                                    w = SKIPS - 1 + pi
                                    parts += [(WT_hi[:, w, wx], cols(S_hi[:, k, :], pi)),
                                              (WT_hi[:, w, wx], cols(S_lo[:, k, :], pi)),
                                              (WT_lo[:, w, wx], cols(S_hi[:, k, :], pi))]
                                for i, (w, h) in enumerate(parts):
                                    ins = pe.matmul(bank, w, h, start=(i == 0), stop=(i == len(parts) - 1))
                                ins.then_inc(gate_ps, 1)

                        def gates_at(pi, dn, back):
                            d = dn - back
                            if d >= 0:
                                return 3 if d < LT else 4
                            return GATES_PREV[pi]
                        GATES_PREV = [3, 3, 4, 4]
                        steps(visit, pe)

                    @block.scalar
                    def _(act):
                        def visit(pi, step, it, k, c, dn):
                            s = dn % 2
                            if not (isinstance(c.n, int) and c.n < 2):
                                act.wait_ge(h_done, c.n - 1)
                            for i, g in enumerate(gates(step)):
                                act.wait_ge(gate_ps, c.g + i + 1)
                                act.activation(cols(G[:, s, g, :], pi), pG[s][g][:, 0:TBS[pi] * NW[pi]],
                                               ACT.Tanh if g == 2 else ACT.Sigmoid,
                                               bias=lstm_b[:, 4 * pi + g:4 * pi + g + 1]).then_inc(gate_sb, 1)
                            act.wait_ge(cell_done, c.n + 1)
                            act.activation(cols(tc_[:, s, :], pi), cols(S_c[:, k, :], pi), ACT.Tanh).then_inc(tanh_done, 1)
                        steps(visit, act)

                    @block.vector
                    def _(dve):
                        def visit(pi, step, it, k, c, dn):
                            s = dn % 2
                            i_, f_, g_, o_ = (cols(G[:, s, g, :], pi) for g in range(4))
                            cell = cols(S_c[:, k, :], pi)
                            order = gates(step)
                            if step:
                                dve.wait_ge(gate_sb, c.g + order.index(1) + 1)
                                dve.tensor_tensor(cols(fc[:, :], pi), f_, cell, ALU.mult).then_inc(fc_done, 1)
                                dve.wait_ge(gate_sb, c.g + max(order.index(0), order.index(2)) + 1)
                                dve.tensor_tensor(cols(ig[:, :], pi), i_, g_, ALU.mult).then_inc(ig_done, 1)
                                dve.wait_ge(fc_done, c.l + 1)
                                dve.wait_ge(ig_done, c.l + 1)
                                dve.tensor_tensor(cell, cols(fc[:, :], pi), cols(ig[:, :], pi), ALU.add).then_inc(cell_done, 1)
                            else:
                                dve.wait_ge(gate_sb, c.g + max(order.index(0), order.index(2)) + 1)
                                dve.tensor_tensor(cell, i_, g_, ALU.mult).then_inc(cell_done, 1)
                            dve.wait_ge(gate_sb, c.g + order.index(3) + 1)
                            dve.wait_ge(tanh_done, c.n + 1)
                            if not (isinstance(c.n, int) and c.n < 2):
                                dve.wait_ge(lo_done, c.n - 1)
                            h = cols(hf[:, s, :], pi)
                            dve.tensor_tensor(h, o_, cols(tc_[:, s, :], pi), ALU.mult).then_inc(h_done, 1)
                            dve.wait_ge(h_done, c.n + 1)
                            if step == pi:
                                to, h = windows(H_hi, pi, step, it, k), grid(hf[:, s, :], pi)
                            else:
                                to = cols(S_hi[:, k, :], pi)
                            dve.tensor_copy(to, h).then_inc(hi_done, 1)
                        steps(visit, dve)

                    @block.gpsimd
                    def _(pool):
                        def visit(pi, step, it, k, c, dn):
                            s = dn % 2
                            pool.wait_ge(hi_done, c.n + 1)
                            if step == pi:
                                to, hi, h = windows(H_lo, pi, step, it, k), windows(H_hi, pi, step, it, k), grid(hf[:, s, :], pi)
                            else:
                                to, hi, h = cols(S_lo[:, k, :], pi), cols(S_hi[:, k, :], pi), cols(hf[:, s, :], pi)
                            pool.tensor_tensor(to, h, hi.bitcast(F32), ALU.subtract).then_inc(lo_done, 1)
                        steps(visit, pool)

            l3 = Scope(nc)
            l3.__enter__()
            V_hi, V_lo = H_hi, H_lo
            with Scope(nc) as sc:
                hs = sc.sb("hs", [P, 2, TB, P])
                z2 = sc.sb("z2", [P, 2, TB, P])
                x3 = sc.sb("x3", [P, 2, TB, P])
                x3T = sc.sb("x3T", [P, 2, TB, P])
                Q_hi = sc.sb("Q_hi", [P, 2, TB, P], F32R)
                Q_lo = sc.sb("Q_lo", [P, 2, TB, P], F32R)
                zs = sc.sb("zs", [P, 2, TC])
                L = sc.sb("L", [P, 2, TC])
                sT = sc.sb("sT", [BH, 2, NE])
                n2 = Norm(sc, "n2", eps[:, 0:1])
                pT = sc.ps("pT")
                pX = sc.ps("pX")
                pQV = [sc.ps(f"pQV{i}") for i in range(2)]
                pE = [sc.ps(f"pE{i}") for i in range(2)]
                pS = [sc.ps(f"pS{i}") for i in range(2)]
                hs_done, tr_done, z_done, x3_done, kept, trx_done, x3T_done, qv_ps, v_hi, q_lo, v_lo, e_ps, zs_done, l_done, s_ps, s_sb = (
                    sc.sem(n) for n in ("hs_done", "tr_done_f", "z_done_f", "x3_done", "kept", "trx_done", "x3T_done", "qv_ps", "v_hi", "q_lo",
                                        "v_lo", "e_ps", "zs_done", "l_done", "s_ps", "s_sb"))
                s_out = [sc.sem(f"s_out{i}") for i in range(2)]

                def skip(t, s, j):
                    pass

                with nc.Block() as block:
                    @block.gpsimd
                    def _(pool):
                        def whole(t, s, j):
                            if late(t):
                                pool.wait_ge(tr_done, t - 1)
                            tl = ds(t * TB, TB)
                            pool.tensor_tensor(hs[:, s, :, :], H_hi[:, tl, :].bitcast(F32), H_lo[:, tl, :].bitcast(F32), ALU.add).then_inc(hs_done, 1)

                        def keep(t, s, j):
                            pool.wait_ge(x3_done, TB * t + TB)
                            pool.tensor_copy(XS[:, ds(t * TB, TB), :], x3[:, s, :, :]).then_inc(kept, 1)
                        pipeline(pool, NT, [whole, keep])

                    @block.tensor
                    def _(pe):
                        def turn(t, s, j):
                            pe.wait_ge(hs_done, t + 1)
                            if late(t):
                                pe.wait_ge(z_done, t)
                            elif t:
                                pe.wait_ge(z_done, 1)
                            for b in range(TB):
                                ins = pe.transpose(pT[:, P * b:P * b + P], hs[:, s, b, :], ident[:, :])
                            ins.then_inc(tr_done, 1)

                        def turn_x(t, s, j):
                            if late(t):
                                pe.wait_ge(x3T_done, t)
                            elif t:
                                pe.wait_ge(x3T_done, 1)
                            for b in range(TB):
                                pe.wait_ge(x3_done, TB * t + b + 1)
                                ins = pe.transpose(pX[:, P * b:P * b + P], x3[:, s, b, :], ident[:, :])
                            ins.then_inc(trx_done, 1)

                        def project(t, s, j):
                            pe.wait_ge(x3T_done, t + 1)
                            for q in range(2):
                                if late(t) or t:
                                    pe.wait_ge(q_lo, 2 * t + q - 1)
                                    pe.wait_ge(v_lo, 2 * t + q - 1)
                                for b in (0, 1):
                                    ins = pe.matmul(pQV[q][:, 2 * P * b:2 * P * b + 2 * P], x3T[:, s, 2 * q + b, :], WQV[:, :], start=True, stop=True)
                                ins.then_inc(qv_ps, 1)

                        def gather(t, s, j):
                            for q in range(2):
                                pe.wait_ge(q_lo, 2 * t + q + 1)
                                if late(t) or t:
                                    pe.wait_ge(l_done, 2 * t + q - 1)
                                for b in (0, 1):
                                    for i, part in enumerate((Q_hi, Q_lo)):
                                        ins = pe.matmul(pE[q][:, NE * b:NE * b + NE], part[:, s, 2 * q + b, :], srcdstT[:, :], start=(i == 0), stop=(i == 1))
                                ins.then_inc(e_ps, 1)

                        def score(t, s, j):
                            if late(t):
                                pe.wait_ge(s_sb, t - 1)
                            for q in range(2):
                                pe.wait_ge(l_done, 2 * t + q + 1)
                                for b in (0, 1):
                                    u = 2 * q + b
                                    ins = pe.matmul(pS[s][0:BH, 0:NE], a_heads[:, u, :], L[:, q, NE * b:NE * b + NE], start=(u == 0), stop=(u == TB - 1))
                            ins.then_inc(s_ps, 1)
                        pipeline(pe, NT, [turn, turn_x, project, gather, score])

                    @block.scalar
                    def _(act):
                        def root(t, s, j):
                            n2.root(act, t, s)

                        def copy_x(t, s, j):
                            act.wait_ge(trx_done, t + 1)
                            if late(t):
                                act.wait_ge(qv_ps, 2 * t - 2)
                            act.copy(x3T[:, s, :, :], pX[:, :].rearrange("p (b d) -> p b d", b=TB)).then_inc(x3T_done, 1)

                        def high(t, s, j):
                            for q in range(2):
                                act.wait_ge(qv_ps, 2 * t + q + 1)
                                if late(t):
                                    act.wait_ge(e_ps, 2 * t + q - 3)
                                both = pQV[q][:, :].rearrange("p (b v d) -> p b v d", b=2, v=2)
                                act.copy(Q_hi[:, s, 2 * q:2 * q + 2, :], both[:, :, 0, :])
                                act.copy(V_hi[:, ds(t * TB + 2 * q, 2), :], both[:, :, 1, :]).then_inc(v_hi, 1)

                        def scale(t, s, j):
                            for q in range(2):
                                act.wait_ge(e_ps, 2 * t + q + 1)
                                if late(t) or t:
                                    act.wait_ge(l_done, 2 * t + q - 1)
                                act.mul(zs[:, q, :], pE[q][:, :], SLOPE).then_inc(zs_done, 1)

                        def copy_s(t, s, j):
                            act.wait_ge(s_ps, t + 1)
                            if late(t):
                                act.wait_ge(s_out[s], 16 * j)
                            act.copy(sT[:, s, :], pS[s][0:BH, 0:NE]).then_inc(s_sb, 1)
                        pipeline(act, NT, [root, copy_x, high, scale, copy_s])

                    @block.vector
                    def _(dve):
                        def end2(t, s, j):
                            tl = ds(t * TB, TB)
                            dve.wait_ge(tr_done, t + 1)
                            dve.tensor_tensor(z2[:, s, :, :], pT[:, :].rearrange("p (b d) -> p b d", b=TB), XS[:, tl, :], ALU.add).then_inc(z_done, 1)
                            dve.wait_ge(z_done, t + 1)
                            n2.stats(dve, z2[:, s, :, :], t, s)
                            if late(t):
                                dve.wait_ge(kept, t - 1)
                                dve.wait_ge(trx_done, t - 1)
                            n2.apply(dve, z2[:, s, :, :], x3[:, s, :, :], t, s, x3_done)

                        def low(t, s, j):
                            for q in range(2):
                                both = pQV[q][:, :].rearrange("p (b v d) -> p b v d", b=2, v=2)
                                dve.wait_ge(v_hi, 2 * t + q + 1)
                                dve.tensor_tensor(Q_lo[:, s, 2 * q:2 * q + 2, :], both[:, :, 0, :], Q_hi[:, s, 2 * q:2 * q + 2, :].bitcast(F32), ALU.subtract).then_inc(q_lo, 1)
                                tl = ds(t * TB + 2 * q, 2)
                                dve.tensor_tensor(V_lo[:, tl, :], both[:, :, 1, :], V_hi[:, tl, :].bitcast(F32), ALU.subtract).then_inc(v_lo, 1)

                        def leaky(t, s, j):
                            for q in range(2):
                                dve.wait_ge(zs_done, 2 * t + q + 1)
                                if late(t) or t:
                                    dve.wait_ge(s_ps, t)
                                dve.tensor_tensor(L[:, q, :], pE[q][:, :], zs[:, q, :], ALU.max).then_inc(l_done, 1)
                        pipeline(dve, NT, [end2, skip, low, leaky])

                    @block.sync
                    def _(sp):
                        def store(t, s, j):
                            sp.wait_ge(s_sb, t + 1)
                            sp.dma_start(score_rows[ds(t, 1), :, :].rearrange("o r e -> (o r) e"), sT[:, s, :]).then_inc(s_out[s], 16)
                        pipeline(sp, NT, [store])
                        for s in range(2):
                            sp.wait_ge(s_out[s], 16 * (NT // 2))

            att = l3.sb("att", [P, EC, NB * HEADS])
            with Scope(nc) as sc:
                BHN = NB * HEADS
                eT = sc.sb("eT", [P, 2, NE])
                run = sc.sb("run", [P, 2, NE])
                eE = sc.sb("eE", [P, EC, BHN])
                rE = sc.sb("rE", [P, EC, BHN])
                dE = sc.sb("dE", [P, EC, BHN])
                ex = sc.sb("ex", [P, EC, BHN])
                rd = sc.sb("rd", [P, EC, BHN])
                pEt, pRt, pM, pD = sc.ps("pEt"), sc.ps("pRt"), sc.ps("pM"), sc.ps("pD")
                e_in, e_ok, r_ok, et_ps, rt_ps, rE_ok, m_ps, d_ok, ex_ok, den_ps, chain = (
                    sc.sem(n) for n in ("e_in", "e_ok", "r_ok", "et_ps", "rt_ps", "rE_ok", "m_ps", "d_ok", "ex_ok", "den_ps", "chain_g"))
                wide = lambda ap: ap.rearrange("p c r -> p (c r)")
                with nc.Block() as block:
                    @block.sync
                    def _(sp):
                        sp.dma_start(eT[:, :, :], score_rows.rearrange("(f t) r e -> (t r) f e", f=2)).then_inc(e_in, 16)

                    @block.vector
                    def _(dve):
                        link = Chain(dve, chain)
                        dve.wait_ge(e_in, 16)
                        link(dve.tensor_tensor(eT[:, :, :], eT[:, :, :], log_adj[:, :].unsqueeze(1).broadcast_to([P, 2, NE]), ALU.add))
                        dve.engine_nop().then_inc(e_ok, 1)
                        for f in range(2):
                            link(dve.tensor_tensor_scan(run[:, f, :], restart[:, :], eT[:, f, :], FAR, ALU.add, ALU.max))
                        dve.engine_nop().then_inc(r_ok, 1)
                        dve.wait_ge(rt_ps, 1)
                        dve.tensor_copy(wide(rE[:, :, :]), pRt[:, :]).then_inc(rE_ok, 1)
                        dve.wait_ge(et_ps, 1)
                        link(dve.tensor_copy(wide(eE[:, :, :]), pEt[:, :]))
                        dve.wait_ge(m_ps, 1)
                        dve.tensor_tensor(wide(dE[:, :, :]), wide(eE[:, :, :]), pM[:, :], ALU.subtract).then_inc(d_ok, 1)
                        dve.wait_ge(den_ps, 1)
                        link(dve.reciprocal(wide(rd[:, :, :]), pD[:, :]))
                        link(dve.tensor_tensor(att[:, :, :], ex[:, :, :], rd[:, :, :], ALU.mult))

                    @block.scalar
                    def _(act):
                        act.wait_ge(d_ok, 1)
                        act.activation(wide(ex[:, :, :]), wide(dE[:, :, :]), ACT.Exp).then_inc(ex_ok, 1)

                    @block.tensor
                    def _(pe):
                        def turn(bank, rows, done):
                            for c in range(EC):
                                for f in range(2):
                                    ins = pe.transpose(bank[:, BHN * c + P * f:BHN * c + P * f + P], rows[:, f, P * c:P * c + P], ident[:, :])
                            ins.then_inc(done, 1)

                        def over_edges(bank, table, rows, done):
                            for c in range(EC):
                                for k in range(EC):
                                    ins = pe.matmul(bank[:, BHN * c:BHN * c + BHN], table[:, k, P * c:P * c + P], rows[:, k, :], start=(k == 0), stop=(k == EC - 1))
                            ins.then_inc(done, 1)
                        pe.wait_ge(e_ok, 1)
                        turn(pEt, eT, et_ps)
                        pe.wait_ge(r_ok, 1)
                        turn(pRt, run, rt_ps)
                        pe.wait_ge(rE_ok, 1)
                        over_edges(pM, last_of, rE, m_ps)
                        pe.wait_ge(ex_ok, 1)
                        over_edges(pD, same, ex, den_ps)

            with Scope(nc) as sc:
                pr = sc.sb("pr", [P, 2, EC, TB, P])
                yT = sc.sb("yT_h", [P, 2, TB, P])
                z3 = sc.sb("z3", [P, 2, TB, P])
                os_ = sc.sb("os_", [P, 2, TB, P])
                n3 = Norm(sc, "n3", eps[:, 0:1])
                pVg = [[sc.ps(f"pVg{i}{c}") for c in range(EC)] for i in range(2)]
                pY = [sc.ps(f"pY{i}") for i in range(2)]
                pZ = [sc.ps(f"pZ{i}") for i in range(2)]
                vg_ps, pr_done, y_ps, y_sb, o_ps, z_done, o_done = (
                    sc.sem(n) for n in ("vg_ps", "pr_done", "y_ps", "y_sb", "o_ps", "z_done_h", "o_done"))
                o_out = [sc.sem(f"o_out{i}") for i in range(2)]
                with nc.Block() as block:
                    @block.tensor
                    def _(pe):
                        def gather(t, s, j):
                            for c in range(EC):
                                if late(t):
                                    pe.wait_ge(pr_done, EC * t + c - 3)
                                for i, part in enumerate((V_hi, V_lo)):
                                    ins = pe.matmul(pVg[s][c][:, :], dstT[:, P * c:P * c + P], part[:, ds(t * TB, TB), :], start=(i == 0), stop=(i == 1))
                                ins.then_inc(vg_ps, 1)

                        def combine(t, s, j):
                            pe.wait_ge(pr_done, EC * t + EC)
                            if late(t):
                                pe.wait_ge(y_sb, t - 1)
                            for b in range(TB):
                                for c in range(EC):
                                    ins = pe.matmul(pY[s][:, P * b:P * b + P], pr[:, s, c, b, :], src1h[:, c, :], start=(c == 0), stop=(c == EC - 1))
                            ins.then_inc(y_ps, 1)

                        def output(t, s, j):
                            pe.wait_ge(y_sb, t + 1)
                            if late(t):
                                pe.wait_ge(z_done, t - 1)
                            for b in range(TB):
                                ins = pe.matmul(pZ[s][:, P * b:P * b + P], yT[:, s, b, :], WoT[:, :], start=True, stop=True)
                            ins.then_inc(o_ps, 1)
                        pipeline(pe, NT, [gather, combine, output])

                    @block.scalar
                    def _(act):
                        def copy_y(t, s, j):
                            act.wait_ge(y_ps, t + 1)
                            if late(t):
                                act.wait_ge(o_ps, t - 1)
                            act.copy(yT[:, s, :, :], pY[s][:, :].rearrange("p (b d) -> p b d", b=TB)).then_inc(y_sb, 1)

                        def root(t, s, j):
                            n3.root(act, t, s)
                        pipeline(act, NT, [lambda t, s, j: None, copy_y, root])

                    @block.vector
                    def _(dve):
                        def weigh(t, s, j):
                            for c in range(EC):
                                dve.wait_ge(vg_ps, EC * t + c + 1)
                                if late(t):
                                    dve.wait_ge(y_ps, t - 1)
                                dve.tensor_tensor(pr[:, s, c, :, :].rearrange("p b (h d) -> p (b h) d", h=HEADS),
                                                  pVg[s][c][:, :].rearrange("p (r d) -> p r d", d=HD),
                                                  att[:, c, ds(t * BH, BH)].unsqueeze(2).broadcast_to([P, BH, HD]), ALU.mult).then_inc(pr_done, 1)

                        def end3(t, s, j):
                            dve.wait_ge(o_ps, t + 1)
                            dve.tensor_tensor(z3[:, s, :, :], pZ[s][:, :].rearrange("p (b d) -> p b d", b=TB), XS[:, ds(t * TB, TB), :], ALU.add).then_inc(z_done, 1)
                            dve.wait_ge(z_done, t + 1)
                            n3.stats(dve, z3[:, s, :, :], t, s)
                            if late(t):
                                dve.wait_ge(o_out[s], 16 * j)
                            n3.apply(dve, z3[:, s, :, :], os_[:, s, :, :], t, s, o_done)
                        pipeline(dve, NT, [weigh, lambda t, s, j: None, end3])

                    @block.sync
                    def _(sp):
                        def store(t, s, j):
                            sp.wait_ge(o_done, TB * t + TB)
                            sp.dma_start(out_tiles[:, ds(t, 1), :, :].rearrange("n o b d -> n (o b) d"), os_[:, s, :, :]).then_inc(o_out[s], 16)
                        pipeline(sp, NT, [store])
                        for s in range(2):
                            sp.wait_ge(o_out[s], 16 * (NT // 2))
            l3.__exit__(None, None, None)


_INS = ['x', 'adj', 'L0_gnn_W1', 'L0_gnn_b1', 'L0_gnn_g1', 'L0_gnn_be1', 'L0_gnn_W2', 'L0_gnn_b2', 'L0_gnn_g2',
        'L0_gnn_be2', 'L1_gnn_W', 'L1_gnn_bias', 'L2_gnn_Wg0', 'L2_gnn_bg0', 'L2_gnn_Wg1', 'L2_gnn_bg1', 'L2_gnn_Wih',
        'L2_gnn_Whh', 'L2_gnn_bih', 'L2_gnn_bhh', 'L3_gnn_W_lin', 'L3_gnn_W_val', 'L3_gnn_a', 'L3_gnn_W_out',
        'L3_gnn_src', 'L3_gnn_dst']


def kernel(**inputs):
    import numpy as _np
    import concourse.bacc as _bacc
    from concourse import mybir as _mybir
    from concourse.bass_utils import run_bass_kernel_spmd as _run

    nc = _bacc.Bacc("TRN2", target_bir_lowering=False, num_devices=1)
    arrays, args = {}, []
    for name in _INS:
        a = _np.ascontiguousarray(inputs[name])
        arrays[f"in_{name}_dram"] = a
        args.append(nc.dram_tensor(f"in_{name}_dram", a.shape, _mybir.dt.from_np(a.dtype), kind="ExternalInput").ap())
    args.append(nc.dram_tensor("out_dram", (NB, P, P), F32, kind="ExternalOutput").ap())
    adj_resnorm_kernel(nc, *args)
    r = _run(nc, [arrays], core_ids=[0])
    return r.results[0]["out_dram"]
```

```python
from contextlib import ExitStack

import concourse.bass as bass
from concourse import mybir

ALU = mybir.AluOpType
ACT = mybir.ActivationFunctionType
AX = mybir.AxisListType
F32 = mybir.dt.float32
F32R = mybir.dt.float32r
I32 = mybir.dt.int32

P = 128
NB = 64
TB = 4
TC = TB * P
NT = NB // TB
NE = 256
EC = NE // P
HEADS = 4
HD = P // HEADS
BH = TB * HEADS
SKIPS = 4
EPS = 1e-5
LOG_EPS = 1e-8
SLOPE = 0.2
FAR = -3.0e38
LT = 4
ds = bass.ds

V_B1, V_G1, V_BE1, V_B2, V_G2, V_BE2, V_BG0, V_BG1, V_A, V_BIH, V_BHH, V_ALL = 0, 2, 4, 6, 7, 8, 9, 10, 11, 12, 28, 44


def pipeline(eng, n, stages, straight=0):
    depth = max(delay for delay, _ in stages)
    peel = max((depth + 3) // 2 * 2, straight)

    def step(t):
        for d, stage in stages:
            if 0 <= t - d < n:
                stage(t - d, (t - d) % 2, (t - d) // 2)

    for t in range(peel):
        step(t)
    with eng.Fori(peel // 2, n // 2) as pair:
        for u in range(2):
            for d, stage in stages:
                stage(2 * pair + (u - d), (u - d) % 2, pair + (u - d) // 2)
    for t in range(n, n + depth):
        step(t)


def late(t):
    return not isinstance(t, int) or t >= 2


def tile_of(ap, t):
    return ap[:, ds(t * TC, TC)]


class Scope:

    def __init__(self, nc):
        self.nc, self.ctx, self.n = nc, ExitStack(), 0

    def __enter__(self):
        self.ctx.__enter__()
        return self

    def __exit__(self, *e):
        return self.ctx.__exit__(*e)

    def sb(self, name, shape, dt=F32):
        return self.ctx.enter_context(self.nc.sbuf_tensor(name, shape, dt))

    def ps(self, name, shape=(P, TC)):
        return self.ctx.enter_context(self.nc.psum_tensor(name, list(shape), F32))

    def sem(self, name):
        return self.ctx.enter_context(self.nc.semaphore(name))


class Chain:

    def __init__(self, eng, sem):
        self.eng, self.sem, self.n = eng, sem, 0

    def __call__(self, ins):
        self.n += 1
        ins.then_inc(self.sem, 1)
        self.eng.wait_ge(self.sem, self.n)


class Norm:

    def __init__(self, sc, name, eps):
        self.st = sc.sb(name + "_st", [P, 2, TB, 6])
        self.mv = sc.sb(name + "_mv", [P, 2, TB, 2])
        self.spare = sc.sb(name + "_spare", [P, 1])
        self.sd = sc.sb(name + "_sd", [P, 2, TB])
        self.rs = sc.sb(name + "_rs", [P, 2, TB])
        self.sh = sc.sb(name + "_sh", [P, 2, TB])
        self.eps = eps
        self.stats_done = sc.sem(name + "_stats_done")
        self.var_done = sc.sem(name + "_var_done")
        self.sd_done = sc.sem(name + "_sd_done")
        self.rs_done = sc.sem(name + "_rs_done")
        self.sh_done = sc.sem(name + "_sh_done")

    def stats(self, dve, z, t, s):
        for b in range(TB):
            dve.bn_stats(self.st[:, s, b, :], z[:, b, :]).then_inc(self.stats_done, 1)
        dve.wait_ge(self.stats_done, TB * t + TB)
        dve.memset(self.spare[:, :], 0.0)
        for b in range(TB):
            dve.bn_aggr(self.mv[:, s, b, :], self.st[:, s, b, :]).then_inc(self.var_done, 1)

    def root(self, act, t, s):
        act.wait_ge(self.var_done, TB * t + TB)
        act.activation(self.sd[:, s, :], self.mv[:, s, :, 1], ACT.Sqrt, bias=self.eps).then_inc(self.sd_done, 1)

    def shift(self, dve, t, s):
        dve.wait_ge(self.sd_done, t + 1)
        dve.reciprocal(self.rs[:, s, :], self.sd[:, s, :]).then_inc(self.rs_done, 1)
        dve.wait_ge(self.rs_done, t + 1)
        dve.scalar_tensor_tensor(out=self.sh[:, s, :], in0=self.mv[:, s, :, 0], scalar=-1.0, in1=self.rs[:, s, :],
                                 op0=ALU.mult, op1=ALU.mult).then_inc(self.sh_done, 1)

    def apply_act(self, act, z, out, t, s, done):
        act.wait_ge(self.sh_done, t + 1)
        for b in range(TB):
            act.activation(out[:, b, :], z[:, b, :], ACT.Identity, scale=self.rs[:, s, b:b + 1],
                           bias=self.sh[:, s, b:b + 1]).then_inc(done, 1)

    def apply(self, dve, z, out, t, s, done):
        dve.wait_ge(self.sd_done, t + 1)
        dve.reciprocal(self.rs[:, s, :], self.sd[:, s, :]).then_inc(self.rs_done, 1)
        dve.wait_ge(self.rs_done, t + 1)
        for b in range(TB):
            ins = dve.tensor_scalar(out[:, b, :], z[:, b, :], self.mv[:, s, b, 0:1], self.rs[:, s, b:b + 1],
                                    ALU.subtract, ALU.mult)
            ins.then_inc(done, 1)


def adj_resnorm_kernel(nc, x, adj, W1, b1, g1, be1, W2, b2, g2, be2, W3, bias3, Wg0, bg0, Wg1, bg1,
                       Wih, Whh, bih, bhh, W_lin, W_val, a, W_out, src, dst, out):
    x_tiles = x.rearrange("(t b) n d -> n t b d", b=TB)
    out_tiles = out.rearrange("(t b) n d -> n t b d", b=TB)
    score_rows = nc.dram_tensor("score_rows", [NT, BH, NE], F32, kind="Internal").ap()

    with Scope(nc) as top:
        sb = top.sb
        eps = sb("eps", [P, 1])
        log_eps = sb("log_eps", [P, 1])
        ident = sb("ident", [P, P])
        vec = sb("vec", [P, V_ALL])
        lstm_b = sb("lstm_b", [P, SKIPS * 4])
        adjT = sb("adjT", [P, P])
        hatT = sb("hatT", [P, P])
        splitT = sb("splitT", [P, 3, P])
        W1T = sb("W1T", [P, 2 * P])
        W2T = sb("W2T", [P, 2, P])
        W3s = sb("W3s", [P, 3, P])
        bias3_all = sb("bias3_all", [P, P])
        Wg0s = sb("Wg0s", [P, P])
        Wg1s = sb("Wg1s", [P, P])
        B0 = sb("B0", [P, P])
        B1 = sb("B1", [P, P])
        WQV = sb("WQV", [P, 2 * P])
        WoT = sb("WoT", [P, P])
        a_heads = sb("a_heads", [P, TB, BH])
        srcdstT = sb("srcdstT", [P, NE], F32R)
        dstT = sb("dstT", [P, NE], F32R)
        src1h = sb("src1h", [P, EC, P])
        same = sb("same", [P, EC, NE])
        last_of = sb("last_of", [P, EC, NE])
        restart = sb("restart", [P, NE])
        log_adj = sb("log_adj", [P, NE])
        XS = sb("XS", [P, NB, P])
        WT_hi = sb("WT_hi", [P, 2 * SKIPS - 1, 4 * P], F32R)
        WT_lo = sb("WT_lo", [P, 2 * SKIPS - 1, 4 * P], F32R)

        picked_rows = sb("picked_rows", [P, EC, P])
        dst1h = sb("dst1h", [P, EC, P])
        srcT = sb("srcT", [P, NE])
        A_sb = sb("A_sb", [P, P])
        iota_row = sb("iota_row", [P, NE])
        iota_col = sb("iota_col", [P, EC])
        srow = sb("srow", [P, 2, NE])
        scol = sb("scol", [P, EC, 2])
        picked = sb("picked", [P, EC])
        ones = sb("ones", [P, P])

        zero_scope = Scope(nc)
        zero_scope.__enter__()
        OP = XS[:, :, :].rearrange("p b n -> p (b n)")
        aff1 = zero_scope.sb("aff1", [P, 2, 4])
        aff2 = zero_scope.sb("aff2", [P, 4])
        st1 = zero_scope.sb("st1", [P, 2, NT, 6])
        st2 = zero_scope.sb("st2", [P, NT, 6])
        mv1 = zero_scope.sb("mv1", [P, 2, 2])
        mv2 = zero_scope.sb("mv2", [P, 2])
        W1T_hi = zero_scope.sb("W1T_hi", [P, 2 * P], F32R)
        W1T_lo = zero_scope.sb("W1T_lo", [P, 2 * P], F32R)
        hidden_scope = Scope(nc)
        hidden_scope.__enter__()
        HP = hidden_scope.sb("HP", [P, 2, NB * P])
        early = Scope(nc)
        early.__enter__()
        Wn = early.sb("Wn", [P, 2 * SKIPS - 1, 4, P])
        idx_row_i = early.sb("idx_row_i", [P, 2, NE], I32)
        idx_col_i = early.sb("idx_col_i", [P, 2, EC], I32)
        idx_col = early.sb("idx_col", [P, EC, 2])
        perm = early.sb("perm", [P, EC, NE])
        spread = early.sb("spread", [P, 2, EC, P])
        xs_a = early.sb("xs_a", [P, 2, TB, P])
        lw_in, idx_in = early.sem("lw_in"), early.sem("idx_in")
        x_in_a = [early.sem(f"x_in_a{i}") for i in range(2)]

        def load_x(sp, xs, x_in, t, s):
            sp.dma_start(xs[:, s, :, :], x_tiles[:, ds(t, 1), :, :].rearrange("n o b d -> n (o b) d")).then_inc(x_in[s], 16)

        with Scope(nc) as sc:
            A_norm = sc.sb("A_norm", [P, P])
            scaled = sc.sb("scaled", [P, P])
            diag_p = sc.sb("diag_p", [P, P])
            deg = sc.sb("deg", [P, 8])
            vrows = sc.sb("vrows", [V_ALL, P])
            W1n = sc.sb("W1n", [P, 2, P])
            W2n = sc.sb("W2n", [P, 2 * P])
            Wlin_n = sc.sb("Wlin_n", [P, P])
            Wval_n = sc.sb("Wval_n", [P, P])
            Wout_n = sc.sb("Wout_n", [P, P])
            adj_in, vec_in, w_in = (sc.sem(n) for n in ("adj_in", "vec_in", "w_in"))
            ident_ok, adjT_ps, adjT_sb, split_ok = (sc.sem(n) for n in ("ident_ok", "adjT_ps", "adjT_sb", "split_ok"))
            norm_ok, col_ps, deg_ok, deg_root, scaled_ok, hat_ps = (sc.sem(n) for n in ("norm_ok", "col_ps", "deg_ok", "deg_root", "scaled_ok", "hat_ps"))
            vec_ps, row_ps, w_ps, w_used = (sc.sem(n) for n in ("vec_ps", "row_ps", "w_ps", "w_used"))
            ones_ok, dve_chain, pool_chain = sc.sem("ones_ok"), sc.sem("dve_chain"), sc.sem("pool_chain")
            pW = [sc.ps(f"pW{i}") for i in range(2)]
            pA = sc.ps("pA")
            pV = sc.ps("pV")
            pL = sc.ps("pL")
            turned = [(W1n[:, 0, :], W1T[:, 0:P]), (W1n[:, 1, :], W1T[:, P:2 * P]),
                      (W2n[:, 0:P], W2T[:, 0, :]), (W2n[:, P:2 * P], W2T[:, 1, :]),
                      (Wlin_n[:, :], WQV[:, 0:P]), (Wval_n[:, :], WQV[:, P:2 * P]), (Wout_n[:, :], WoT[:, :])]
            N_VEC, N_W = 11, 9

            with nc.Block() as block:
                @block.sync
                def _(sp):
                    sp.dma_start(A_sb[:, :], adj).then_inc(adj_in, 16)
                    sp.dma_start(W1n[:, :, :], W1.rearrange("(k p) d -> p k d", p=P)).then_inc(w_in, 16)
                    sp.dma_start(W2n[:, :], W2).then_inc(w_in, 16)
                    sp.dma_start(Wlin_n[:, :], W_lin).then_inc(w_in, 16)
                    sp.dma_start(Wval_n[:, :], W_val).then_inc(w_in, 16)
                    sp.dma_start(Wout_n[:, :], W_out).then_inc(w_in, 16)
                    for t in range(2):
                        load_x(sp, xs_a, x_in_a, t, t)
                    for i, v in enumerate((src, dst)):
                        sp.dma_start(idx_col_i[:, i, :], v.rearrange("(c p) -> p c", p=P), allow_slow_non_contiguous=True).then_inc(idx_in, 16)
                        sp.dma_start(idx_row_i[:, i, :], v.rearrange("(o e) -> o e", o=1).broadcast_to([P, NE])).then_inc(idx_in, 16)
                    sp.dma_start(W3s[:, :, :], W3.rearrange("k f o -> f k o")).then_inc(w_in, 16)
                    sp.dma_start(Wg0s[:, :], Wg0).then_inc(w_in, 16)
                    sp.dma_start(Wg1s[:, :], Wg1).then_inc(w_in, 16)
                    sp.dma_start(bias3_all[:, :], bias3.rearrange("(o e) -> o e", o=1).broadcast_to([P, P])).then_inc(w_in, 16)
                    sp.dma_start(Wn[:, 0:SKIPS, :, :], Wih.rearrange("p (g r) d -> r p g d", r=P)).then_inc(lw_in, 16)
                    sp.dma_start(Wn[:, SKIPS:, :, :], Whh[1:SKIPS].rearrange("p (g r) d -> r p g d", r=P)).then_inc(lw_in, 16)

                @block.scalar
                def _(act):
                    for v, at, k in ((b1, V_B1, 2), (g1, V_G1, 2), (be1, V_BE1, 2), (b2, V_B2, 1), (g2, V_G2, 1),
                                     (be2, V_BE2, 1), (bg0, V_BG0, 1), (bg1, V_BG1, 1)):
                        act.dma_start(vrows[at:at + k, :], v.rearrange("(k p) -> k p", p=P)).then_inc(vec_in, 16)
                    act.dma_start(vrows[V_A:V_A + 1, :], a.rearrange("h d -> (h d)").rearrange("(k p) -> k p", p=P)).then_inc(vec_in, 16)
                    act.dma_start(vrows[V_BIH:V_BIH + 16, :], bih.rearrange("s (g p) -> (s g) p", p=P)).then_inc(vec_in, 16)
                    act.dma_start(vrows[V_BHH:V_BHH + 16, :], bhh.rearrange("s (g p) -> (s g) p", p=P)).then_inc(vec_in, 16)
                    act.wait_ge(deg_ok, 1)
                    act.activation(deg[:, 5:6], deg[:, 4:5], ACT.Sqrt).then_inc(deg_root, 1)

                @block.gpsimd
                def _(pool):
                    link = Chain(pool, pool_chain)
                    link(pool.memset(ident[:, :], 0.0))
                    pool.affine_select(out=ident[:, :], in_=ident[:, :], compare_op=ALU.not_equal, fill=1.0,
                                       base=0, pattern=[[-1, P]], channel_multiplier=1).then_inc(ident_ok, 1)
                    pool.wait_ge(adjT_sb, 1)
                    for k, (op, base, mult, step) in enumerate(((ALU.is_equal, 0, 1, -1), (ALU.is_gt, 0, 1, -1), (ALU.is_gt, 0, -1, 1))):
                        pool.affine_select(out=splitT[:, k, :], in_=adjT[:, :], compare_op=op, fill=0.0,
                                           base=base, pattern=[[step, P]], channel_multiplier=mult).then_inc(split_ok, 1)

                @block.vector
                def _(dve):
                    link = Chain(dve, dve_chain)
                    dve.memset(eps[:, :], EPS)
                    dve.memset(log_eps[:, :], LOG_EPS)
                    dve.memset(a_heads[:, :, :], 0.0).then_inc(ones_ok, 1)
                    dve.memset(ones[:, :], 1.0).then_inc(ones_ok, 1)
                    dve.wait_ge(adj_in, 16)
                    dve.wait_ge(ident_ok, 1)
                    link(dve.tensor_tensor(A_norm[:, :], A_sb[:, :], ident[:, :], ALU.add))
                    dve.tensor_tensor(diag_p[:, :], A_norm[:, :], ident[:, :], ALU.mult).then_inc(norm_ok, 1)
                    link(dve.tensor_reduce(deg[:, 0:1], A_norm[:, :], AX.X, ALU.add))
                    dve.wait_ge(norm_ok, 1)
                    link(dve.tensor_reduce(deg[:, 1:2], diag_p[:, :], AX.X, ALU.add))
                    link(dve.tensor_tensor(deg[:, 2:3], deg[:, 0:1], deg[:, 1:2], ALU.subtract))
                    dve.wait_ge(col_ps, 1)
                    link(dve.tensor_tensor(deg[:, 3:4], deg[:, 2:3], pL[:, 0:1], ALU.add))
                    dve.reciprocal(deg[:, 4:5], deg[:, 3:4]).then_inc(deg_ok, 1)
                    dve.wait_ge(adjT_ps, 1)
                    dve.tensor_copy(adjT[:, :], pA[:, 0:P]).then_inc(adjT_sb, 1)
                    dve.wait_ge(deg_root, 1)
                    dve.tensor_scalar(scaled[:, :], A_norm[:, :], deg[:, 5:6], None, ALU.mult).then_inc(scaled_ok, 1)
                    for i, (_, to) in enumerate(turned):
                        dve.wait_ge(w_ps, i + 1)
                        dve.tensor_copy(to, pW[i % 2][:, 0:P]).then_inc(w_used, 1)
                    dve.wait_ge(w_used, len(turned))
                    link(dve.tensor_copy(W1T_hi[:, :], W1T[:, :]))
                    dve.tensor_tensor(W1T_lo[:, :], W1T[:, :], W1T_hi[:, :].bitcast(F32), ALU.subtract)
                    dve.wait_ge(hat_ps, 1)
                    dve.tensor_scalar(hatT[:, :], pA[:, P:2 * P], deg[:, 5:6], None, ALU.mult)
                    dve.wait_ge(vec_ps, 1)
                    link(dve.tensor_copy(vec[:, :], pV[:, 0:V_ALL]))
                    dve.tensor_tensor(lstm_b[:, :], vec[:, V_BIH:V_BHH], vec[:, V_BHH:V_ALL], ALU.add)
                    for u in range(TB):
                        for h in range(HEADS):
                            rows = slice(HD * h, HD * h + HD)
                            dve.tensor_copy(a_heads[rows, u, HEADS * u + h:HEADS * u + h + 1], vec[rows, V_A:V_A + 1])
                    dve.wait_ge(row_ps, 1)
                    dve.tensor_scalar(B0[:, :], pL[:, 2 * P:3 * P], vec[:, V_BG0:V_BG0 + 1], None, ALU.mult)
                    dve.tensor_scalar(B1[:, :], pL[:, 2 * P:3 * P], vec[:, V_BG1:V_BG1 + 1], None, ALU.mult)

                @block.tensor
                def _(pe):
                    pe.wait_ge(ident_ok, 1)
                    pe.wait_ge(adj_in, 16)
                    pe.transpose(pA[:, 0:P], A_sb[:, :], ident[:, :]).then_inc(adjT_ps, 1)
                    pe.wait_ge(norm_ok, 1)
                    pe.wait_ge(ones_ok, 2)
                    pe.matmul(pL[:, 0:1], A_norm[:, :], ones[:, 0:1], start=True, stop=True).then_inc(col_ps, 1)
                    pe.wait_ge(w_in, 16 * N_W)
                    for i, (w, _) in enumerate(turned):
                        if i >= 2:
                            pe.wait_ge(w_used, i - 1)
                        pe.transpose(pW[i % 2][:, 0:P], w, ident[:, :]).then_inc(w_ps, 1)
                    pe.wait_ge(scaled_ok, 1)
                    pe.transpose(pA[:, P:2 * P], scaled[:, :], ident[:, :]).then_inc(hat_ps, 1)
                    pe.wait_ge(vec_in, 16 * N_VEC)
                    pe.transpose(pV[:, 0:V_ALL], vrows[:, :], ident[0:V_ALL, 0:V_ALL]).then_inc(vec_ps, 1)
                    pe.wait_ge(adjT_sb, 1)
                    pe.matmul(pL[:, 2 * P:3 * P], ones[:, :], adjT[:, :], start=True, stop=True).then_inc(row_ps, 1)

        if True:
            def batchnorm(dve, act_sem, dve_sem, link, st, mv, aff, gamma, beta, k):
                link(dve.bn_aggr(mv, st))
                dve.engine_nop().then_inc(dve_sem, 1)
                dve.wait_ge(act_sem, k + 1)
                link(dve.reciprocal(aff[:, 1:2], aff[:, 0:1]))
                link(dve.tensor_tensor(aff[:, 2:3], gamma, aff[:, 1:2], ALU.mult))
                link(dve.tensor_tensor(aff[:, 1:2], mv[:, 0:1], aff[:, 2:3], ALU.mult))
                link(dve.tensor_tensor(aff[:, 3:4], beta, aff[:, 1:2], ALU.subtract))

            with Scope(nc) as sc:
                agg_hi = sc.sb("agg_hi", [P, 2, TC], F32R)
                agg_lo = sc.sb("agg_lo", [P, 2, TC], F32R)
                idx_row = sc.sb("idx_row", [P, 2, NE])
                iota_i = sc.sb("iota_i", [P, NE], I32)
                iota_ci = sc.sb("iota_ci", [P, EC], I32)
                key_row = sc.sb("key_row", [P, NE])
                key_col = sc.sb("key_col", [P, EC])
                lower = sc.sb("lower", [P, EC, NE])
                rank = sc.sb("rank", [P, EC])
                lower_ok, rank_ok = sc.sem("lower_ok"), sc.sem("rank_ok")
                pMix = [sc.ps(f"pMix{i}") for i in range(2)]
                pHid = [[sc.ps(f"pHid{i}{k}") for k in range(2)] for i in range(2)]
                pLW = [sc.ps(f"pLW{i}") for i in range(2)]
                xs, x_in = xs_a, x_in_a
                mix_done, agg_done, low_done, hid_done, hp_done, stat_done, var_done, root_done, chain = (
                    sc.sem(n) for n in ("mix_done", "agg_done", "low_done", "hid_done", "hp_done", "stat_done", "var_done_a", "root_done_a", "chain_a"))
                lw_ps, lw_hi, lw_lo, perm_ok, sorted_ps, pool_chain = (
                    sc.sem(n) for n in ("lw_ps", "lw_hi", "lw_lo", "perm_ok", "sorted_ps", "pool_chain_a"))
                N_LW = 2 * SKIPS - 1
                assert N_LW < NT // 2
                with nc.Block() as block:
                    @block.sync
                    def _(sp):
                        def load(t, s, j):
                            if late(t):
                                sp.wait_ge(mix_done, t - 1)
                                load_x(sp, xs, x_in, t, s)
                        pipeline(sp, NT, [(0, load)])

                    @block.gpsimd
                    def _(pool):
                        link = Chain(pool, pool_chain)
                        pool.iota(iota_i[:, :], pattern=[[1, NE]], base=0, channel_multiplier=0)
                        link(pool.iota(iota_ci[:, :], pattern=[[P, EC]], base=0, channel_multiplier=1))
                        pool.wait_ge(idx_in, 64)
                        pool.tensor_copy(iota_row[:, :], iota_i[:, :])
                        pool.tensor_copy(iota_col[:, :], iota_ci[:, :])
                        for i in range(2):
                            pool.tensor_copy(idx_row[:, i, :], idx_row_i[:, i, :])
                            link(pool.tensor_copy(idx_col[:, :, i], idx_col_i[:, i, :]))
                        pool.tensor_scalar(key_row[:, :], idx_row[:, 0, :], float(NE), None, ALU.mult)
                        link(pool.tensor_scalar(key_col[:, :], idx_col[:, :, 0], float(NE), None, ALU.mult))
                        pool.tensor_tensor(key_row[:, :], key_row[:, :], iota_row[:, :], ALU.add)
                        link(pool.tensor_tensor(key_col[:, :], key_col[:, :], iota_col[:, :], ALU.add))
                        for c in range(EC):
                            pool.tensor_scalar(lower[:, c, :], key_row[:, :], key_col[:, c:c + 1], None, ALU.is_lt).then_inc(lower_ok, 1)
                            for i in range(2):
                                link(pool.tensor_scalar(spread[:, i, c, :], ones[:, :], idx_col[:, c, i:i + 1], None, ALU.mult))
                        pool.wait_ge(rank_ok, 1)
                        for c in range(EC):
                            link(pool.tensor_scalar(perm[:, c, :], iota_row[:, :], rank[:, c:c + 1], None, ALU.is_equal))
                        pool.engine_nop().then_inc(perm_ok, 1)

                    @block.tensor
                    def _(pe):
                        def lstm_weights(t, s, j):
                            if isinstance(t, int) and t < N_LW:
                                if t == 0:
                                    pe.wait_ge(lw_in, 32)
                                if late(t):
                                    pe.wait_ge(lw_lo, t - 1)
                                for g in range(4):
                                    ins = pe.transpose(pLW[s][:, P * g:P * g + P], Wn[:, t, g, :], ident[:, :])
                                ins.then_inc(lw_ps, 1)

                        def mix(t, s, j):
                            pe.wait_ge(x_in[s], 16 * j + 16)
                            if late(t):
                                pe.wait_ge(low_done, t - 1)
                            for b in range(TB):
                                ins = pe.matmul(pMix[s][:, P * b:P * b + P], xs[:, s, b, :], hatT[:, :], start=True, stop=True)
                            ins.then_inc(mix_done, 1)

                        def hidden(t, s, j):
                            pe.wait_ge(low_done, t + 1)
                            if late(t):
                                pe.wait_ge(hp_done, 2 * t - 2)
                            for k in range(2):
                                w = slice(P * k, P * k + P)
                                pe.matmul(pHid[s][k][:, :], W1T_hi[:, w], agg_hi[:, s, :], start=True, stop=False)
                                pe.matmul(pHid[s][k][:, :], W1T_hi[:, w], agg_lo[:, s, :], start=False, stop=False)
                                pe.matmul(pHid[s][k][:, :], W1T_lo[:, w], agg_hi[:, s, :], start=False, stop=True).then_inc(hid_done, 1)
                        pipeline(pe, NT, [(0, mix), (0, lstm_weights), (1, hidden)], straight=8)
                        pe.wait_ge(perm_ok, 1)
                        pe.wait_ge(lw_lo, N_LW)
                        for i in range(2):
                            for c in range(EC):
                                pe.matmul(pLW[0][:, NE * i:NE * i + NE], spread[:, i, c, :], perm[:, c, :],
                                          start=(c == 0), stop=(c == EC - 1))
                        for r in range(EC):
                            for c in range(EC):
                                ins = pe.matmul(pLW[1][:, 2 * r:2 * r + 2], perm[:, c, P * r:P * r + P], idx_col[:, c, :],
                                                start=(c == 0), stop=(c == EC - 1))
                        ins.then_inc(sorted_ps, 1)

                    @block.scalar
                    def _(act):
                        def lstm_high(t, s, j):
                            if isinstance(t, int) and t < N_LW:
                                act.wait_ge(lw_ps, t + 1)
                                act.copy(WT_hi[:, t, :], pLW[s][:, :]).then_inc(lw_hi, 1)

                        def copy_mix(t, s, j):
                            act.wait_ge(mix_done, t + 1)
                            if late(t):
                                act.wait_ge(hid_done, 2 * t - 2)
                            act.copy(agg_hi[:, s, :], pMix[s][:, :]).then_inc(agg_done, 1)

                        def copy_hidden(t, s, j):
                            for k in range(2):
                                act.wait_ge(hid_done, 2 * t + k + 1)
                                act.activation(HP[:, k, ds(t * TC, TC)], pHid[s][k][:, :], ACT.Identity,
                                               bias=vec[:, V_B1 + k:V_B1 + k + 1]).then_inc(hp_done, 1)
                        pipeline(act, NT, [(0, copy_mix), (0, lstm_high), (1, copy_hidden)], straight=8)
                        act.wait_ge(sorted_ps, 1)
                        act.copy(srow[:, :, :], pLW[0][:, :].rearrange("p (i e) -> p i e", i=2))
                        act.copy(scol[:, :, :], pLW[1][:, 0:2 * EC].rearrange("p (c i) -> p c i", i=2))
                        for k in range(2):
                            act.wait_ge(var_done, k + 1)
                            act.activation(aff1[:, k, 0:1], mv1[:, k, 1:2], ACT.Sqrt, bias=eps[:, 0:1]).then_inc(root_done, 1)

                    @block.vector
                    def _(dve):
                        def lstm_low(t, s, j):
                            if isinstance(t, int) and t < N_LW:
                                dve.wait_ge(lw_hi, t + 1)
                                dve.tensor_tensor(WT_lo[:, t, :], pLW[s][:, :], WT_hi[:, t, :].bitcast(F32),
                                                  ALU.subtract).then_inc(lw_lo, 1)
                            elif isinstance(t, int) and t == N_LW:
                                dve.wait_ge(lower_ok, EC)
                                dve.tensor_reduce(rank[:, :], lower[:, :, :], AX.X, ALU.add).then_inc(rank_ok, 1)

                        def low(t, s, j):
                            dve.wait_ge(agg_done, t + 1)
                            dve.tensor_tensor(agg_lo[:, s, :], pMix[s][:, :], agg_hi[:, s, :].bitcast(F32), ALU.subtract).then_inc(low_done, 1)

                        def stats(t, s, j):
                            for k in range(2):
                                dve.wait_ge(hp_done, 2 * t + k + 1)
                                dve.bn_stats(st1[:, k, ds(t, 1), :].rearrange("p o s -> p (o s)"), HP[:, k, ds(t * TC, TC)]).then_inc(stat_done, 1)
                        pipeline(dve, NT, [(0, low), (0, lstm_low), (2, stats)], straight=8)
                        dve.wait_ge(stat_done, 2 * NT)
                        link = Chain(dve, chain)
                        for k in range(2):
                            batchnorm(dve, root_done, var_done, link, st1[:, k, :, :], mv1[:, k, :], aff1[:, k, :],
                                      vec[:, V_G1 + k:V_G1 + k + 1], vec[:, V_BE1 + k:V_BE1 + k + 1], k)
            early.__exit__(None, None, None)

            with Scope(nc) as sc:
                hr = sc.sb("hr", [P, 2, 2, TC])
                less = sc.sb("less", [P, EC, NE])
                less_ok, ends_ok = sc.sem("less_ok"), sc.sem("ends_ok")
                ends = sc.sb("ends", [P, EC])
                is_last = sc.sb("is_last", [P, EC])
                pOut = [sc.ps(f"pOut_b{i}") for i in range(2)]
                pPick = sc.ps("pPick")
                src_ok, picked_ps, pool_chain = sc.sem("src_ok"), sc.sem("picked_ps"), sc.sem("pool_chain_b")
                relu_done, out_done, op_done, stat_done, var_done, root_done, chain = (
                    sc.sem(n) for n in ("relu_done", "out_done_b", "op_done", "stat_done_b", "var_done_b", "root_done_b", "chain_b"))
                with nc.Block() as block:
                    @block.scalar
                    def _(act):
                        def relu(t, s, j):
                            if late(t):
                                act.wait_ge(out_done, t - 1)
                            for k in range(2):
                                act.activation(hr[:, s, k, :], HP[:, k, ds(t * TC, TC)], ACT.Relu, scale=aff1[:, k, 2:3],
                                               bias=aff1[:, k, 3:4]).then_inc(relu_done, 1)
                        pipeline(act, NT, [(0, relu)])
                        act.wait_ge(picked_ps, 1)
                        act.copy(picked_rows[:, :, :], pPick[:, 0:EC * P].rearrange("p (c n) -> p c n", c=EC))
                        act.wait_ge(var_done, 1)
                        act.activation(aff2[:, 0:1], mv2[:, 1:2], ACT.Sqrt, bias=eps[:, 0:1]).then_inc(root_done, 1)

                    @block.tensor
                    def _(pe):
                        def second(t, s, j):
                            if late(t):
                                pe.wait_ge(op_done, t - 1)
                            for k in range(2):
                                pe.wait_ge(relu_done, 2 * t + k + 1)
                                ins = pe.matmul(pOut[s][:, :], W2T[:, k, :], hr[:, s, k, :], start=(k == 0), stop=(k == 1))
                            ins.then_inc(out_done, 1)
                        pipeline(pe, NT, [(0, second)])
                        pe.wait_ge(src_ok, 1)
                        for c in range(EC):
                            ins = pe.matmul(pPick[:, P * c:P * c + P], srcT[:, P * c:P * c + P], A_sb[:, :], start=True, stop=True)
                        ins.then_inc(picked_ps, 1)

                    @block.gpsimd
                    def _(pool):
                        link = Chain(pool, pool_chain)
                        for c in range(EC):
                            pool.tensor_scalar(less[:, c, :], srow[:, 0, :], scol[:, c, 0:1], None, ALU.is_le).then_inc(less_ok, 1)
                        pool.tensor_scalar(srcT[:, :], srow[:, 0, :], iota_col[:, 0:1], None, ALU.is_equal).then_inc(src_ok, 1)
                        link(pool.tensor_scalar(dstT[:, :], srow[:, 1, :], iota_col[:, 0:1], None, ALU.is_equal))
                        pool.wait_ge(src_ok, 1)
                        link(pool.tensor_tensor(srcdstT[:, :], srcT[:, :], dstT[:, :].bitcast(F32), ALU.add))
                        for c in range(EC):
                            pool.tensor_scalar(src1h[:, c, :], iota_row[:, 0:P], scol[:, c, 0:1], None, ALU.is_equal)
                            pool.tensor_scalar(dst1h[:, c, :], iota_row[:, 0:P], scol[:, c, 1:2], None, ALU.is_equal)
                            link(pool.tensor_scalar(same[:, c, :], srow[:, 0, :], scol[:, c, 0:1], None, ALU.is_equal))
                        pool.wait_ge(ends_ok, 1)
                        link(pool.tensor_tensor(ends[:, :], ends[:, :], iota_col[:, :], ALU.subtract))
                        link(pool.tensor_scalar(is_last[:, :], ends[:, :], 1.0, None, ALU.is_equal))
                        for c in range(EC):
                            pool.tensor_scalar(last_of[:, c, :], same[:, c, :], is_last[:, c:c + 1], None, ALU.mult)
                        pool.memset(restart[:, 0:1], 0.0)
                        link(pool.tensor_tensor(restart[:, 1:NE], srow[:, 0, 1:NE], srow[:, 0, 0:NE - 1], ALU.subtract))
                        pool.tensor_scalar(restart[:, 1:NE], restart[:, 1:NE], 0.0, FAR, ALU.is_gt, ALU.mult)

                    @block.vector
                    def _(dve):
                        def copy(t, s, j):
                            dve.wait_ge(out_done, t + 1)
                            dve.tensor_scalar(tile_of(OP, t), pOut[s][:, :], vec[:, V_B2:V_B2 + 1], None, ALU.add).then_inc(op_done, 1)

                        def stats(t, s, j):
                            dve.wait_ge(op_done, t + 1)
                            dve.bn_stats(st2[:, ds(t, 1), :].rearrange("p o s -> p (o s)"), tile_of(OP, t)).then_inc(stat_done, 1)
                        def count_ends(t, s, j):
                            if isinstance(t, int) and t == 6:
                                dve.wait_ge(less_ok, EC)
                                dve.tensor_reduce(ends[:, :], less[:, :, :], AX.X, ALU.add).then_inc(ends_ok, 1)
                        pipeline(dve, NT, [(0, copy), (1, stats), (1, count_ends)], straight=8)
                        dve.wait_ge(stat_done, NT)
                        batchnorm(dve, root_done, var_done, Chain(dve, chain), st2[:, :, :], mv2[:, :], aff2[:, :],
                                  vec[:, V_G2:V_G2 + 1], vec[:, V_BE2:V_BE2 + 1], 0)

            hidden_scope.__exit__(None, None, None)

            with Scope(nc) as sc:
                xs = sc.sb("xs_c", [P, 2, TB, P])
                yT = sc.sb("yT_c", [P, 2, TC])
                z0 = sc.sb("z0", [P, 2, TB, P])
                x1 = sc.sb("x1", [P, 2, TB, P])
                x1b = sc.sb("x1b", [P, 2, TB, P])
                mixed = sc.sb("mixed", [P, 2, 3, TB, P])
                z1 = sc.sb("z1", [P, 2, TB, P])
                pool_chain = sc.sem("pool_chain_c")
                n0, n1 = Norm(sc, "n0", eps[:, 0:1]), Norm(sc, "n1", eps[:, 0:1])
                pTr = [sc.ps(f"pTr{i}") for i in range(2)]
                pMx = [sc.ps(f"pMx{i}") for i in range(4)]
                pO = [sc.ps(f"pO_c{i}") for i in range(2)]
                x_in = [sc.sem(f"x_in_c{i}") for i in range(2)]
                y_done, tr_done, z0_done, x1_done, xb_done, mx_done, mixed_done, prod_done, z1_done, x2_done = (
                    sc.sem(n) for n in ("y_done", "tr_done", "z0_done", "x1_done", "xb_done", "mx_done", "mixed_done", "prod_done", "z1_done", "x2_done"))
                with nc.Block() as block:
                    @block.sync
                    def _(sp):
                        def load(t, s, j):
                            if late(t):
                                sp.wait_ge(z0_done, t - 1)
                            sp.dma_start(xs[:, s, :, :], x_tiles[:, ds(t, 1), :, :].rearrange("n o b d -> n (o b) d")).then_inc(x_in[s], 16)
                        pipeline(sp, NT, [(0, load)])

                    @block.gpsimd
                    def _(pool):
                        def add_bias(t, s, j):
                            pool.wait_ge(x1_done, TB * t + TB)
                            if late(t):
                                pool.wait_ge(z1_done, t - 1)
                            pool.tensor_tensor(x1b[:, s, :, :], x1[:, s, :, :],
                                               bias3_all[:, :].unsqueeze(1).broadcast_to([P, TB, P]), ALU.add).then_inc(xb_done, 1)
                        pipeline(pool, NT, [(1, add_bias)])
                        link = Chain(pool, pool_chain)
                        for c in range(EC):
                            link(pool.tensor_tensor(dst1h[:, c, :], dst1h[:, c, :], picked_rows[:, c, :], ALU.mult))

                    @block.tensor
                    def _(pe):
                        def turn(t, s, j):
                            pe.wait_ge(y_done, t + 1)
                            if late(t):
                                pe.wait_ge(z0_done, t - 1)
                            for b in range(TB):
                                ins = pe.transpose(pTr[s][:, P * b:P * b + P], yT[:, s, P * b:P * b + P], ident[:, :])
                            ins.then_inc(tr_done, 1)

                        def mix(t, s, j):
                            for b in range(TB):
                                pe.wait_ge(x1_done, TB * t + b + 1)
                                if late(t):
                                    pe.wait_ge(mixed_done, TB * t + b - 3)
                                elif t:
                                    pe.wait_ge(mixed_done, b + 1)
                                pe.matmul(pMx[b][:, 0:3 * P], x1[:, s, b, :], splitT[:, :, :], start=True, stop=True).then_inc(mx_done, 1)

                        def product(t, s, j):
                            if late(t):
                                pe.wait_ge(z1_done, t - 1)
                            for b in range(TB):
                                pe.wait_ge(mixed_done, TB * t + b + 1)
                                for k in range(3):
                                    ins = pe.matmul(pO[s][:, P * b:P * b + P], mixed[:, s, k, b, :], W3s[:, k, :], start=(k == 0), stop=(k == 2))
                            ins.then_inc(prod_done, 1)
                        pipeline(pe, NT, [(1, turn), (3, product), (2, mix)])

                    @block.scalar
                    def _(act):
                        def norm_y(t, s, j):
                            if late(t):
                                act.wait_ge(tr_done, t - 1)
                            act.activation(yT[:, s, :], tile_of(OP, t), ACT.Identity, scale=aff2[:, 2:3], bias=aff2[:, 3:4]).then_inc(y_done, 1)

                        def root0(t, s, j):
                            n0.root(act, t, s)

                        def copy_mixed(t, s, j):
                            for b in range(TB):
                                act.wait_ge(mx_done, TB * t + b + 1)
                                if late(t) and b == 0:
                                    act.wait_ge(prod_done, t - 1)
                                act.copy(mixed[:, s, :, b, :], pMx[b][:, 0:3 * P].rearrange("p (k i) -> p k i", k=3)).then_inc(mixed_done, 1)

                        def root1(t, s, j):
                            n1.root(act, t, s)

                        def apply1(t, s, j):
                            n1.apply_act(act, z1[:, s, :, :], XS[:, ds(t * TB, TB), :], t, s, x2_done)

                        pipeline(act, NT, [(0, norm_y), (1, root0), (2, copy_mixed), (4, apply1), (3, root1)])

                    @block.vector
                    def _(dve):
                        def stats0(t, s, j):
                            dve.wait_ge(tr_done, t + 1)
                            dve.wait_ge(x_in[s], 16 * j + 16)
                            dve.tensor_tensor(z0[:, s, :, :], pTr[s][:, :].rearrange("p (b d) -> p b d", b=TB), xs[:, s, :, :], ALU.add).then_inc(z0_done, 1)
                            dve.wait_ge(z0_done, t + 1)
                            n0.stats(dve, z0[:, s, :, :], t, s)

                        def apply0(t, s, j):
                            if late(t):
                                dve.wait_ge(mx_done, TB * t - TB)
                                dve.wait_ge(xb_done, t - 1)
                            n0.apply(dve, z0[:, s, :, :], x1[:, s, :, :], t, s, x1_done)

                        def stats1(t, s, j):
                            dve.wait_ge(prod_done, t + 1)
                            dve.wait_ge(xb_done, t + 1)
                            if late(t):
                                dve.wait_ge(x2_done, TB * t - TB)
                            dve.tensor_tensor(z1[:, s, :, :], pO[s][:, :].rearrange("p (b d) -> p b d", b=TB), x1b[:, s, :, :], ALU.add).then_inc(z1_done, 1)
                            dve.wait_ge(z1_done, t + 1)
                            n1.stats(dve, z1[:, s, :, :], t, s)

                        def shift1(t, s, j):
                            n1.shift(dve, t, s)

                        pipeline(dve, NT, [(1, stats0), (4, shift1), (3, stats1), (1, apply0)])

        zero_scope.__exit__(None, None, None)

        with Scope(nc) as l2:
            H_hi = l2.sb("H_hi", [P, NB, P], F32R)
            H_lo = l2.sb("H_lo", [P, NB, P], F32R)

            with Scope(nc) as sc:
                logs = sc.sb("logs", [P, EC])
                log_spread = sc.sb("log_spread", [P, EC, P])
                picked_ok, log_ok, spread_ok, logrow_ps, pool_chain = (sc.sem(n) for n in ("picked_ok", "log_ok", "spread_ok", "logrow_ps", "pool_chain_d"))
                xc = sc.sb("xc", [P, 2, TB, P])
                ag = sc.sb("ag", [P, 2, TC])
                h1p = sc.sb("h1p", [P, 2, TB, P])
                h1 = sc.sb("h1", [P, 2, TB, P])
                gs = sc.sb("gs", [P, 2, TB, P])
                h2p = sc.sb("h2p", [P, 2, TB, P])
                h2 = sc.sb("h2", [P, 2, TB, P])
                pAg = [sc.ps(f"pAg{i}") for i in range(2)]
                pH1 = [sc.ps(f"pH1{i}") for i in range(2)]
                pG = [sc.ps(f"pG{i}") for i in range(2)]
                pH2 = [sc.ps(f"pH2{i}") for i in range(2)]
                c_done, a_done, ag_done, g0_done, h1p_done, h1_done, g1_done, gs_done, m2_done, h2p_done, hi_done, h2_done, lo_done = (
                    sc.sem(n) for n in ("c_done", "a_done", "ag_done", "g0_done", "h1p_done", "h1_done", "g1_done", "gs_done",
                                        "m2_done", "h2p_done", "hi_done_d", "h2_done", "lo_done_d"))
                with nc.Block() as block:
                    @block.gpsimd
                    def _(pool):
                        def low(t, s, j):
                            pool.wait_ge(h2_done, t + 1)
                            pool.wait_ge(hi_done, t + 1)
                            pool.tensor_tensor(H_lo[:, ds(t * TB, TB), :], h2[:, s, :, :], H_hi[:, ds(t * TB, TB), :].bitcast(F32), ALU.subtract).then_inc(lo_done, 1)
                        link = Chain(pool, pool_chain)
                        pool.wait_ge(log_ok, 1)
                        for c in range(EC):
                            link(pool.tensor_scalar(log_spread[:, c, :], ones[:, :], logs[:, c:c + 1], None, ALU.mult))
                        pool.engine_nop().then_inc(spread_ok, 1)
                        pipeline(pool, NT, [(5, low)])

                    @block.tensor
                    def _(pe):
                        def mix1(t, s, j):
                            pe.wait_ge(c_done, t + 1)
                            if late(t):
                                pe.wait_ge(ag_done, t - 1)
                            for b in range(TB):
                                ins = pe.matmul(pAg[s][:, P * b:P * b + P], xc[:, s, b, :], adjT[:, :], start=True, stop=True)
                            ins.then_inc(a_done, 1)

                        def prod1(t, s, j):
                            pe.wait_ge(ag_done, t + 1)
                            if late(t):
                                pe.wait_ge(h1p_done, t - 1)
                            pe.matmul(pH1[s][:, :], Wg0s[:, :], ag[:, s, :], start=True, stop=True).then_inc(g0_done, 1)

                        def prod2(t, s, j):
                            pe.wait_ge(h1_done, t + 1)
                            if late(t):
                                pe.wait_ge(gs_done, t - 1)
                            for b in range(TB):
                                ins = pe.matmul(pG[s][:, P * b:P * b + P], h1[:, s, b, :], Wg1s[:, :], start=True, stop=True)
                            ins.then_inc(g1_done, 1)

                        def mix2(t, s, j):
                            pe.wait_ge(gs_done, t + 1)
                            if late(t):
                                pe.wait_ge(h2p_done, t - 1)
                            for b in range(TB):
                                ins = pe.matmul(pH2[s][:, P * b:P * b + P], gs[:, s, b, :], adjT[:, :], start=True, stop=True)
                            ins.then_inc(m2_done, 1)
                        pipeline(pe, NT, [(1, mix1), (2, prod1), (3, prod2), (4, mix2)])
                        pe.wait_ge(spread_ok, 1)
                        pe.wait_ge(ag_done, NT)
                        for c in range(EC):
                            ins = pe.matmul(pAg[0][:, P * c:P * c + P], log_spread[:, c, :], ident[:, :], start=True, stop=True)
                        ins.then_inc(logrow_ps, 1)

                    @block.scalar
                    def _(act):
                        def c1(t, s, j):
                            act.wait_ge(a_done, t + 1)
                            if late(t):
                                act.wait_ge(g0_done, t - 1)
                            act.copy(ag[:, s, :], pAg[s][:, :]).then_inc(ag_done, 1)

                        def r1(t, s, j):
                            act.wait_ge(h1p_done, t + 1)
                            if late(t):
                                act.wait_ge(g1_done, t - 1)
                            act.activation(h1[:, s, :, :], h1p[:, s, :, :], ACT.Relu).then_inc(h1_done, 1)

                        def c2(t, s, j):
                            act.wait_ge(g1_done, t + 1)
                            if late(t):
                                act.wait_ge(m2_done, t - 1)
                            act.copy(gs[:, s, :, :], pG[s][:, :].rearrange("p (b d) -> p b d", b=TB)).then_inc(gs_done, 1)

                        def r2(t, s, j):
                            act.wait_ge(h2p_done, t + 1)
                            if late(t):
                                act.wait_ge(lo_done, t - 1)
                            act.activation(h2[:, s, :, :], h2p[:, s, :, :], ACT.Relu).then_inc(h2_done, 1)
                        act.wait_ge(picked_ok, 1)
                        act.activation(logs[:, :], picked[:, :], ACT.Ln, bias=log_eps[:, 0:1]).then_inc(log_ok, 1)
                        pipeline(act, NT, [(1, c1), (2, r1), (3, c2), (4, r2)])

                    @block.vector
                    def _(dve):
                        def fetch(t, s, j):
                            if late(t):
                                dve.wait_ge(a_done, t - 1)
                            dve.tensor_copy(xc[:, s, :, :], XS[:, ds(t * TB, TB), :]).then_inc(c_done, 1)

                        def a1(t, s, j):
                            dve.wait_ge(g0_done, t + 1)
                            if late(t):
                                dve.wait_ge(h1_done, t - 1)
                            dve.tensor_tensor(h1p[:, s, :, :], pH1[s][:, :].rearrange("p (b d) -> p b d", b=TB),
                                              B0[:, :].unsqueeze(1).broadcast_to([P, TB, P]), ALU.add).then_inc(h1p_done, 1)

                        def a2(t, s, j):
                            dve.wait_ge(m2_done, t + 1)
                            if late(t):
                                dve.wait_ge(h2_done, t - 1)
                            dve.tensor_tensor(h2p[:, s, :, :], pH2[s][:, :].rearrange("p (b d) -> p b d", b=TB),
                                              B1[:, :].unsqueeze(1).broadcast_to([P, TB, P]), ALU.add).then_inc(h2p_done, 1)
                            dve.wait_ge(h2p_done, t + 1)
                            dve.tensor_scalar(H_hi[:, ds(t * TB, TB), :], h2p[:, s, :, :], 0.0, None, ALU.max).then_inc(hi_done, 1)
                        dve.tensor_reduce(picked[:, :], dst1h[:, :, :], AX.X, ALU.add).then_inc(picked_ok, 1)
                        pipeline(dve, NT, [(0, fetch), (2, a1), (4, a2)])
                        dve.wait_ge(logrow_ps, 1)
                        dve.tensor_copy(log_adj[:, :], pAg[0][:, 0:NE])

            with Scope(nc) as sc:
                S_c = sc.sb("S_c", [P, LT, TC])
                S_hi = sc.sb("S_hi", [P, LT, TC], F32R)
                S_lo = sc.sb("S_lo", [P, LT, TC], F32R)
                G = sc.sb("G", [P, 2, 4, TC])
                fc = sc.sb("fc", [P, TC])
                ig = sc.sb("ig", [P, TC])
                tc_ = sc.sb("tc_", [P, 2, TC])
                hf = sc.sb("hf", [P, 2, TC])
                pG = [[sc.ps(f"pG{i}{g}") for g in range(4)] for i in range(2)]
                gate_ps, gate_sb, cell_done, tanh_done, h_done, hi_done, lo_done, fc_done, ig_done = (
                    sc.sem(n) for n in ("gate_ps", "gate_sb", "cell_done", "tanh_done", "h_done", "hi_done", "lo_done", "fc_done", "ig_done"))
                FIRST, LATER = (0, 2, 3), (1, 0, 2, 3)
                NW = [P // p for p in range(1, SKIPS + 1)]
                TBS = [4, 8, 8, 16]
                GROUPS = [NB // (tb * LT) for tb in TBS]

                class Count:

                    def __init__(self, n, g, l):
                        self.n, self.g, self.l = n, g, l

                def steps(visit, eng):
                    n = g = l = 0
                    for pi in range(SKIPS):
                        p = pi + 1
                        per_n = LT * p
                        per_l = LT * (p - 1)
                        per_g = LT * 3 + per_l * 4

                        def group(it, n0, g0, l0):
                            dn = dg = dl = 0
                            for step in range(p):
                                for k in range(LT):
                                    visit(pi, step, it, k, Count(n0 + dn, g0 + dg, l0 + dl), dn)
                                    dn += 1
                                    dg += 3 if step == 0 else 4
                                    dl += step > 0
                        if pi == 0:
                            group(0, n, g, l)
                            with eng.Fori(1, GROUPS[0]) as it:
                                group(it, n + per_n * it, g + per_g * it, l)
                        elif GROUPS[pi] > 1:
                            with eng.Fori(0, GROUPS[pi]) as it:
                                group(it, n + per_n * it, g + per_g * it, l + per_l * it)
                        else:
                            group(0, n, g, l)
                        n += per_n * GROUPS[pi]
                        g += per_g * GROUPS[pi]
                        l += per_l * GROUPS[pi]

                def windows(Hx, pi, step, it, k):
                    tb, p = TBS[pi], pi + 1
                    return Hx[:, ds((it * LT + k) * tb, tb), step:step + p * (NW[pi] - 1) + 1:p]

                def cols(ap, pi):
                    n = TBS[pi] * NW[pi]
                    return ap[:, 0:n]

                def grid(ap, pi):
                    return cols(ap, pi).rearrange("p (b w) -> p b w", b=TBS[pi])

                def gates(step):
                    return LATER if step else FIRST

                with nc.Block() as block:
                    @block.tensor
                    def _(pe):
                        def visit(pi, step, it, k, c, dn):
                            s = dn % 2
                            early = isinstance(c.n, int) and c.n < 2
                            if not early:
                                pe.wait_ge(gate_sb, c.g - gates_at(pi, dn, 1))
                            if pi > 0 and step == 0:
                                pe.wait_ge(lo_done, c.n - LT + 1)
                            if step > 0:
                                pe.wait_ge(lo_done, c.n - LT + 1)
                            for g in gates(step):
                                bank = pG[s][g][:, 0:TBS[pi] * NW[pi]]
                                wx = slice(P * g, P * g + P)
                                parts = [(WT_hi[:, pi, wx], windows(H_hi, pi, step, it, k)),
                                         (WT_hi[:, pi, wx], windows(H_lo, pi, step, it, k)),
                                         (WT_lo[:, pi, wx], windows(H_hi, pi, step, it, k))]
                                if step:
                                    w = SKIPS - 1 + pi
                                    parts += [(WT_hi[:, w, wx], cols(S_hi[:, k, :], pi)),
                                              (WT_hi[:, w, wx], cols(S_lo[:, k, :], pi)),
                                              (WT_lo[:, w, wx], cols(S_hi[:, k, :], pi))]
                                for i, (w, h) in enumerate(parts):
                                    ins = pe.matmul(bank, w, h, start=(i == 0), stop=(i == len(parts) - 1))
                                ins.then_inc(gate_ps, 1)

                        def gates_at(pi, dn, back):
                            d = dn - back
                            if d >= 0:
                                return 3 if d < LT else 4
                            return GATES_PREV[pi]
                        GATES_PREV = [3, 3, 4, 4]
                        steps(visit, pe)

                    @block.scalar
                    def _(act):
                        def visit(pi, step, it, k, c, dn):
                            s = dn % 2
                            if not (isinstance(c.n, int) and c.n < 2):
                                act.wait_ge(h_done, c.n - 1)
                            for i, g in enumerate(gates(step)):
                                act.wait_ge(gate_ps, c.g + i + 1)
                                act.activation(cols(G[:, s, g, :], pi), pG[s][g][:, 0:TBS[pi] * NW[pi]],
                                               ACT.Tanh if g == 2 else ACT.Sigmoid,
                                               bias=lstm_b[:, 4 * pi + g:4 * pi + g + 1]).then_inc(gate_sb, 1)
                            act.wait_ge(cell_done, c.n + 1)
                            act.activation(cols(tc_[:, s, :], pi), cols(S_c[:, k, :], pi), ACT.Tanh).then_inc(tanh_done, 1)
                        steps(visit, act)

                    @block.vector
                    def _(dve):
                        def visit(pi, step, it, k, c, dn):
                            s = dn % 2
                            i_, f_, g_, o_ = (cols(G[:, s, g, :], pi) for g in range(4))
                            cell = cols(S_c[:, k, :], pi)
                            order = gates(step)
                            if step:
                                dve.wait_ge(gate_sb, c.g + order.index(1) + 1)
                                dve.tensor_tensor(cols(fc[:, :], pi), f_, cell, ALU.mult).then_inc(fc_done, 1)
                                dve.wait_ge(gate_sb, c.g + max(order.index(0), order.index(2)) + 1)
                                dve.tensor_tensor(cols(ig[:, :], pi), i_, g_, ALU.mult).then_inc(ig_done, 1)
                                dve.wait_ge(fc_done, c.l + 1)
                                dve.wait_ge(ig_done, c.l + 1)
                                dve.tensor_tensor(cell, cols(fc[:, :], pi), cols(ig[:, :], pi), ALU.add).then_inc(cell_done, 1)
                            else:
                                dve.wait_ge(gate_sb, c.g + max(order.index(0), order.index(2)) + 1)
                                dve.tensor_tensor(cell, i_, g_, ALU.mult).then_inc(cell_done, 1)
                            dve.wait_ge(gate_sb, c.g + order.index(3) + 1)
                            dve.wait_ge(tanh_done, c.n + 1)
                            if not (isinstance(c.n, int) and c.n < 2):
                                dve.wait_ge(lo_done, c.n - 1)
                            h = cols(hf[:, s, :], pi)
                            dve.tensor_tensor(h, o_, cols(tc_[:, s, :], pi), ALU.mult).then_inc(h_done, 1)
                            dve.wait_ge(h_done, c.n + 1)
                            if step == pi:
                                to, h = windows(H_hi, pi, step, it, k), grid(hf[:, s, :], pi)
                            else:
                                to = cols(S_hi[:, k, :], pi)
                            dve.tensor_copy(to, h).then_inc(hi_done, 1)
                        steps(visit, dve)

                    @block.gpsimd
                    def _(pool):
                        def visit(pi, step, it, k, c, dn):
                            s = dn % 2
                            pool.wait_ge(hi_done, c.n + 1)
                            if step == pi:
                                to, hi, h = windows(H_lo, pi, step, it, k), windows(H_hi, pi, step, it, k), grid(hf[:, s, :], pi)
                            else:
                                to, hi, h = cols(S_lo[:, k, :], pi), cols(S_hi[:, k, :], pi), cols(hf[:, s, :], pi)
                            pool.tensor_tensor(to, h, hi.bitcast(F32), ALU.subtract).then_inc(lo_done, 1)
                        steps(visit, pool)

            l3 = Scope(nc)
            l3.__enter__()
            V_hi, V_lo = H_hi, H_lo
            with Scope(nc) as sc:
                hs = sc.sb("hs", [P, 2, TB, P])
                z2 = sc.sb("z2", [P, 2, TB, P])
                x3 = sc.sb("x3", [P, 2, TB, P])
                x3T = sc.sb("x3T", [P, 2, TB, P])
                Q_hi = sc.sb("Q_hi", [P, 2, TB, P], F32R)
                Q_lo = sc.sb("Q_lo", [P, 2, TB, P], F32R)
                zs = sc.sb("zs", [P, 2, 2, TC])
                L = sc.sb("L", [P, 2, 2, TC])
                sT = sc.sb("sT", [BH, 2, NE])
                n2 = Norm(sc, "n2", eps[:, 0:1])
                pT = sc.ps("pT")
                pX = sc.ps("pX")
                pQV = [sc.ps(f"pQV{i}") for i in range(2)]
                pE = [sc.ps(f"pE{i}") for i in range(2)]
                pS = [sc.ps(f"pS{i}") for i in range(2)]
                hs_done, tr_done, z_done, x3_done, kept, trx_done, x3T_done, qv_ps, v_hi, q_lo, v_lo, e_ps, zs_done, l_done, s_ps, s_sb = (
                    sc.sem(n) for n in ("hs_done", "tr_done_f", "z_done_f", "x3_done", "kept", "trx_done", "x3T_done", "qv_ps", "v_hi", "q_lo",
                                        "v_lo", "e_ps", "zs_done", "l_done", "s_ps", "s_sb"))
                s_out = [sc.sem(f"s_out{i}") for i in range(2)]

                with nc.Block() as block:
                    @block.gpsimd
                    def _(pool):
                        def whole(t, s, j):
                            if late(t):
                                pool.wait_ge(tr_done, t - 1)
                            tl = ds(t * TB, TB)
                            pool.tensor_tensor(hs[:, s, :, :], H_hi[:, tl, :].bitcast(F32), H_lo[:, tl, :].bitcast(F32), ALU.add).then_inc(hs_done, 1)

                        def keep(t, s, j):
                            pool.wait_ge(x3_done, TB * t + TB)
                            pool.tensor_copy(XS[:, ds(t * TB, TB), :], x3[:, s, :, :]).then_inc(kept, 1)
                        pipeline(pool, NT, [(0, whole), (2, keep)])

                    @block.tensor
                    def _(pe):
                        def turn(t, s, j):
                            pe.wait_ge(hs_done, t + 1)
                            if late(t):
                                pe.wait_ge(z_done, t)
                            elif t:
                                pe.wait_ge(z_done, 1)
                            for b in range(TB):
                                ins = pe.transpose(pT[:, P * b:P * b + P], hs[:, s, b, :], ident[:, :])
                            ins.then_inc(tr_done, 1)

                        def turn_x(t, s, j):
                            if late(t):
                                pe.wait_ge(x3T_done, t)
                            elif t:
                                pe.wait_ge(x3T_done, 1)
                            for b in range(TB):
                                pe.wait_ge(x3_done, TB * t + b + 1)
                                ins = pe.transpose(pX[:, P * b:P * b + P], x3[:, s, b, :], ident[:, :])
                            ins.then_inc(trx_done, 1)

                        def project(t, s, j):
                            pe.wait_ge(x3T_done, t + 1)
                            for q in range(2):
                                if late(t) or t:
                                    pe.wait_ge(q_lo, 2 * t + q - 1)
                                    pe.wait_ge(v_lo, 2 * t + q - 1)
                                for b in (0, 1):
                                    ins = pe.matmul(pQV[q][:, 2 * P * b:2 * P * b + 2 * P], x3T[:, s, 2 * q + b, :], WQV[:, :], start=True, stop=True)
                                ins.then_inc(qv_ps, 1)

                        def gather(t, s, j):
                            for q in range(2):
                                pe.wait_ge(q_lo, 2 * t + q + 1)
                                if late(t) or t:
                                    pe.wait_ge(l_done, 2 * t + q - 1)
                                for b in (0, 1):
                                    for i, part in enumerate((Q_hi, Q_lo)):
                                        ins = pe.matmul(pE[q][:, NE * b:NE * b + NE], part[:, s, 2 * q + b, :], srcdstT[:, :], start=(i == 0), stop=(i == 1))
                                ins.then_inc(e_ps, 1)

                        def score(t, s, j):
                            if late(t):
                                pe.wait_ge(s_sb, t - 1)
                            for q in range(2):
                                pe.wait_ge(l_done, 2 * t + q + 1)
                                for b in (0, 1):
                                    u = 2 * q + b
                                    ins = pe.matmul(pS[s][0:BH, 0:NE], a_heads[:, u, :], L[:, s, q, NE * b:NE * b + NE], start=(u == 0), stop=(u == TB - 1))
                            ins.then_inc(s_ps, 1)
                        pipeline(pe, NT, [(1, turn), (4, gather), (2, turn_x), (3, project), (5, score)])

                    @block.scalar
                    def _(act):
                        def root(t, s, j):
                            n2.root(act, t, s)

                        def apply2(t, s, j):
                            if late(t):
                                act.wait_ge(kept, t - 1)
                                act.wait_ge(trx_done, t - 1)
                            n2.apply_act(act, z2[:, s, :, :], x3[:, s, :, :], t, s, x3_done)

                        def copy_x(t, s, j):
                            act.wait_ge(trx_done, t + 1)
                            if late(t):
                                act.wait_ge(qv_ps, 2 * t - 2)
                            act.copy(x3T[:, s, :, :], pX[:, :].rearrange("p (b d) -> p b d", b=TB)).then_inc(x3T_done, 1)

                        def high(t, s, j):
                            for q in range(2):
                                act.wait_ge(qv_ps, 2 * t + q + 1)
                                if late(t):
                                    act.wait_ge(e_ps, 2 * t + q - 3)
                                both = pQV[q][:, :].rearrange("p (b v d) -> p b v d", b=2, v=2)
                                act.copy(Q_hi[:, s, 2 * q:2 * q + 2, :], both[:, :, 0, :])
                                act.copy(V_hi[:, ds(t * TB + 2 * q, 2), :], both[:, :, 1, :]).then_inc(v_hi, 1)

                        def scale(t, s, j):
                            for q in range(2):
                                act.wait_ge(e_ps, 2 * t + q + 1)
                                if late(t):
                                    act.wait_ge(l_done, 2 * t + q - 3)
                                act.mul(zs[:, s, q, :], pE[q][:, :], SLOPE).then_inc(zs_done, 1)

                        def copy_s(t, s, j):
                            act.wait_ge(s_ps, t + 1)
                            if late(t):
                                act.wait_ge(s_out[s], 16 * j)
                            act.copy(sT[:, s, :], pS[s][0:BH, 0:NE]).then_inc(s_sb, 1)
                        pipeline(act, NT, [(4, scale), (1, root), (2, copy_x), (3, high), (1, apply2), (5, copy_s)])

                    @block.vector
                    def _(dve):
                        def stats2(t, s, j):
                            tl = ds(t * TB, TB)
                            dve.wait_ge(tr_done, t + 1)
                            if late(t):
                                dve.wait_ge(x3_done, TB * t - TB)
                            dve.tensor_tensor(z2[:, s, :, :], pT[:, :].rearrange("p (b d) -> p b d", b=TB), XS[:, tl, :], ALU.add).then_inc(z_done, 1)
                            dve.wait_ge(z_done, t + 1)
                            n2.stats(dve, z2[:, s, :, :], t, s)

                        def shift2(t, s, j):
                            n2.shift(dve, t, s)

                        def low(t, s, j):
                            for q in range(2):
                                both = pQV[q][:, :].rearrange("p (b v d) -> p b v d", b=2, v=2)
                                dve.wait_ge(v_hi, 2 * t + q + 1)
                                dve.tensor_tensor(Q_lo[:, s, 2 * q:2 * q + 2, :], both[:, :, 0, :], Q_hi[:, s, 2 * q:2 * q + 2, :].bitcast(F32), ALU.subtract).then_inc(q_lo, 1)
                                tl = ds(t * TB + 2 * q, 2)
                                dve.tensor_tensor(V_lo[:, tl, :], both[:, :, 1, :], V_hi[:, tl, :].bitcast(F32), ALU.subtract).then_inc(v_lo, 1)

                        def leaky(t, s, j):
                            for q in range(2):
                                dve.wait_ge(zs_done, 2 * t + q + 1)
                                if late(t):
                                    dve.wait_ge(s_ps, t - 1)
                                dve.tensor_tensor(L[:, s, q, :], pE[q][:, :], zs[:, s, q, :], ALU.max).then_inc(l_done, 1)
                        pipeline(dve, NT, [(1, stats2), (4, leaky), (1, shift2), (3, low)])

                    @block.sync
                    def _(sp):
                        def store(t, s, j):
                            sp.wait_ge(s_sb, t + 1)
                            sp.dma_start(score_rows[ds(t, 1), :, :].rearrange("o r e -> (o r) e"), sT[:, s, :]).then_inc(s_out[s], 16)
                        pipeline(sp, NT, [(0, store)])
                        for s in range(2):
                            sp.wait_ge(s_out[s], 16 * (NT // 2))

            att = l3.sb("att", [P, EC, NB * HEADS])
            with Scope(nc) as sc:
                BHN = NB * HEADS
                eT = sc.sb("eT", [P, 2, NE])
                run = sc.sb("run", [P, 2, NE])
                eE = sc.sb("eE", [P, EC, BHN])
                rE = sc.sb("rE", [P, EC, BHN])
                dE = sc.sb("dE", [P, EC, BHN])
                ex = sc.sb("ex", [P, EC, BHN])
                rd = sc.sb("rd", [P, EC, BHN])
                pEt, pRt, pM, pD = sc.ps("pEt"), sc.ps("pRt"), sc.ps("pM"), sc.ps("pD")
                e_in, e_ok, r_ok, et_ps, rt_ps, rE_ok, m_ps, d_ok, ex_ok, den_ps, chain = (
                    sc.sem(n) for n in ("e_in", "e_ok", "r_ok", "et_ps", "rt_ps", "rE_ok", "m_ps", "d_ok", "ex_ok", "den_ps", "chain_g"))
                wide = lambda ap: ap.rearrange("p c r -> p (c r)")
                with nc.Block() as block:
                    @block.sync
                    def _(sp):
                        sp.dma_start(eT[:, :, :], score_rows.rearrange("(f t) r e -> (t r) f e", f=2)).then_inc(e_in, 16)

                    @block.vector
                    def _(dve):
                        link = Chain(dve, chain)
                        dve.wait_ge(e_in, 16)
                        link(dve.tensor_tensor(eT[:, :, :], eT[:, :, :], log_adj[:, :].unsqueeze(1).broadcast_to([P, 2, NE]), ALU.add))
                        dve.engine_nop().then_inc(e_ok, 1)
                        for f in range(2):
                            link(dve.tensor_tensor_scan(run[:, f, :], restart[:, :], eT[:, f, :], FAR, ALU.add, ALU.max))
                        dve.engine_nop().then_inc(r_ok, 1)
                        dve.wait_ge(rt_ps, 1)
                        dve.tensor_copy(wide(rE[:, :, :]), pRt[:, :]).then_inc(rE_ok, 1)
                        dve.wait_ge(et_ps, 1)
                        link(dve.tensor_copy(wide(eE[:, :, :]), pEt[:, :]))
                        dve.wait_ge(m_ps, 1)
                        dve.tensor_tensor(wide(dE[:, :, :]), wide(eE[:, :, :]), pM[:, :], ALU.subtract).then_inc(d_ok, 1)
                        dve.wait_ge(den_ps, 1)
                        link(dve.reciprocal(wide(rd[:, :, :]), pD[:, :]))
                        link(dve.tensor_tensor(att[:, :, :], ex[:, :, :], rd[:, :, :], ALU.mult))

                    @block.scalar
                    def _(act):
                        act.wait_ge(d_ok, 1)
                        act.activation(wide(ex[:, :, :]), wide(dE[:, :, :]), ACT.Exp).then_inc(ex_ok, 1)

                    @block.tensor
                    def _(pe):
                        def turn(bank, rows, done):
                            for c in range(EC):
                                for f in range(2):
                                    ins = pe.transpose(bank[:, BHN * c + P * f:BHN * c + P * f + P], rows[:, f, P * c:P * c + P], ident[:, :])
                            ins.then_inc(done, 1)

                        def over_edges(bank, table, rows, done):
                            for c in range(EC):
                                for k in range(EC):
                                    ins = pe.matmul(bank[:, BHN * c:BHN * c + BHN], table[:, k, P * c:P * c + P], rows[:, k, :], start=(k == 0), stop=(k == EC - 1))
                            ins.then_inc(done, 1)
                        pe.wait_ge(e_ok, 1)
                        turn(pEt, eT, et_ps)
                        pe.wait_ge(r_ok, 1)
                        turn(pRt, run, rt_ps)
                        pe.wait_ge(rE_ok, 1)
                        over_edges(pM, last_of, rE, m_ps)
                        pe.wait_ge(ex_ok, 1)
                        over_edges(pD, same, ex, den_ps)

            with Scope(nc) as sc:
                pr = sc.sb("pr", [P, 2, EC, TB, P])
                yT = sc.sb("yT_h", [P, 2, TB, P])
                z3 = sc.sb("z3", [P, 2, TB, P])
                os_ = sc.sb("os_", [P, 2, TB, P])
                n3 = Norm(sc, "n3", eps[:, 0:1])
                pVg = [[sc.ps(f"pVg{i}{c}") for c in range(EC)] for i in range(2)]
                pY = [sc.ps(f"pY{i}") for i in range(2)]
                pZ = [sc.ps(f"pZ{i}") for i in range(2)]
                vg_ps, pr_done, y_ps, y_sb, o_ps, z_done, o_done = (
                    sc.sem(n) for n in ("vg_ps", "pr_done", "y_ps", "y_sb", "o_ps", "z_done_h", "o_done"))
                o_out = [sc.sem(f"o_out{i}") for i in range(2)]
                with nc.Block() as block:
                    @block.tensor
                    def _(pe):
                        def gather(t, s, j):
                            for c in range(EC):
                                if late(t):
                                    pe.wait_ge(pr_done, EC * t + c - 3)
                                for i, part in enumerate((V_hi, V_lo)):
                                    ins = pe.matmul(pVg[s][c][:, :], dstT[:, P * c:P * c + P], part[:, ds(t * TB, TB), :], start=(i == 0), stop=(i == 1))
                                ins.then_inc(vg_ps, 1)

                        def combine(t, s, j):
                            pe.wait_ge(pr_done, EC * t + EC)
                            if late(t):
                                pe.wait_ge(y_sb, t - 1)
                            for b in range(TB):
                                for c in range(EC):
                                    ins = pe.matmul(pY[s][:, P * b:P * b + P], pr[:, s, c, b, :], src1h[:, c, :], start=(c == 0), stop=(c == EC - 1))
                            ins.then_inc(y_ps, 1)

                        def output(t, s, j):
                            pe.wait_ge(y_sb, t + 1)
                            if late(t):
                                pe.wait_ge(z_done, t - 1)
                            for b in range(TB):
                                ins = pe.matmul(pZ[s][:, P * b:P * b + P], yT[:, s, b, :], WoT[:, :], start=True, stop=True)
                            ins.then_inc(o_ps, 1)
                        pipeline(pe, NT, [(0, gather), (1, combine), (2, output)])

                    @block.scalar
                    def _(act):
                        def copy_y(t, s, j):
                            act.wait_ge(y_ps, t + 1)
                            if late(t):
                                act.wait_ge(o_ps, t - 1)
                            act.copy(yT[:, s, :, :], pY[s][:, :].rearrange("p (b d) -> p b d", b=TB)).then_inc(y_sb, 1)

                        def root(t, s, j):
                            n3.root(act, t, s)

                        def apply3(t, s, j):
                            if late(t):
                                act.wait_ge(o_out[s], 16 * j)
                            n3.apply_act(act, z3[:, s, :, :], os_[:, s, :, :], t, s, o_done)
                        pipeline(act, NT, [(1, copy_y), (3, apply3), (2, root)])

                    @block.vector
                    def _(dve):
                        def weigh(t, s, j):
                            for c in range(EC):
                                dve.wait_ge(vg_ps, EC * t + c + 1)
                                if late(t):
                                    dve.wait_ge(y_ps, t - 1)
                                dve.tensor_tensor(pr[:, s, c, :, :].rearrange("p b (h d) -> p (b h) d", h=HEADS),
                                                  pVg[s][c][:, :].rearrange("p (r d) -> p r d", d=HD),
                                                  att[:, c, ds(t * BH, BH)].unsqueeze(2).broadcast_to([P, BH, HD]), ALU.mult).then_inc(pr_done, 1)

                        def stats3(t, s, j):
                            dve.wait_ge(o_ps, t + 1)
                            if late(t):
                                dve.wait_ge(o_done, TB * t - TB)
                            dve.tensor_tensor(z3[:, s, :, :], pZ[s][:, :].rearrange("p (b d) -> p b d", b=TB), XS[:, ds(t * TB, TB), :], ALU.add).then_inc(z_done, 1)
                            dve.wait_ge(z_done, t + 1)
                            n3.stats(dve, z3[:, s, :, :], t, s)

                        def shift3(t, s, j):
                            n3.shift(dve, t, s)
                        pipeline(dve, NT, [(0, weigh), (3, shift3), (2, stats3)])

                    @block.sync
                    def _(sp):
                        def store(t, s, j):
                            sp.wait_ge(o_done, TB * t + TB)
                            sp.dma_start(out_tiles[:, ds(t, 1), :, :].rearrange("n o b d -> n (o b) d"), os_[:, s, :, :]).then_inc(o_out[s], 16)
                        pipeline(sp, NT, [(0, store)])
                        for s in range(2):
                            sp.wait_ge(o_out[s], 16 * (NT // 2))
            l3.__exit__(None, None, None)


_INS = ['x', 'adj', 'L0_gnn_W1', 'L0_gnn_b1', 'L0_gnn_g1', 'L0_gnn_be1', 'L0_gnn_W2', 'L0_gnn_b2', 'L0_gnn_g2',
        'L0_gnn_be2', 'L1_gnn_W', 'L1_gnn_bias', 'L2_gnn_Wg0', 'L2_gnn_bg0', 'L2_gnn_Wg1', 'L2_gnn_bg1', 'L2_gnn_Wih',
        'L2_gnn_Whh', 'L2_gnn_bih', 'L2_gnn_bhh', 'L3_gnn_W_lin', 'L3_gnn_W_val', 'L3_gnn_a', 'L3_gnn_W_out',
        'L3_gnn_src', 'L3_gnn_dst']


def kernel(**inputs):
    import numpy as _np
    import concourse.bacc as _bacc
    from concourse import mybir as _mybir
    from concourse.bass_utils import run_bass_kernel_spmd as _run

    nc = _bacc.Bacc("TRN2", target_bir_lowering=False, num_devices=1)
    arrays, args = {}, []
    for name in _INS:
        a = _np.ascontiguousarray(inputs[name])
        arrays[f"in_{name}_dram"] = a
        args.append(nc.dram_tensor(f"in_{name}_dram", a.shape, _mybir.dt.from_np(a.dtype), kind="ExternalInput").ap())
    args.append(nc.dram_tensor("out_dram", (NB, P, P), F32, kind="ExternalOutput").ap())
    adj_resnorm_kernel(nc, *args)
    r = _run(nc, [arrays], core_ids=[0])
    return r.results[0]["out_dram"]
```

```python
from contextlib import ExitStack

import concourse.bass as bass
from concourse import mybir

ALU = mybir.AluOpType
ACT = mybir.ActivationFunctionType
AX = mybir.AxisListType
F32 = mybir.dt.float32
F32R = mybir.dt.float32r
I32 = mybir.dt.int32

P = 128
NB = 64
TB = 4
TC = TB * P
NT = NB // TB
NE = 256
EC = NE // P
HEADS = 4
HD = P // HEADS
BH = TB * HEADS
SKIPS = 4
STEPS = 4
EPS = 1e-5
LOG_EPS = 1e-8
SLOPE = 0.2
FAR = -3.0e38
ds = bass.ds

V_B1, V_G1, V_BE1, V_B2, V_G2, V_BE2, V_BG0, V_BG1, V_A, V_BIH, V_BHH, V_ALL = 0, 2, 4, 6, 7, 8, 9, 10, 11, 12, 28, 44


def pipeline(eng, n, stages, straight=0):
    depth = max(delay for delay, _ in stages)
    peel = -(-max(depth + 1, straight) // STEPS) * STEPS

    def step(t):
        for d, stage in stages:
            if 0 <= t - d < n:
                stage(t - d, (t - d) % 2, (t - d) // 2)

    for t in range(peel):
        step(t)
    with eng.Fori(peel // STEPS, n // STEPS) as turn:
        for u in range(STEPS):
            for d, stage in stages:
                stage(STEPS * turn + (u - d), (u - d) % 2, STEPS // 2 * turn + (u - d) // 2)
    for t in range(n, n + depth):
        step(t)


def late(t):
    return not isinstance(t, int) or t >= 2


def tile_of(ap, t):
    return ap[:, ds(t * TC, TC)]


class Scope:

    def __init__(self, nc):
        self.nc, self.ctx, self.n = nc, ExitStack(), 0

    def __enter__(self):
        self.ctx.__enter__()
        return self

    def __exit__(self, *e):
        return self.ctx.__exit__(*e)

    def sb(self, name, shape, dt=F32):
        return self.ctx.enter_context(self.nc.sbuf_tensor(name, shape, dt))

    def ps(self, name, shape=(P, TC)):
        return self.ctx.enter_context(self.nc.psum_tensor(name, list(shape), F32))

    def sem(self, name):
        return self.ctx.enter_context(self.nc.semaphore(name))


class Chain:

    def __init__(self, eng, sem):
        self.eng, self.sem, self.n = eng, sem, 0

    def __call__(self, ins):
        self.n += 1
        ins.then_inc(self.sem, 1)
        self.eng.wait_ge(self.sem, self.n)


class Norm:

    def __init__(self, sc, name, eps):
        self.st = sc.sb(name + "_st", [P, 2, TB, 6])
        self.mv = sc.sb(name + "_mv", [P, 2, TB, 2])
        self.spare = sc.sb(name + "_spare", [P, 1])
        self.sd = sc.sb(name + "_sd", [P, 2, TB])
        self.rs = sc.sb(name + "_rs", [P, 2, TB])
        self.sh = sc.sb(name + "_sh", [P, 2, TB])
        self.eps = eps
        self.stats_done = sc.sem(name + "_stats_done")
        self.var_done = sc.sem(name + "_var_done")
        self.sd_done = sc.sem(name + "_sd_done")
        self.rs_done = sc.sem(name + "_rs_done")
        self.sh_done = sc.sem(name + "_sh_done")

    def stats(self, dve, z, t, s):
        for b in range(TB):
            dve.bn_stats(self.st[:, s, b, :], z[:, b, :]).then_inc(self.stats_done, 1)
        dve.wait_ge(self.stats_done, TB * t + TB)
        dve.memset(self.spare[:, :], 0.0)
        for b in range(TB):
            dve.bn_aggr(self.mv[:, s, b, :], self.st[:, s, b, :]).then_inc(self.var_done, 1)

    def root(self, act, t, s):
        act.wait_ge(self.var_done, TB * t + TB)
        act.activation(self.sd[:, s, :], self.mv[:, s, :, 1], ACT.Sqrt, bias=self.eps).then_inc(self.sd_done, 1)

    def shift(self, dve, t, s):
        dve.wait_ge(self.sd_done, t + 1)
        dve.reciprocal(self.rs[:, s, :], self.sd[:, s, :]).then_inc(self.rs_done, 1)
        dve.wait_ge(self.rs_done, t + 1)
        dve.scalar_tensor_tensor(out=self.sh[:, s, :], in0=self.mv[:, s, :, 0], scalar=-1.0, in1=self.rs[:, s, :],
                                 op0=ALU.mult, op1=ALU.mult).then_inc(self.sh_done, 1)

    def apply_act(self, act, z, out, t, s, done):
        act.wait_ge(self.sh_done, t + 1)
        for b in range(TB):
            act.activation(out[:, b, :], z[:, b, :], ACT.Identity, scale=self.rs[:, s, b:b + 1],
                           bias=self.sh[:, s, b:b + 1]).then_inc(done, 1)

    def apply(self, dve, z, out, t, s, done):
        dve.wait_ge(self.sd_done, t + 1)
        dve.reciprocal(self.rs[:, s, :], self.sd[:, s, :]).then_inc(self.rs_done, 1)
        dve.wait_ge(self.rs_done, t + 1)
        for b in range(TB):
            ins = dve.tensor_scalar(out[:, b, :], z[:, b, :], self.mv[:, s, b, 0:1], self.rs[:, s, b:b + 1],
                                    ALU.subtract, ALU.mult)
            ins.then_inc(done, 1)


class SoftmaxBuffers:

    def __init__(self, sc):
        self.eT = sc.sb("eT", [P, NE])
        self.run = sc.sb("run", [P, NE])
        self.both = sc.sb("both", [P, 2, EC, P])
        self.dE = sc.sb("dE", [P, EC, P])
        self.ex = sc.sb("ex", [P, EC, P])
        self.rd = sc.sb("rd", [P, EC, P])
        self.e_in, self.chain, self.r_ok, self.turned, self.both_ok, self.m_ps, self.d_ok, self.ex_ok, self.den_ps = (
            sc.sem(n) for n in ("e_in", "soft_chain", "r_ok", "turned", "both_ok", "m_ps", "d_ok", "ex_ok", "den_ps"))


def wide(ap):
    return ap.rearrange("p c r -> p (c r)")


class Softmax:

    def __init__(self, f, buf, bank, score_rows, log_adj, restart, last_of, same, ident, att):
        self.f, self.buf, self.bank = f, buf, bank
        self.score_rows, self.log_adj, self.restart, self.last_of, self.same, self.ident = score_rows, log_adj, restart, last_of, same, ident
        self.att = att[:, :, P * f:P * f + P]

    def load(self, sp):
        half = self.score_rows[self.f * (NT // 2):(self.f + 1) * (NT // 2)]
        sp.dma_start(self.buf.eT[:, :], half.rearrange("t r e -> (t r) e")).then_inc(self.buf.e_in, 16)

    def scan(self, dve):
        eT = self.buf.eT[:, :]
        dve.wait_ge(self.buf.e_in, 16 * self.f + 16)
        dve.tensor_tensor(eT, eT, self.log_adj[:, :], ALU.add).then_inc(self.buf.chain, 1)
        dve.wait_ge(self.buf.chain, 3 * self.f + 1)
        dve.tensor_tensor_scan(self.buf.run[:, :], self.restart[:, :], eT, FAR, ALU.add, ALU.max).then_inc(self.buf.r_ok, 1)

    def turn(self, pe):
        pe.wait_ge(self.buf.r_ok, self.f + 1)
        for i, rows in enumerate((self.buf.eT, self.buf.run)):
            for c in range(EC):
                at = (EC * i + c) * P
                ins = pe.transpose(self.bank[:, at:at + P], rows[:, P * c:P * c + P], self.ident[:, :])
        ins.then_inc(self.buf.turned, 1)

    def copy(self, dve):
        dve.wait_ge(self.buf.turned, self.f + 1)
        dve.tensor_copy(self.buf.both[:, :, :, :].rearrange("p i c r -> p (i c r)"), self.bank[:, :]).then_inc(self.buf.both_ok, 1)

    def over_edges(self, pe, half, table, rows, done):
        for c in range(EC):
            at = (EC * half + c) * P
            for k in range(EC):
                ins = pe.matmul(self.bank[:, at:at + P], table[:, k, P * c:P * c + P], rows[:, k, :], start=(k == 0), stop=(k == EC - 1))
        ins.then_inc(done, 1)

    def maximum(self, pe):
        pe.wait_ge(self.buf.both_ok, self.f + 1)
        self.over_edges(pe, 0, self.last_of, self.buf.both[:, 1, :, :], self.buf.m_ps)

    def subtract(self, dve):
        dve.wait_ge(self.buf.m_ps, self.f + 1)
        dve.tensor_tensor(wide(self.buf.dE[:, :, :]), wide(self.buf.both[:, 0, :, :]), self.bank[:, 0:EC * P], ALU.subtract).then_inc(self.buf.d_ok, 1)

    def exp(self, act):
        act.wait_ge(self.buf.d_ok, self.f + 1)
        act.activation(wide(self.buf.ex[:, :, :]), wide(self.buf.dE[:, :, :]), ACT.Exp).then_inc(self.buf.ex_ok, 1)

    def total(self, pe):
        pe.wait_ge(self.buf.ex_ok, self.f + 1)
        self.over_edges(pe, 1, self.same, self.buf.ex, self.buf.den_ps)

    def divide(self, dve):
        dve.wait_ge(self.buf.den_ps, self.f + 1)
        dve.reciprocal(wide(self.buf.rd[:, :, :]), self.bank[:, EC * P:2 * EC * P]).then_inc(self.buf.chain, 1)
        dve.wait_ge(self.buf.chain, 3 * self.f + 2)
        dve.tensor_tensor(self.att, self.buf.ex[:, :, :], self.buf.rd[:, :, :], ALU.mult).then_inc(self.buf.chain, 1)
        dve.wait_ge(self.buf.chain, 3 * self.f + 3)


def at_tiles(steps):
    def stage(t, s, j):
        if isinstance(t, int) and t in steps:
            steps[t]()
    return stage


def adj_resnorm_kernel(nc, x, adj, W1, b1, g1, be1, W2, b2, g2, be2, W3, bias3, Wg0, bg0, Wg1, bg1,
                       Wih, Whh, bih, bhh, W_lin, W_val, a, W_out, src, dst, out):
    x_tiles = x.rearrange("(t b) n d -> n t b d", b=TB)
    out_tiles = out.rearrange("(t b) n d -> n t b d", b=TB)
    score_rows = nc.dram_tensor("score_rows", [NT, BH, NE], F32, kind="Internal").ap()

    with Scope(nc) as top:
        sb = top.sb
        eps = sb("eps", [P, 1])
        log_eps = sb("log_eps", [P, 1])
        ident = sb("ident", [P, P])
        vec = sb("vec", [P, V_ALL])
        lstm_b = sb("lstm_b", [P, SKIPS * 4])
        adjT = sb("adjT", [P, P])
        hatT = sb("hatT", [P, P])
        W2T = sb("W2T", [P, 2, P])
        W3s = sb("W3s", [P, 3, P])
        bias3_all = sb("bias3_all", [P, P])
        Wg0s = sb("Wg0s", [P, P])
        Wg1s = sb("Wg1s", [P, P])
        B0 = sb("B0", [P, P])
        B1 = sb("B1", [P, P])
        WQV = sb("WQV", [P, 2 * P])
        WQV_hi, WQV_lo = sb("WQV_hi", [P, 2 * P], F32R), sb("WQV_lo", [P, 2 * P], F32R)
        WoT = sb("WoT", [P, P])
        a_heads = sb("a_heads", [P, TB, BH])
        srcdstT = sb("srcdstT", [P, NE], F32R)
        dstT = sb("dstT", [P, NE], F32R)
        src1h = sb("src1h", [P, EC, P])
        same = sb("same", [P, EC, NE])
        last_of = sb("last_of", [P, EC, NE])
        restart = sb("restart", [P, NE])
        log_adj = sb("log_adj", [P, NE])
        XS = sb("XS", [P, NB, P])
        WT_hi = sb("WT_hi", [P, 2 * SKIPS - 1, 4 * P], F32R)
        WT_lo = sb("WT_lo", [P, 2 * SKIPS - 1, 4 * P], F32R)

        picked_rows = sb("picked_rows", [P, EC, P])
        dst1h = sb("dst1h", [P, EC, P])
        srcT = sb("srcT", [P, NE])
        A_sb = sb("A_sb", [P, P])
        iota_row = sb("iota_row", [P, NE])
        iota_col = sb("iota_col", [P, EC])
        srow = sb("srow", [P, 2, NE])
        scol = sb("scol", [P, EC, 2])
        picked = sb("picked", [P, EC])
        ones = sb("ones", [P, P])

        zero_scope = Scope(nc)
        zero_scope.__enter__()
        splitT = zero_scope.sb("splitT", [P, 3, P])
        splitT_hi = zero_scope.sb("splitT_hi", [P, 3, P], F32R)
        splitT_lo = zero_scope.sb("splitT_lo", [P, 3, P], F32R)
        OP = XS[:, :, :].rearrange("p b n -> p (b n)")
        aff1 = zero_scope.sb("aff1", [P, 2, 4])
        aff2 = zero_scope.sb("aff2", [P, 4])
        st1 = zero_scope.sb("st1", [P, 2, NT, 6])
        st2 = zero_scope.sb("st2", [P, NT, 6])
        mv1 = zero_scope.sb("mv1", [P, 2, 2])
        mv2 = zero_scope.sb("mv2", [P, 2])
        W1T_hi = zero_scope.sb("W1T_hi", [P, 2 * P], F32R)
        W1T_lo = zero_scope.sb("W1T_lo", [P, 2 * P], F32R)
        xs_c = zero_scope.sb("xs_c", [P, 2, TB, P])
        x_in_c = [zero_scope.sem(f"x_in_c{i}") for i in range(2)]
        hidden_scope = Scope(nc)
        hidden_scope.__enter__()
        HP = hidden_scope.sb("HP", [P, 2, NB * P])
        early = Scope(nc)
        early.__enter__()
        Wn = early.sb("Wn", [P, 2 * SKIPS - 1, 4, P])
        idx_row_i = early.sb("idx_row_i", [P, 2, NE], I32)
        idx_col_i = early.sb("idx_col_i", [P, 2, EC], I32)
        idx_col = early.sb("idx_col", [P, EC, 2])
        perm = early.sb("perm", [P, EC, NE])
        spread = early.sb("spread", [P, 2, EC, P])
        xs_a = early.sb("xs_a", [P, 2, TB, P])
        W2n = early.sb("W2n", [P, 2 * P])
        Wlin_n = early.sb("Wlin_n", [P, P])
        Wval_n = early.sb("Wval_n", [P, P])
        Wout_n = early.sb("Wout_n", [P, P])
        idx_in, turned_in, w_in = (early.sem(n) for n in ("idx_in", "turned_in", "w_in"))
        lw_in = [early.sem(f"lw_in{i}") for i in range(2)]
        x_in_a = [early.sem(f"x_in_a{i}") for i in range(2)]

        def load_x(sp, xs, x_in, t, s):
            sp.dma_start(xs[:, s, :, :], x_tiles[:, ds(t, 1), :, :].rearrange("n o b d -> n (o b) d")).then_inc(x_in[s], 16)

        with Scope(nc) as sc:
            A_norm = sc.sb("A_norm", [P, P])
            scaled = sc.sb("scaled", [P, P])
            diag_p = sc.sb("diag_p", [P, P])
            deg = sc.sb("deg", [P, 8])
            vrows = sc.sb("vrows", [V_ALL, P])
            W1n = sc.sb("W1n", [P, 2, P])
            adj_in, vec_in, w1_in = (sc.sem(n) for n in ("adj_in", "vec_in", "w1_in"))
            ident_ok, adjT_ps, adjT_sb = (sc.sem(n) for n in ("ident_ok", "adjT_ps", "adjT_sb"))
            norm_ok, col_ps, deg_ok, deg_root, scaled_ok, hat_ps = (sc.sem(n) for n in ("norm_ok", "col_ps", "deg_ok", "deg_root", "scaled_ok", "hat_ps"))
            vec_ps, w1_ps = sc.sem("vec_ps"), sc.sem("w1_ps")
            ones_ok, dve_chain, pool_chain = sc.sem("ones_ok"), sc.sem("dve_chain"), sc.sem("pool_chain")
            pW = sc.ps("pW")
            pA = sc.ps("pA")
            pV = sc.ps("pV")
            pL = sc.ps("pL")
            N_VEC = 11

            with nc.Block() as block:
                @block.sync
                def _(sp):
                    sp.dma_start(A_sb[:, :], adj).then_inc(adj_in, 16)
                    sp.dma_start(W1n[:, :, :], W1.rearrange("(k p) d -> p k d", p=P)).then_inc(w1_in, 16)
                    for v, at, k in ((b1, V_B1, 2), (g1, V_G1, 2), (be1, V_BE1, 2), (b2, V_B2, 1), (g2, V_G2, 1),
                                     (be2, V_BE2, 1), (bg0, V_BG0, 1), (bg1, V_BG1, 1)):
                        sp.dma_start(vrows[at:at + k, :], v.rearrange("(k p) -> k p", p=P)).then_inc(vec_in, 16)
                    sp.dma_start(vrows[V_A:V_A + 1, :], a.rearrange("h d -> (h d)").rearrange("(k p) -> k p", p=P)).then_inc(vec_in, 16)
                    sp.dma_start(vrows[V_BIH:V_BIH + 16, :], bih.rearrange("s (g p) -> (s g) p", p=P)).then_inc(vec_in, 16)
                    sp.dma_start(vrows[V_BHH:V_BHH + 16, :], bhh.rearrange("s (g p) -> (s g) p", p=P)).then_inc(vec_in, 16)
                    for i, v in enumerate((src, dst)):
                        sp.dma_start(idx_col_i[:, i, :], v.rearrange("(c p) -> p c", p=P), allow_slow_non_contiguous=True).then_inc(idx_in, 16)
                        sp.dma_start(idx_row_i[:, i, :], v.rearrange("(o e) -> o e", o=1).broadcast_to([P, NE])).then_inc(idx_in, 16)

                @block.scalar
                def _(act):
                    for t in range(2):
                        load_x(act, xs_a, x_in_a, t, t)
                    act.wait_ge(deg_ok, 1)
                    act.activation(deg[:, 5:6], deg[:, 4:5], ACT.Sqrt).then_inc(deg_root, 1)

                @block.gpsimd
                def _(pool):
                    link = Chain(pool, pool_chain)
                    link(pool.memset(ident[:, :], 0.0))
                    pool.affine_select(out=ident[:, :], in_=ident[:, :], compare_op=ALU.not_equal, fill=1.0,
                                       base=0, pattern=[[-1, P]], channel_multiplier=1).then_inc(ident_ok, 1)
                    pool.wait_ge(adjT_sb, 1)
                    for k, (op, base, mult, step) in enumerate(((ALU.is_equal, 0, 1, -1), (ALU.is_gt, 0, 1, -1), (ALU.is_gt, 0, -1, 1))):
                        pool.affine_select(out=splitT[:, k, :], in_=adjT[:, :], compare_op=op, fill=0.0,
                                           base=base, pattern=[[step, P]], channel_multiplier=mult)

                @block.vector
                def _(dve):
                    link = Chain(dve, dve_chain)
                    dve.memset(eps[:, :], EPS)
                    dve.memset(log_eps[:, :], LOG_EPS)
                    dve.memset(a_heads[:, :, :], 0.0).then_inc(ones_ok, 1)
                    dve.memset(ones[:, :], 1.0).then_inc(ones_ok, 1)
                    dve.wait_ge(adj_in, 16)
                    dve.wait_ge(ident_ok, 1)
                    link(dve.tensor_tensor(A_norm[:, :], A_sb[:, :], ident[:, :], ALU.add))
                    dve.tensor_tensor(diag_p[:, :], A_norm[:, :], ident[:, :], ALU.mult).then_inc(norm_ok, 1)
                    link(dve.tensor_reduce(deg[:, 0:1], A_norm[:, :], AX.X, ALU.add))
                    dve.wait_ge(norm_ok, 1)
                    link(dve.tensor_reduce(deg[:, 1:2], diag_p[:, :], AX.X, ALU.add))
                    link(dve.tensor_tensor(deg[:, 2:3], deg[:, 0:1], deg[:, 1:2], ALU.subtract))
                    dve.wait_ge(col_ps, 1)
                    link(dve.tensor_tensor(deg[:, 3:4], deg[:, 2:3], pL[:, 0:1], ALU.add))
                    dve.reciprocal(deg[:, 4:5], deg[:, 3:4]).then_inc(deg_ok, 1)
                    dve.wait_ge(adjT_ps, 1)
                    dve.tensor_copy(adjT[:, :], pA[:, 0:P]).then_inc(adjT_sb, 1)
                    dve.wait_ge(deg_root, 1)
                    dve.tensor_scalar(scaled[:, :], A_norm[:, :], deg[:, 5:6], None, ALU.mult).then_inc(scaled_ok, 1)
                    dve.wait_ge(w1_ps, 1)
                    link(dve.tensor_copy(W1T_hi[:, :], pW[:, 0:2 * P]))
                    dve.tensor_tensor(W1T_lo[:, :], pW[:, 0:2 * P], W1T_hi[:, :].bitcast(F32), ALU.subtract)
                    dve.wait_ge(hat_ps, 1)
                    dve.tensor_scalar(hatT[:, :], pA[:, P:2 * P], deg[:, 5:6], None, ALU.mult)
                    dve.wait_ge(vec_ps, 1)
                    dve.tensor_copy(vec[:, :], pV[:, 0:V_ALL])

                @block.tensor
                def _(pe):
                    pe.wait_ge(ident_ok, 1)
                    pe.wait_ge(adj_in, 16)
                    pe.transpose(pA[:, 0:P], A_sb[:, :], ident[:, :]).then_inc(adjT_ps, 1)
                    pe.wait_ge(norm_ok, 1)
                    pe.wait_ge(ones_ok, 2)
                    pe.matmul(pL[:, 0:1], A_norm[:, :], ones[:, 0:1], start=True, stop=True).then_inc(col_ps, 1)
                    pe.wait_ge(w1_in, 16)
                    for k in range(2):
                        ins = pe.transpose(pW[:, P * k:P * k + P], W1n[:, k, :], ident[:, :])
                    ins.then_inc(w1_ps, 1)
                    pe.wait_ge(scaled_ok, 1)
                    pe.transpose(pA[:, P:2 * P], scaled[:, :], ident[:, :]).then_inc(hat_ps, 1)
                    pe.wait_ge(vec_in, 16 * N_VEC)
                    pe.transpose(pV[:, 0:V_ALL], vrows[:, :], ident[0:V_ALL, 0:V_ALL]).then_inc(vec_ps, 1)

        def batchnorm(dve, act_sem, dve_sem, link, st, mv, aff, gamma, beta, k):
            link(dve.bn_aggr(mv, st))
            dve.engine_nop().then_inc(dve_sem, 1)
            dve.wait_ge(act_sem, k + 1)
            link(dve.reciprocal(aff[:, 1:2], aff[:, 0:1]))
            link(dve.tensor_tensor(aff[:, 2:3], gamma, aff[:, 1:2], ALU.mult))
            link(dve.tensor_tensor(aff[:, 1:2], mv[:, 0:1], aff[:, 2:3], ALU.mult))
            link(dve.tensor_tensor(aff[:, 3:4], beta, aff[:, 1:2], ALU.subtract))

        with Scope(nc) as sc:
            agg_hi = sc.sb("agg_hi", [P, 2, TC], F32R)
            agg_lo = sc.sb("agg_lo", [P, 2, TC], F32R)
            idx_row = sc.sb("idx_row", [P, 2, NE])
            iota_i = sc.sb("iota_i", [P, NE], I32)
            iota_ci = sc.sb("iota_ci", [P, EC], I32)
            key_row = sc.sb("key_row", [P, NE])
            key_col = sc.sb("key_col", [P, EC])
            lower = sc.sb("lower", [P, EC, NE])
            rank = sc.sb("rank", [P, EC])
            lower_ok, rank_ok = sc.sem("lower_ok"), sc.sem("rank_ok")
            pMix = [sc.ps(f"pMix{i}") for i in range(2)]
            pHid = [[sc.ps(f"pHid{i}{k}") for k in range(2)] for i in range(2)]
            pLW = [sc.ps(f"pLW{i}") for i in range(2)]
            xs, x_in = xs_a, x_in_a
            mix_done, agg_done, low_done, hid_done, hp_done, stat_done, var_done, root_done, chain = (
                sc.sem(n) for n in ("mix_done", "agg_done", "low_done", "hid_done", "hp_done", "stat_done", "var_done_a", "root_done_a", "chain_a"))
            part_ps, lw_hi, part_used, perm_ok, sorted_ps, pool_chain = (
                sc.sem(n) for n in ("part_ps", "lw_hi", "part_used", "perm_ok", "sorted_ps", "pool_chain_a"))
            N_PARTS = 2 + 2 * SKIPS - 1
            PART_OF = {t: part for part, t in enumerate([1, 2] + list(range(4, 4 + 2 * SKIPS - 1)))}
            turned_at = lambda t: PART_OF.get(t) if isinstance(t, int) else None
            with nc.Block() as block:
                @block.sync
                def _(sp):
                    for to, w in ((W2n, W2), (Wlin_n, W_lin), (Wval_n, W_val), (Wout_n, W_out)):
                        sp.dma_start(to[:, :], w).then_inc(turned_in, 16)

                    def lstm_weights(k):
                        if k >= 2:
                            sp.wait_ge(part_ps, k + 1)
                        w = Wih[k:k + 1] if k < SKIPS else Whh[k - SKIPS + 1:k - SKIPS + 2]
                        sp.dma_start(Wn[:, k, :, :], w.rearrange("p (g r) d -> r (p g) d", r=P)).then_inc(lw_in[k % 2], 16)

                    def later_weights():
                        sp.dma_start(W3s[:, :, :], W3.rearrange("k f o -> f k o")).then_inc(w_in, 16)
                        sp.dma_start(Wg0s[:, :], Wg0).then_inc(w_in, 16)
                        sp.dma_start(Wg1s[:, :], Wg1).then_inc(w_in, 16)
                        sp.dma_start(bias3_all[:, :], bias3.rearrange("(o e) -> o e", o=1).broadcast_to([P, P])).then_inc(w_in, 16)

                    def load(t, s, j):
                        if late(t):
                            sp.wait_ge(mix_done, t - 1)
                            load_x(sp, xs, x_in, t, s)
                    pipeline(sp, NT, [(0, load), (0, at_tiles({k + (3 if k >= 2 else 2): lambda k=k: lstm_weights(k) for k in range(2 * SKIPS - 1)})),
                                      (0, at_tiles({10: later_weights}))], straight=12)

                @block.gpsimd
                def _(pool):
                    link = Chain(pool, pool_chain)
                    pool.iota(iota_i[:, :], pattern=[[1, NE]], base=0, channel_multiplier=0)
                    link(pool.iota(iota_ci[:, :], pattern=[[P, EC]], base=0, channel_multiplier=1))
                    pool.wait_ge(idx_in, 64)
                    pool.tensor_copy(iota_row[:, :], iota_i[:, :])
                    pool.tensor_copy(iota_col[:, :], iota_ci[:, :])
                    for i in range(2):
                        pool.tensor_copy(idx_row[:, i, :], idx_row_i[:, i, :])
                        link(pool.tensor_copy(idx_col[:, :, i], idx_col_i[:, i, :]))
                    pool.tensor_scalar(key_row[:, :], idx_row[:, 0, :], float(NE), None, ALU.mult)
                    link(pool.tensor_scalar(key_col[:, :], idx_col[:, :, 0], float(NE), None, ALU.mult))
                    pool.tensor_tensor(key_row[:, :], key_row[:, :], iota_row[:, :], ALU.add)
                    link(pool.tensor_tensor(key_col[:, :], key_col[:, :], iota_col[:, :], ALU.add))
                    for c in range(EC):
                        pool.tensor_scalar(lower[:, c, :], key_row[:, :], key_col[:, c:c + 1], None, ALU.is_lt).then_inc(lower_ok, 1)
                        for i in range(2):
                            link(pool.tensor_scalar(spread[:, i, c, :], ones[:, :], idx_col[:, c, i:i + 1], None, ALU.mult))
                    pool.wait_ge(rank_ok, 1)
                    for c in range(EC):
                        link(pool.tensor_scalar(perm[:, c, :], iota_row[:, :], rank[:, c:c + 1], None, ALU.is_equal))
                    pool.engine_nop().then_inc(perm_ok, 1)
                    pool.wait_ge(part_used, 1)
                    for whole, hi, lo in ((splitT[:, :, :], splitT_hi[:, :, :], splitT_lo[:, :, :]),
                                          (WQV[:, :], WQV_hi[:, :], WQV_lo[:, :])):
                        link(pool.tensor_copy(hi, whole))
                        pool.tensor_tensor(lo, whole, hi.bitcast(F32), ALU.subtract)

                @block.tensor
                def _(pe):
                    def turn_weights(t, s, j):
                        part = turned_at(t)
                        if part is None:
                            return
                        if part >= 2:
                            pe.wait_ge(part_used, part - 1)
                        bank = pLW[part % 2]
                        if part == 0:
                            pe.wait_ge(turned_in, 16 * 4)
                            for i, w in enumerate((W2n[:, 0:P], W2n[:, P:2 * P], Wlin_n[:, :], Wval_n[:, :])):
                                ins = pe.transpose(bank[:, P * i:P * i + P], w, ident[:, :])
                        elif part == 1:
                            pe.transpose(bank[:, 0:P], Wout_n[:, :], ident[:, :])
                            ins = pe.matmul(bank[:, P:2 * P], ones[:, :], adjT[:, :], start=True, stop=True)
                        else:
                            pe.wait_ge(lw_in[part % 2], 16 * (part // 2))
                            for g in range(4):
                                ins = pe.transpose(bank[:, P * g:P * g + P], Wn[:, part - 2, g, :], ident[:, :])
                        ins.then_inc(part_ps, 1)

                    def mix(t, s, j):
                        pe.wait_ge(x_in[s], 16 * j + 16)
                        if late(t):
                            pe.wait_ge(low_done, t - 1)
                        for b in range(TB):
                            ins = pe.matmul(pMix[s][:, P * b:P * b + P], xs[:, s, b, :], hatT[:, :], start=True, stop=True)
                        ins.then_inc(mix_done, 1)

                    def hidden(t, s, j):
                        pe.wait_ge(low_done, t + 1)
                        if late(t):
                            pe.wait_ge(hp_done, 2 * t - 2)
                        for k in range(2):
                            w = slice(P * k, P * k + P)
                            pe.matmul(pHid[s][k][:, :], W1T_hi[:, w], agg_hi[:, s, :], start=True, stop=False)
                            pe.matmul(pHid[s][k][:, :], W1T_hi[:, w], agg_lo[:, s, :], start=False, stop=False)
                            pe.matmul(pHid[s][k][:, :], W1T_lo[:, w], agg_hi[:, s, :], start=False, stop=True).then_inc(hid_done, 1)
                    pipeline(pe, NT, [(0, mix), (0, turn_weights), (1, hidden)], straight=12)
                    pe.wait_ge(perm_ok, 1)
                    pe.wait_ge(part_used, N_PARTS)
                    pe.wait_ge(w_in, 64)
                    for i in range(2):
                        for c in range(EC):
                            pe.matmul(pLW[0][:, NE * i:NE * i + NE], spread[:, i, c, :], perm[:, c, :],
                                      start=(c == 0), stop=(c == EC - 1))
                    for r in range(EC):
                        for c in range(EC):
                            ins = pe.matmul(pLW[1][:, 2 * r:2 * r + 2], perm[:, c, P * r:P * r + P], idx_col[:, c, :],
                                            start=(c == 0), stop=(c == EC - 1))
                    ins.then_inc(sorted_ps, 1)

                @block.scalar
                def _(act):
                    def lstm_high(t, s, j):
                        part = turned_at(t)
                        if part is not None and part >= 2:
                            act.wait_ge(part_ps, part + 1)
                            act.copy(WT_hi[:, part - 2, :], pLW[part % 2][:, :]).then_inc(lw_hi, 1)

                    def copy_mix(t, s, j):
                        act.wait_ge(mix_done, t + 1)
                        if late(t):
                            act.wait_ge(hid_done, 2 * t - 2)
                        act.copy(agg_hi[:, s, :], pMix[s][:, :]).then_inc(agg_done, 1)

                    def copy_hidden(t, s, j):
                        for k in range(2):
                            act.wait_ge(hid_done, 2 * t + k + 1)
                            act.activation(HP[:, k, ds(t * TC, TC)], pHid[s][k][:, :], ACT.Identity,
                                           bias=vec[:, V_B1 + k:V_B1 + k + 1]).then_inc(hp_done, 1)
                    pipeline(act, NT, [(0, copy_mix), (0, lstm_high), (1, copy_hidden)], straight=12)
                    act.wait_ge(sorted_ps, 1)
                    act.copy(srow[:, :, :], pLW[0][:, :].rearrange("p (i e) -> p i e", i=2))
                    act.copy(scol[:, :, :], pLW[1][:, 0:2 * EC].rearrange("p (c i) -> p c i", i=2))
                    for k in range(2):
                        act.wait_ge(var_done, k + 1)
                        act.activation(aff1[:, k, 0:1], mv1[:, k, 1:2], ACT.Sqrt, bias=eps[:, 0:1]).then_inc(root_done, 1)

                @block.vector
                def _(dve):
                    def take_weights(t, s, j):
                        part = turned_at(t)
                        if part is None:
                            return
                        bank = pLW[part % 2]
                        dve.wait_ge(part_ps, part + 1)
                        if part == 0:
                            dve.tensor_copy(W2T[:, :, :].rearrange("p k o -> p (k o)"), bank[:, 0:2 * P])
                            dve.tensor_copy(WQV[:, :], bank[:, 2 * P:4 * P]).then_inc(part_used, 1)
                        elif part == 1:
                            dve.tensor_copy(WoT[:, :], bank[:, 0:P])
                            dve.tensor_scalar(B0[:, :], bank[:, P:2 * P], vec[:, V_BG0:V_BG0 + 1], None, ALU.mult)
                            dve.tensor_scalar(B1[:, :], bank[:, P:2 * P], vec[:, V_BG1:V_BG1 + 1], None, ALU.mult).then_inc(part_used, 1)
                        else:
                            dve.wait_ge(lw_hi, part - 1)
                            dve.tensor_tensor(WT_lo[:, part - 2, :], bank[:, :], WT_hi[:, part - 2, :].bitcast(F32),
                                              ALU.subtract).then_inc(part_used, 1)

                    def count_lower():
                        dve.wait_ge(lower_ok, EC)
                        dve.tensor_reduce(rank[:, :], lower[:, :, :], AX.X, ALU.add).then_inc(rank_ok, 1)

                    def vectors():
                        dve.tensor_tensor(lstm_b[:, :], vec[:, V_BIH:V_BHH], vec[:, V_BHH:V_ALL], ALU.add)
                        for u in range(TB):
                            for h in range(HEADS):
                                rows = slice(HD * h, HD * h + HD)
                                dve.tensor_copy(a_heads[rows, u, HEADS * u + h:HEADS * u + h + 1], vec[rows, V_A:V_A + 1])

                    def low(t, s, j):
                        dve.wait_ge(agg_done, t + 1)
                        dve.tensor_tensor(agg_lo[:, s, :], pMix[s][:, :], agg_hi[:, s, :].bitcast(F32), ALU.subtract).then_inc(low_done, 1)

                    def stats(t, s, j):
                        for k in range(2):
                            dve.wait_ge(hp_done, 2 * t + k + 1)
                            dve.bn_stats(st1[:, k, ds(t, 1), :].rearrange("p o s -> p (o s)"), HP[:, k, ds(t * TC, TC)]).then_inc(stat_done, 1)
                    pipeline(dve, NT, [(0, low), (0, take_weights), (2, stats), (0, at_tiles({3: vectors, 8: count_lower}))], straight=12)
                    dve.wait_ge(stat_done, 2 * NT)
                    link = Chain(dve, chain)
                    for k in range(2):
                        batchnorm(dve, root_done, var_done, link, st1[:, k, :, :], mv1[:, k, :], aff1[:, k, :],
                                  vec[:, V_G1 + k:V_G1 + k + 1], vec[:, V_BE1 + k:V_BE1 + k + 1], k)
        early.__exit__(None, None, None)

        with Scope(nc) as sc:
            hr = sc.sb("hr", [P, 2, 2, TC])
            less = sc.sb("less", [P, EC, NE])
            less_ok, ends_ok = sc.sem("less_ok"), sc.sem("ends_ok")
            ends = sc.sb("ends", [P, EC])
            is_last = sc.sb("is_last", [P, EC])
            pOut = [sc.ps(f"pOut_b{i}") for i in range(2)]
            pPick = sc.ps("pPick")
            src_ok, picked_ps, pool_chain = sc.sem("src_ok"), sc.sem("picked_ps"), sc.sem("pool_chain_b")
            relu_done, out_done, op_done, stat_done, var_done, root_done, chain = (
                sc.sem(n) for n in ("relu_done", "out_done_b", "op_done", "stat_done_b", "var_done_b", "root_done_b", "chain_b"))
            with nc.Block() as block:
                @block.sync
                def _(sp):
                    for t in range(2):
                        load_x(sp, xs_c, x_in_c, t, t)

                @block.scalar
                def _(act):
                    def relu(t, s, j):
                        if late(t):
                            act.wait_ge(out_done, t - 1)
                        for k in range(2):
                            act.activation(hr[:, s, k, :], HP[:, k, ds(t * TC, TC)], ACT.Relu, scale=aff1[:, k, 2:3],
                                           bias=aff1[:, k, 3:4]).then_inc(relu_done, 1)
                    pipeline(act, NT, [(0, relu)])
                    act.wait_ge(picked_ps, 1)
                    act.copy(picked_rows[:, :, :], pPick[:, 0:EC * P].rearrange("p (c n) -> p c n", c=EC))
                    act.wait_ge(var_done, 1)
                    act.activation(aff2[:, 0:1], mv2[:, 1:2], ACT.Sqrt, bias=eps[:, 0:1]).then_inc(root_done, 1)

                @block.tensor
                def _(pe):
                    def second(t, s, j):
                        if late(t):
                            pe.wait_ge(op_done, t - 1)
                        for k in range(2):
                            pe.wait_ge(relu_done, 2 * t + k + 1)
                            ins = pe.matmul(pOut[s][:, :], W2T[:, k, :], hr[:, s, k, :], start=(k == 0), stop=(k == 1))
                        ins.then_inc(out_done, 1)
                    pipeline(pe, NT, [(0, second)])
                    pe.wait_ge(src_ok, 1)
                    for c in range(EC):
                        ins = pe.matmul(pPick[:, P * c:P * c + P], srcT[:, P * c:P * c + P], A_sb[:, :], start=True, stop=True)
                    ins.then_inc(picked_ps, 1)

                @block.gpsimd
                def _(pool):
                    link = Chain(pool, pool_chain)
                    for c in range(EC):
                        pool.tensor_scalar(less[:, c, :], srow[:, 0, :], scol[:, c, 0:1], None, ALU.is_le).then_inc(less_ok, 1)
                    pool.tensor_scalar(srcT[:, :], srow[:, 0, :], iota_col[:, 0:1], None, ALU.is_equal).then_inc(src_ok, 1)
                    link(pool.tensor_scalar(dstT[:, :], srow[:, 1, :], iota_col[:, 0:1], None, ALU.is_equal))
                    pool.wait_ge(src_ok, 1)
                    link(pool.tensor_tensor(srcdstT[:, :], srcT[:, :], dstT[:, :].bitcast(F32), ALU.add))
                    for c in range(EC):
                        pool.tensor_scalar(src1h[:, c, :], iota_row[:, 0:P], scol[:, c, 0:1], None, ALU.is_equal)
                        pool.tensor_scalar(dst1h[:, c, :], iota_row[:, 0:P], scol[:, c, 1:2], None, ALU.is_equal)
                        link(pool.tensor_scalar(same[:, c, :], srow[:, 0, :], scol[:, c, 0:1], None, ALU.is_equal))
                    pool.wait_ge(ends_ok, 1)
                    link(pool.tensor_tensor(ends[:, :], ends[:, :], iota_col[:, :], ALU.subtract))
                    link(pool.tensor_scalar(is_last[:, :], ends[:, :], 1.0, None, ALU.is_equal))
                    for c in range(EC):
                        pool.tensor_scalar(last_of[:, c, :], same[:, c, :], is_last[:, c:c + 1], None, ALU.mult)
                    pool.memset(restart[:, 0:1], 0.0)
                    link(pool.tensor_tensor(restart[:, 1:NE], srow[:, 0, 1:NE], srow[:, 0, 0:NE - 1], ALU.subtract))
                    pool.tensor_scalar(restart[:, 1:NE], restart[:, 1:NE], 0.0, FAR, ALU.is_gt, ALU.mult)

                @block.vector
                def _(dve):
                    def copy(t, s, j):
                        dve.wait_ge(out_done, t + 1)
                        dve.tensor_scalar(tile_of(OP, t), pOut[s][:, :], vec[:, V_B2:V_B2 + 1], None, ALU.add).then_inc(op_done, 1)

                    def stats(t, s, j):
                        dve.wait_ge(op_done, t + 1)
                        dve.bn_stats(st2[:, ds(t, 1), :].rearrange("p o s -> p (o s)"), tile_of(OP, t)).then_inc(stat_done, 1)
                    def count_ends(t, s, j):
                        if isinstance(t, int) and t == 6:
                            dve.wait_ge(less_ok, EC)
                            dve.tensor_reduce(ends[:, :], less[:, :, :], AX.X, ALU.add).then_inc(ends_ok, 1)
                    pipeline(dve, NT, [(1, stats), (0, copy), (1, count_ends)], straight=8)
                    dve.wait_ge(stat_done, NT)
                    batchnorm(dve, root_done, var_done, Chain(dve, chain), st2[:, :, :], mv2[:, :], aff2[:, :],
                              vec[:, V_G2:V_G2 + 1], vec[:, V_BE2:V_BE2 + 1], 0)

        hidden_scope.__exit__(None, None, None)

        with Scope(nc) as sc:
            xs, x_in = xs_c, x_in_c
            yT = sc.sb("yT_c", [P, 2, TC])
            z0 = sc.sb("z0", [P, 2, TB, P])
            x1 = sc.sb("x1", [P, 2, TB, P])
            x1_hi = sc.sb("x1_hi", [P, 2, TB, P], F32R)
            x1_lo = sc.sb("x1_lo", [P, 2, TB, P], F32R)
            mixed = sc.sb("mixed", [P, 2, 3, TB, P])
            z1 = sc.sb("z1", [P, 2, TB, P])
            pool_chain = sc.sem("pool_chain_c")
            n0, n1 = Norm(sc, "n0", eps[:, 0:1]), Norm(sc, "n1", eps[:, 0:1])
            pTr = [sc.ps(f"pTr{i}") for i in range(2)]
            pMx = [sc.ps(f"pMx{i}") for i in range(4)]
            pO = [sc.ps(f"pO_c{i}") for i in range(2)]
            hi_done, lo_done = sc.sem("hi_done_c"), sc.sem("lo_done_c")
            y_done, tr_done, z0_done, x1_done, xb_done, mx_done, mixed_done, prod_done, z1_done, x2_done = (
                sc.sem(n) for n in ("y_done", "tr_done", "z0_done", "x1_done", "xb_done", "mx_done", "mixed_done", "prod_done", "z1_done", "x2_done"))
            with nc.Block() as block:
                @block.sync
                def _(sp):
                    def load(t, s, j):
                        if late(t):
                            sp.wait_ge(z0_done, t - 1)
                            load_x(sp, xs, x_in, t, s)
                    pipeline(sp, NT, [(0, load)])

                @block.gpsimd
                def _(pool):
                    def low(t, s, j):
                        pool.wait_ge(hi_done, t + 1)
                        pool.tensor_tensor(x1_lo[:, s, :, :], x1[:, s, :, :], x1_hi[:, s, :, :].bitcast(F32), ALU.subtract).then_inc(lo_done, 1)

                    def add_bias(t, s, j):
                        pool.wait_ge(x1_done, TB * t + TB)
                        pool.tensor_tensor(XS[:, ds(t * TB, TB), :], x1[:, s, :, :],
                                           bias3_all[:, :].unsqueeze(1).broadcast_to([P, TB, P]), ALU.add).then_inc(xb_done, 1)
                    pipeline(pool, NT, [(2, low), (2, add_bias)])
                    link = Chain(pool, pool_chain)
                    for c in range(EC):
                        link(pool.tensor_tensor(dst1h[:, c, :], dst1h[:, c, :], picked_rows[:, c, :], ALU.mult))

                @block.tensor
                def _(pe):
                    def turn(t, s, j):
                        pe.wait_ge(y_done, t + 1)
                        if late(t):
                            pe.wait_ge(z0_done, t - 1)
                        for b in range(TB):
                            ins = pe.transpose(pTr[s][:, P * b:P * b + P], yT[:, s, P * b:P * b + P], ident[:, :])
                        ins.then_inc(tr_done, 1)

                    def mix(t, s, j):
                        pe.wait_ge(lo_done, t + 1)
                        for b in range(TB):
                            if late(t):
                                pe.wait_ge(mixed_done, TB * t + b - 3)
                            elif t:
                                pe.wait_ge(mixed_done, b + 1)
                            pe.matmul(pMx[b][:, 0:3 * P], x1_hi[:, s, b, :], splitT_hi[:, :, :], start=True, stop=False)
                            pe.matmul(pMx[b][:, 0:3 * P], x1_hi[:, s, b, :], splitT_lo[:, :, :], start=False, stop=False)
                            pe.matmul(pMx[b][:, 0:3 * P], x1_lo[:, s, b, :], splitT_hi[:, :, :], start=False, stop=True).then_inc(mx_done, 1)

                    def product(t, s, j):
                        if late(t):
                            pe.wait_ge(z1_done, t - 1)
                        for b in range(TB):
                            pe.wait_ge(mixed_done, TB * t + b + 1)
                            for k in range(3):
                                ins = pe.matmul(pO[s][:, P * b:P * b + P], mixed[:, s, k, b, :], W3s[:, k, :], start=(k == 0), stop=(k == 2))
                        ins.then_inc(prod_done, 1)
                    pipeline(pe, NT, [(1, turn), (3, product), (2, mix)])

                @block.scalar
                def _(act):
                    def norm_y(t, s, j):
                        if late(t):
                            act.wait_ge(tr_done, t - 1)
                        act.activation(yT[:, s, :], tile_of(OP, t), ACT.Identity, scale=aff2[:, 2:3], bias=aff2[:, 3:4]).then_inc(y_done, 1)

                    def high(t, s, j):
                        act.wait_ge(x1_done, TB * t + TB)
                        if late(t):
                            act.wait_ge(mx_done, TB * t - TB)
                        act.copy(x1_hi[:, s, :, :], x1[:, s, :, :]).then_inc(hi_done, 1)

                    def root0(t, s, j):
                        n0.root(act, t, s)

                    def copy_mixed(t, s, j):
                        for b in range(TB):
                            act.wait_ge(mx_done, TB * t + b + 1)
                            if late(t) and b == 0:
                                act.wait_ge(prod_done, t - 1)
                            act.copy(mixed[:, s, :, b, :], pMx[b][:, 0:3 * P].rearrange("p (k i) -> p k i", k=3)).then_inc(mixed_done, 1)

                    def root1(t, s, j):
                        n1.root(act, t, s)

                    def apply1(t, s, j):
                        n1.apply_act(act, z1[:, s, :, :], XS[:, ds(t * TB, TB), :], t, s, x2_done)

                    pipeline(act, NT, [(2, high), (0, norm_y), (1, root0), (5, apply1), (2, copy_mixed), (4, root1)])

                @block.vector
                def _(dve):
                    def stats0(t, s, j):
                        dve.wait_ge(tr_done, t + 1)
                        dve.wait_ge(x_in[s], 16 * j + 16)
                        dve.tensor_tensor(z0[:, s, :, :], pTr[s][:, :].rearrange("p (b d) -> p b d", b=TB), xs[:, s, :, :], ALU.add).then_inc(z0_done, 1)
                        dve.wait_ge(z0_done, t + 1)
                        n0.stats(dve, z0[:, s, :, :], t, s)

                    def apply0(t, s, j):
                        if late(t):
                            dve.wait_ge(lo_done, t - 1)
                            dve.wait_ge(xb_done, t - 1)
                        n0.apply(dve, z0[:, s, :, :], x1[:, s, :, :], t, s, x1_done)

                    def stats1(t, s, j):
                        dve.wait_ge(prod_done, t + 1)
                        dve.wait_ge(xb_done, t + 1)
                        if late(t):
                            dve.wait_ge(x2_done, TB * t - TB)
                        dve.tensor_tensor(z1[:, s, :, :], pO[s][:, :].rearrange("p (b d) -> p b d", b=TB), XS[:, ds(t * TB, TB), :], ALU.add).then_inc(z1_done, 1)
                        dve.wait_ge(z1_done, t + 1)
                        n1.stats(dve, z1[:, s, :, :], t, s)

                    def shift1(t, s, j):
                        n1.shift(dve, t, s)

                    pipeline(dve, NT, [(1, stats0), (5, shift1), (1, apply0), (4, stats1)])

        zero_scope.__exit__(None, None, None)

        with Scope(nc) as l2:
            H_hi = l2.sb("H_hi", [P, NB, P], F32R)
            H_lo = l2.sb("H_lo", [P, NB, P], F32R)

            with Scope(nc) as sc:
                logs = sc.sb("logs", [P, EC])
                log_spread = sc.sb("log_spread", [P, EC, P])
                picked_ok, log_ok, spread_ok, logrow_ps, pool_chain = (sc.sem(n) for n in ("picked_ok", "log_ok", "spread_ok", "logrow_ps", "pool_chain_d"))
                xc = sc.sb("xc", [P, 2, TB, P])
                ag = sc.sb("ag", [P, 2, TC])
                h1p = sc.sb("h1p", [P, 2, TB, P])
                h1 = sc.sb("h1", [P, 2, TB, P])
                gs = sc.sb("gs", [P, 2, TB, P])
                h2p = sc.sb("h2p", [P, 2, TB, P])
                h2 = sc.sb("h2", [P, 2, TB, P])
                pAg = [sc.ps(f"pAg{i}") for i in range(2)]
                pH1 = [sc.ps(f"pH1{i}") for i in range(2)]
                pG = [sc.ps(f"pG{i}") for i in range(2)]
                pH2 = [sc.ps(f"pH2{i}") for i in range(2)]
                c_done, a_done, ag_done, g0_done, h1p_done, h1_done, g1_done, gs_done, m2_done, h2p_done, hi_done, h2_done, lo_done = (
                    sc.sem(n) for n in ("c_done", "a_done", "ag_done", "g0_done", "h1p_done", "h1_done", "g1_done", "gs_done",
                                        "m2_done", "h2p_done", "hi_done_d", "h2_done", "lo_done_d"))
                with nc.Block() as block:
                    @block.gpsimd
                    def _(pool):
                        def low(t, s, j):
                            pool.wait_ge(h2_done, t + 1)
                            pool.wait_ge(hi_done, t + 1)
                            pool.tensor_tensor(H_lo[:, ds(t * TB, TB), :], h2[:, s, :, :], H_hi[:, ds(t * TB, TB), :].bitcast(F32), ALU.subtract).then_inc(lo_done, 1)
                        link = Chain(pool, pool_chain)

                        def spread_logs():
                            pool.wait_ge(log_ok, 1)
                            for c in range(EC):
                                link(pool.tensor_scalar(log_spread[:, c, :], ones[:, :], logs[:, c:c + 1], None, ALU.mult))
                            pool.engine_nop().then_inc(spread_ok, 1)
                        pipeline(pool, NT, [(5, low), (0, at_tiles({4: spread_logs}))])

                    @block.tensor
                    def _(pe):
                        def mix1(t, s, j):
                            pe.wait_ge(c_done, t + 1)
                            if late(t):
                                pe.wait_ge(ag_done, t - 1)
                            for b in range(TB):
                                ins = pe.matmul(pAg[s][:, P * b:P * b + P], xc[:, s, b, :], adjT[:, :], start=True, stop=True)
                            ins.then_inc(a_done, 1)

                        def prod1(t, s, j):
                            pe.wait_ge(ag_done, t + 1)
                            if late(t):
                                pe.wait_ge(h1p_done, t - 1)
                            pe.matmul(pH1[s][:, :], Wg0s[:, :], ag[:, s, :], start=True, stop=True).then_inc(g0_done, 1)

                        def prod2(t, s, j):
                            pe.wait_ge(h1_done, t + 1)
                            if late(t):
                                pe.wait_ge(gs_done, t - 1)
                            for b in range(TB):
                                ins = pe.matmul(pG[s][:, P * b:P * b + P], h1[:, s, b, :], Wg1s[:, :], start=True, stop=True)
                            ins.then_inc(g1_done, 1)

                        def mix2(t, s, j):
                            pe.wait_ge(gs_done, t + 1)
                            if late(t):
                                pe.wait_ge(h2p_done, t - 1)
                            for b in range(TB):
                                ins = pe.matmul(pH2[s][:, P * b:P * b + P], gs[:, s, b, :], adjT[:, :], start=True, stop=True)
                            ins.then_inc(m2_done, 1)
                        pipeline(pe, NT, [(1, mix1), (2, prod1), (3, prod2), (4, mix2)])
                        pe.wait_ge(spread_ok, 1)
                        pe.wait_ge(ag_done, NT)
                        for c in range(EC):
                            ins = pe.matmul(pAg[0][:, P * c:P * c + P], log_spread[:, c, :], ident[:, :], start=True, stop=True)
                        ins.then_inc(logrow_ps, 1)

                    @block.scalar
                    def _(act):
                        def c1(t, s, j):
                            act.wait_ge(a_done, t + 1)
                            if late(t):
                                act.wait_ge(g0_done, t - 1)
                            act.copy(ag[:, s, :], pAg[s][:, :]).then_inc(ag_done, 1)

                        def r1(t, s, j):
                            act.wait_ge(h1p_done, t + 1)
                            if late(t):
                                act.wait_ge(g1_done, t - 1)
                            act.activation(h1[:, s, :, :], h1p[:, s, :, :], ACT.Relu).then_inc(h1_done, 1)

                        def c2(t, s, j):
                            act.wait_ge(g1_done, t + 1)
                            if late(t):
                                act.wait_ge(m2_done, t - 1)
                            act.copy(gs[:, s, :, :], pG[s][:, :].rearrange("p (b d) -> p b d", b=TB)).then_inc(gs_done, 1)

                        def r2(t, s, j):
                            act.wait_ge(h2p_done, t + 1)
                            if late(t):
                                act.wait_ge(lo_done, t - 1)
                            act.activation(h2[:, s, :, :], h2p[:, s, :, :], ACT.Relu).then_inc(h2_done, 1)

                        def log_picked():
                            act.wait_ge(picked_ok, 1)
                            act.activation(logs[:, :], picked[:, :], ACT.Ln, bias=log_eps[:, 0:1]).then_inc(log_ok, 1)
                        pipeline(act, NT, [(1, c1), (2, r1), (3, c2), (4, r2), (0, at_tiles({3: log_picked}))])

                    @block.vector
                    def _(dve):
                        def fetch(t, s, j):
                            if late(t):
                                dve.wait_ge(a_done, t - 1)
                            dve.tensor_copy(xc[:, s, :, :], XS[:, ds(t * TB, TB), :]).then_inc(c_done, 1)

                        def a1(t, s, j):
                            dve.wait_ge(g0_done, t + 1)
                            if late(t):
                                dve.wait_ge(h1_done, t - 1)
                            dve.tensor_tensor(h1p[:, s, :, :], pH1[s][:, :].rearrange("p (b d) -> p b d", b=TB),
                                              B0[:, :].unsqueeze(1).broadcast_to([P, TB, P]), ALU.add).then_inc(h1p_done, 1)

                        def a2(t, s, j):
                            dve.wait_ge(m2_done, t + 1)
                            if late(t):
                                dve.wait_ge(h2_done, t - 1)
                            dve.tensor_tensor(h2p[:, s, :, :], pH2[s][:, :].rearrange("p (b d) -> p b d", b=TB),
                                              B1[:, :].unsqueeze(1).broadcast_to([P, TB, P]), ALU.add).then_inc(h2p_done, 1)
                            dve.wait_ge(h2p_done, t + 1)
                            dve.tensor_scalar(H_hi[:, ds(t * TB, TB), :], h2p[:, s, :, :], 0.0, None, ALU.max).then_inc(hi_done, 1)

                        def sum_picked():
                            dve.tensor_reduce(picked[:, :], dst1h[:, :, :], AX.X, ALU.add).then_inc(picked_ok, 1)
                        pipeline(dve, NT, [(0, fetch), (2, a1), (4, a2), (0, at_tiles({2: sum_picked}))])
                        dve.wait_ge(logrow_ps, 1)
                        dve.tensor_copy(log_adj[:, :], pAg[0][:, 0:NE])

            with Scope(nc) as sc:
                PLACES = 6
                S_c = sc.sb("S_c", [P, PLACES, TC])
                S_hi = sc.sb("S_hi", [P, PLACES, TC], F32R)
                S_lo = sc.sb("S_lo", [P, PLACES, TC], F32R)
                G = sc.sb("G", [P, 2, 4, TC])
                pG = [[sc.ps(f"pG{i}{g}") for g in range(4)] for i in range(2)]
                gate_ps, gate_sb, cell_done, tanh_done, h_done, hi_done, lo_done, fc_done, ig_done = (
                    sc.sem(n) for n in ("gate_ps", "gate_sb", "cell_done", "tanh_done", "h_done", "hi_done", "lo_done", "fc_done", "ig_done"))
                I, F, G_, O = range(4)
                FIRST, LATER = (I, G_, O), (F, I, G_, O)
                WINDOWS = [P // p for p in range(1, SKIPS + 1)]
                TILE_B = [4, 8, 8, 16]

                HEAD = [(0, k, 0, 0) for k in range(4)]
                LOOP_TURNS = 3
                LOOP = [(1, 0, 0, 2), (0, 4, 0, 4), (1, 1, 0, 2), (0, 5, 0, 4), (1, 0, 1, 2), (0, 6, 0, 4), (1, 1, 1, 2), (0, 7, 0, 4)]
                REST = [(pi, k, step, 0) for pi, k, step in (
                    (1, 6, 0), (2, 0, 0), (1, 7, 0), (2, 1, 0), (1, 6, 1), (2, 0, 1), (2, 2, 0), (1, 7, 1),
                    (2, 1, 1), (2, 3, 0), (2, 0, 2), (2, 2, 1), (2, 1, 2), (2, 4, 0), (2, 3, 1), (2, 2, 2),
                    (2, 5, 0), (2, 4, 1), (2, 3, 2), (3, 0, 0), (2, 5, 1), (2, 4, 2), (2, 6, 0), (3, 0, 1),
                    (2, 5, 2), (2, 7, 0), (2, 6, 1), (3, 0, 2), (3, 1, 0), (2, 7, 1), (2, 6, 2), (3, 1, 1),
                    (2, 7, 2), (3, 2, 0), (3, 1, 2), (3, 3, 0), (3, 2, 1), (3, 0, 3), (3, 3, 1), (3, 2, 2),
                    (3, 1, 3), (3, 3, 2), (3, 2, 3), (3, 3, 3))]
                PLAN = [(1, HEAD), (LOOP_TURNS, LOOP), (1, REST)]
                PLACE = {(pi, k): 2 * pi + k % 2 for part in (HEAD, LOOP) for pi, k, _, _ in part}
                free = [4, 5, 0, 2, 1, 3]
                for pi, k, step, _ in REST:
                    if step == 0:
                        PLACE[pi, k] = free.pop(0)
                    if step == pi:
                        free.append(PLACE[pi, k])
                ORDER = [(pi, k + more * it, step) for turns, part in PLAN for it in range(turns) for pi, k, step, more in part]

                def gates(step):
                    return LATER if step else FIRST

                def width(pi):
                    return TILE_B[pi] * WINDOWS[pi]

                def behind(pi, k, step):
                    if step:
                        return ORDER.index((pi, k, step - 1)) + 1
                    if pi == 0:
                        return 0
                    tb, tb_before = TILE_B[pi], TILE_B[pi - 1]
                    return max(ORDER.index((pi - 1, b // tb_before, pi - 1)) for b in range(k * tb, k * tb + tb, tb_before)) + 1

                class TileStep:

                    def __init__(self, pi, k, step, n, g, l, needs):
                        self.pi, self.k, self.step = pi, k, step
                        self.gates = gates(step)
                        self.n, self.g, self.l, self.needs = n, g, l, needs
                        self.fresh = isinstance(n, int) and n < 2
                        self.ends = self.step == pi

                    def windows(self, H):
                        tb, p = TILE_B[self.pi], self.pi + 1
                        return H[:, ds(self.k * tb, tb), self.step:self.step + p * (WINDOWS[self.pi] - 1) + 1:p]

                def over(eng, visit, flush):
                    n = g = l = 0
                    for turns, part in PLAN:
                        size = len(part)
                        per_g = sum(len(gates(step)) for _, _, step, _ in part)
                        per_l = sum(step > 0 for _, _, step, _ in part)
                        needs = [max(behind(pi, k + more * it, step) - size * it for it in range(turns)) for pi, k, step, more in part]

                        def turn(it):
                            dg = dl = 0
                            ts = None
                            for q, (pi, k, step, more) in enumerate(part):
                                prev = ts
                                ts = TileStep(pi, more * it + k, step, size * it + (n + q), per_g * it + (g + dg), per_l * it + (l + dl),
                                              size * it + needs[q] if needs[q] else None)
                                ts.slot = (n + q) % 2
                                ts.place = PLACE[pi, k]
                                visit(ts, prev)
                                dg += len(ts.gates)
                                dl += step > 0
                            flush(ts)
                        if turns > 1:
                            with eng.Fori(0, turns) as it:
                                turn(it)
                        else:
                            turn(0)
                        n += size * turns
                        g += per_g * turns
                        l += per_l * turns

                def cols(ap, ts):
                    return ap[:, 0:width(ts.pi)]

                with nc.Block() as block:
                    @block.tensor
                    def _(pe):
                        def visit(ts, prev):
                            if ts.needs is not None:
                                pe.wait_ge(lo_done, ts.needs)
                            for j, g in enumerate(ts.gates):
                                if not ts.fresh:
                                    pe.wait_ge(gate_sb, ts.g - (len(prev.gates) if prev else 3) - (len(ts.gates) - 1 - j))
                                wx = slice(P * g, P * g + P)
                                parts = [(WT_hi[:, ts.pi, wx], ts.windows(H_hi)), (WT_hi[:, ts.pi, wx], ts.windows(H_lo)),
                                         (WT_lo[:, ts.pi, wx], ts.windows(H_hi))]
                                if ts.step:
                                    w, h_hi, h_lo = SKIPS - 1 + ts.pi, cols(S_hi[:, ts.place, :], ts), cols(S_lo[:, ts.place, :], ts)
                                    parts += [(WT_hi[:, w, wx], h_hi), (WT_hi[:, w, wx], h_lo), (WT_lo[:, w, wx], h_hi)]
                                for i, (w, h) in enumerate(parts):
                                    ins = pe.matmul(cols(pG[ts.slot][g], ts), w, h, start=(i == 0), stop=(i == len(parts) - 1))
                                ins.then_inc(gate_ps, 1)
                        over(pe, visit, lambda ts: None)

                    @block.scalar
                    def _(act):
                        def gate(ts, i):
                            g = ts.gates[i]
                            if g == O and not ts.fresh:
                                act.wait_ge(lo_done, ts.n - 1)
                            act.wait_ge(gate_ps, ts.g + i + 1)
                            act.activation(cols(G[:, ts.slot, g, :], ts), cols(pG[ts.slot][g], ts),
                                           ACT.Tanh if g == G_ else ACT.Sigmoid,
                                           bias=lstm_b[:, 4 * ts.pi + g:4 * ts.pi + g + 1]).then_inc(gate_sb, 1)

                        def cell_tanh(ts):
                            act.wait_ge(cell_done, ts.n + 1)
                            act.activation(cols(G[:, ts.slot, G_, :], ts), cols(S_c[:, ts.place, :], ts), ACT.Tanh).then_inc(tanh_done, 1)

                        def visit(ts, prev):
                            if not ts.fresh:
                                act.wait_ge(h_done, ts.n - 1)
                            gate(ts, 0)
                            gate(ts, 1)
                            if prev:
                                cell_tanh(prev)
                            for i in range(2, len(ts.gates)):
                                gate(ts, i)
                        over(act, visit, cell_tanh)

                    @block.vector
                    def _(dve):
                        def finish(ts):
                            dve.wait_ge(gate_sb, ts.g + len(ts.gates))
                            dve.wait_ge(tanh_done, ts.n + 1)
                            h = cols(G[:, ts.slot, O, :], ts)
                            dve.tensor_tensor(h, cols(G[:, ts.slot, O, :], ts), cols(G[:, ts.slot, G_, :], ts), ALU.mult).then_inc(h_done, 1)
                            dve.wait_ge(h_done, ts.n + 1)
                            if ts.ends:
                                dve.tensor_copy(ts.windows(H_hi), h.rearrange("p (b w) -> p b w", b=TILE_B[ts.pi])).then_inc(hi_done, 1)
                            else:
                                dve.tensor_copy(cols(S_hi[:, ts.place, :], ts), h).then_inc(hi_done, 1)

                        def visit(ts, prev):
                            i_, f_, g_ = (cols(G[:, ts.slot, g, :], ts) for g in (I, F, G_))
                            cell = cols(S_c[:, ts.place, :], ts)
                            if ts.step:
                                dve.wait_ge(cell_done, ts.n)
                                dve.wait_ge(gate_sb, ts.g + 1)
                                dve.tensor_tensor(f_, f_, cell, ALU.mult).then_inc(fc_done, 1)
                                if prev:
                                    finish(prev)
                                dve.wait_ge(gate_sb, ts.g + 3)
                                dve.tensor_tensor(i_, i_, g_, ALU.mult).then_inc(ig_done, 1)
                                dve.wait_ge(fc_done, ts.l + 1)
                                dve.wait_ge(ig_done, ts.l + 1)
                                dve.tensor_tensor(cell, f_, i_, ALU.add).then_inc(cell_done, 1)
                            else:
                                dve.wait_ge(gate_sb, ts.g + 2)
                                dve.tensor_tensor(cell, i_, g_, ALU.mult).then_inc(cell_done, 1)
                                if prev:
                                    finish(prev)
                        over(dve, visit, finish)

                    @block.gpsimd
                    def _(pool):
                        def visit(ts, prev):
                            pool.wait_ge(hi_done, ts.n + 1)
                            h = cols(G[:, ts.slot, O, :], ts)
                            if ts.ends:
                                pool.tensor_tensor(ts.windows(H_lo), h.rearrange("p (b w) -> p b w", b=TILE_B[ts.pi]),
                                                   ts.windows(H_hi).bitcast(F32), ALU.subtract).then_inc(lo_done, 1)
                            else:
                                pool.tensor_tensor(cols(S_lo[:, ts.place, :], ts), h, cols(S_hi[:, ts.place, :], ts).bitcast(F32), ALU.subtract).then_inc(lo_done, 1)
                        over(pool, visit, lambda ts: None)

            l3 = Scope(nc)
            l3.__enter__()
            V_hi, V_lo = H_hi, H_lo
            att = l3.sb("att", [P, EC, NB * HEADS])
            soft_buf = SoftmaxBuffers(l3)
            sT = l3.sb("sT", [BH, 2, NE])
            s_out = [l3.sem(f"s_out{i}") for i in range(2)]
            soft_tables = (l3.ps("pSoft"), score_rows, log_adj, restart, last_of, same, ident, att)
            with Scope(nc) as sc:
                hs = sc.sb("hs", [P, 2, TB, P])
                z2 = sc.sb("z2", [P, 2, TB, P])
                x3 = sc.sb("x3", [P, 2, TB, P])
                x3T_hi = sc.sb("x3T_hi", [P, 2, TB, P], F32R)
                x3T_lo = sc.sb("x3T_lo", [P, 2, TB, P], F32R)
                x3l_done = sc.sem("x3l_done")
                Q_hi = sc.sb("Q_hi", [P, 2, TB, P], F32R)
                Q_lo = sc.sb("Q_lo", [P, 2, TB, P], F32R)
                V = sc.sb("V", [P, 2, TB, P])
                L = sc.sb("L", [P, 2, 2, TC])
                n2 = Norm(sc, "n2", eps[:, 0:1])
                pT = sc.ps("pT")
                pX = sc.ps("pX")
                pQV = [sc.ps(f"pQV{i}") for i in range(2)]
                pE = [sc.ps(f"pE{i}") for i in range(2)]
                pS = sc.ps("pS")
                hs_done, tr_done, z_done, x3_done, kept, trx_done, x3T_done, qv_ps, qv_copied, q_lo, v_lo, e_ps, zs_done, l_done, s_ps, s_sb = (
                    sc.sem(n) for n in ("hs_done", "tr_done_f", "z_done_f", "x3_done", "kept", "trx_done", "x3T_done", "qv_ps", "qv_copied", "q_lo",
                                        "v_lo", "e_ps", "zs_done", "l_done", "s_ps", "s_sb"))
                soft = Softmax(0, soft_buf, *soft_tables)

                with nc.Block() as block:
                    @block.gpsimd
                    def _(pool):
                        def whole(t, s, j):
                            if late(t):
                                pool.wait_ge(tr_done, t - 1)
                            tl = ds(t * TB, TB)
                            pool.tensor_tensor(hs[:, s, :, :], H_hi[:, tl, :].bitcast(F32), H_lo[:, tl, :].bitcast(F32), ALU.add).then_inc(hs_done, 1)

                        def keep(t, s, j):
                            pool.wait_ge(x3_done, TB * t + TB)
                            pool.tensor_copy(XS[:, ds(t * TB, TB), :], x3[:, s, :, :]).then_inc(kept, 1)

                        def v_low(t, s, j):
                            pool.wait_ge(qv_copied, 2 * t + 2)
                            tl = ds(t * TB, TB)
                            pool.tensor_tensor(V_lo[:, tl, :], V[:, s, :, :], V_hi[:, tl, :].bitcast(F32), ALU.subtract).then_inc(v_lo, 1)
                        pipeline(pool, NT, [(0, whole), (4, v_low), (2, keep)])

                    @block.tensor
                    def _(pe):
                        def turn(t, s, j):
                            pe.wait_ge(hs_done, t + 1)
                            if late(t):
                                pe.wait_ge(z_done, t)
                            elif t:
                                pe.wait_ge(z_done, 1)
                            for b in range(TB):
                                ins = pe.transpose(pT[:, P * b:P * b + P], hs[:, s, b, :], ident[:, :])
                            ins.then_inc(tr_done, 1)

                        def turn_x(t, s, j):
                            if late(t):
                                pe.wait_ge(x3l_done, t)
                            elif t:
                                pe.wait_ge(x3l_done, 1)
                            for b in range(TB):
                                pe.wait_ge(x3_done, TB * t + b + 1)
                                ins = pe.transpose(pX[:, P * b:P * b + P], x3[:, s, b, :], ident[:, :])
                            ins.then_inc(trx_done, 1)

                        def project(t, s, j):
                            pe.wait_ge(x3l_done, t + 1)
                            for q in range(2):
                                if late(t) or t:
                                    pe.wait_ge(q_lo, 2 * t + q - 1)
                                for b in (0, 1):
                                    of_b = pQV[q][:, 2 * P * b:2 * P * b + 2 * P]
                                    pe.matmul(of_b, x3T_hi[:, s, 2 * q + b, :], WQV_hi[:, :], start=True, stop=False)
                                    pe.matmul(of_b, x3T_hi[:, s, 2 * q + b, :], WQV_lo[:, :], start=False, stop=False)
                                    ins = pe.matmul(of_b, x3T_lo[:, s, 2 * q + b, :], WQV_hi[:, :], start=False, stop=True)
                                ins.then_inc(qv_ps, 1)

                        def gather(t, s, j):
                            for q in range(2):
                                pe.wait_ge(q_lo, 2 * t + q + 1)
                                if late(t) or t:
                                    pe.wait_ge(l_done, 2 * t + q - 1)
                                for b in (0, 1):
                                    for i, part in enumerate((Q_hi, Q_lo)):
                                        ins = pe.matmul(pE[q][:, NE * b:NE * b + NE], part[:, s, 2 * q + b, :], srcdstT[:, :], start=(i == 0), stop=(i == 1))
                                ins.then_inc(e_ps, 1)

                        def score(t, s, j):
                            if late(t):
                                pe.wait_ge(s_sb, t)
                            elif t:
                                pe.wait_ge(s_sb, 1)
                            for q in range(2):
                                pe.wait_ge(l_done, 2 * t + q + 1)
                                for b in (0, 1):
                                    u = 2 * q + b
                                    ins = pe.matmul(pS[0:BH, 0:NE], a_heads[:, u, :], L[:, s, q, NE * b:NE * b + NE], start=(u == 0), stop=(u == TB - 1))
                            ins.then_inc(s_ps, 1)
                        pipeline(pe, NT, [(1, turn), (4, gather), (2, turn_x), (3, project), (5, score),
                                           (5, at_tiles({13: lambda: soft.turn(pe), 14: lambda: soft.maximum(pe)}))])

                    @block.scalar
                    def _(act):
                        def root(t, s, j):
                            n2.root(act, t, s)

                        def apply2(t, s, j):
                            if late(t):
                                act.wait_ge(kept, t - 1)
                                act.wait_ge(trx_done, t - 1)
                            n2.apply_act(act, z2[:, s, :, :], x3[:, s, :, :], t, s, x3_done)

                        def copy_x(t, s, j):
                            act.wait_ge(trx_done, t + 1)
                            if late(t):
                                act.wait_ge(qv_ps, 2 * t - 2)
                            act.copy(x3T_hi[:, s, :, :], pX[:, :].rearrange("p (b d) -> p b d", b=TB)).then_inc(x3T_done, 1)

                        def high(t, s, j):
                            if late(t):
                                act.wait_ge(v_lo, t - 1)
                            for q in range(2):
                                act.wait_ge(qv_ps, 2 * t + q + 1)
                                if late(t):
                                    act.wait_ge(e_ps, 2 * t + q - 3)
                                both = pQV[q][:, :].rearrange("p (b v d) -> p b v d", b=2, v=2)
                                act.copy(Q_hi[:, s, 2 * q:2 * q + 2, :], both[:, :, 0, :])
                                act.copy(V[:, s, 2 * q:2 * q + 2, :], both[:, :, 1, :])
                                act.copy(V_hi[:, ds(t * TB + 2 * q, 2), :], both[:, :, 1, :]).then_inc(qv_copied, 1)

                        def scale(t, s, j):
                            for q in range(2):
                                act.wait_ge(e_ps, 2 * t + q + 1)
                                if late(t):
                                    act.wait_ge(s_ps, t - 1)
                                act.mul(L[:, s, q, :], pE[q][:, :], SLOPE).then_inc(zs_done, 1)

                        def copy_s(t, s, j):
                            act.wait_ge(s_ps, t + 1)
                            if late(t):
                                act.wait_ge(s_out[s], 16 * j)
                            act.copy(sT[:, s, :], pS[0:BH, 0:NE]).then_inc(s_sb, 1)
                        pipeline(act, NT, [(4, scale), (1, root), (2, copy_x), (3, high), (1, apply2), (5, copy_s), (5, at_tiles({15: lambda: soft.exp(act)}))])

                    @block.vector
                    def _(dve):
                        def stats2(t, s, j):
                            tl = ds(t * TB, TB)
                            dve.wait_ge(tr_done, t + 1)
                            if late(t):
                                dve.wait_ge(x3_done, TB * t - TB)
                            dve.tensor_tensor(z2[:, s, :, :], pT[:, :].rearrange("p (b d) -> p b d", b=TB), XS[:, tl, :], ALU.add).then_inc(z_done, 1)
                            dve.wait_ge(z_done, t + 1)
                            n2.stats(dve, z2[:, s, :, :], t, s)

                        def shift2(t, s, j):
                            n2.shift(dve, t, s)

                        def x_low(t, s, j):
                            dve.wait_ge(x3T_done, t + 1)
                            dve.tensor_tensor(x3T_lo[:, s, :, :], pX[:, :].rearrange("p (b d) -> p b d", b=TB), x3T_hi[:, s, :, :].bitcast(F32), ALU.subtract).then_inc(x3l_done, 1)

                        def low(t, s, j):
                            for q in range(2):
                                both = pQV[q][:, :].rearrange("p (b v d) -> p b v d", b=2, v=2)
                                dve.wait_ge(qv_copied, 2 * t + q + 1)
                                dve.tensor_tensor(Q_lo[:, s, 2 * q:2 * q + 2, :], both[:, :, 0, :], Q_hi[:, s, 2 * q:2 * q + 2, :].bitcast(F32), ALU.subtract).then_inc(q_lo, 1)

                        def leaky(t, s, j):
                            for q in range(2):
                                dve.wait_ge(zs_done, 2 * t + q + 1)
                                dve.tensor_tensor(L[:, s, q, :], pE[q][:, :], L[:, s, q, :], ALU.max).then_inc(l_done, 1)
                        pipeline(dve, NT, [(1, stats2), (4, leaky), (1, shift2), (2, x_low), (3, low),
                                            (5, at_tiles({12: lambda: soft.scan(dve), 14: lambda: soft.copy(dve), 15: lambda: soft.subtract(dve)}))])

                    @block.sync
                    def _(sp):
                        def store(t, s, j):
                            sp.wait_ge(s_sb, t + 1)
                            sp.dma_start(score_rows[ds(t, 1), :, :].rearrange("o r e -> (o r) e"), sT[:, s, :]).then_inc(s_out[s], 16)

                        def load_half():
                            for i in range(2):
                                sp.wait_ge(s_out[i], 16 * (NT // 4))
                            soft.load(sp)
                        pipeline(sp, NT, [(5, at_tiles({11: load_half})), (5, store)])

            with Scope(nc) as sc:
                pr = sc.sb("pr", [P, 2, EC, TB, P])
                yT = sc.sb("yT_h", [P, 2, TB, P])
                z3 = sc.sb("z3", [P, 2, TB, P])
                os_ = sc.sb("os_", [P, 2, TB, P])
                n3 = Norm(sc, "n3", eps[:, 0:1])
                pVg = [[sc.ps(f"pVg{i}{c}") for c in range(EC)] for i in range(2)]
                pY = [sc.ps(f"pY{i}") for i in range(2)]
                pZ = sc.ps("pZ")
                soft = Softmax(1, soft_buf, *soft_tables)
                soft_before = Softmax(0, soft_buf, *soft_tables)
                vg_ps, pr_done, y_ps, y_sb, o_ps, z_done, o_done = (
                    sc.sem(n) for n in ("vg_ps", "pr_done", "y_ps", "y_sb", "o_ps", "z_done_h", "o_done"))
                o_out = [sc.sem(f"o_out{i}") for i in range(2)]
                with nc.Block() as block:
                    @block.tensor
                    def _(pe):
                        def gather(t, s, j):
                            for c in range(EC):
                                if late(t):
                                    pe.wait_ge(pr_done, EC * t + c - 3)
                                for i, part in enumerate((V_hi, V_lo)):
                                    ins = pe.matmul(pVg[s][c][:, :], dstT[:, P * c:P * c + P], part[:, ds(t * TB, TB), :], start=(i == 0), stop=(i == 1))
                                ins.then_inc(vg_ps, 1)

                        def combine(t, s, j):
                            pe.wait_ge(pr_done, EC * t + EC)
                            if late(t):
                                pe.wait_ge(y_sb, t - 1)
                            for b in range(TB):
                                for c in range(EC):
                                    ins = pe.matmul(pY[s][:, P * b:P * b + P], pr[:, s, c, b, :], src1h[:, c, :], start=(c == 0), stop=(c == EC - 1))
                            ins.then_inc(y_ps, 1)

                        def output(t, s, j):
                            pe.wait_ge(y_sb, t + 1)
                            if late(t):
                                pe.wait_ge(z_done, t)
                            elif t:
                                pe.wait_ge(z_done, 1)
                            for b in range(TB):
                                ins = pe.matmul(pZ[:, P * b:P * b + P], yT[:, s, b, :], WoT[:, :], start=True, stop=True)
                            ins.then_inc(o_ps, 1)
                        pipeline(pe, NT, [(0, at_tiles({0: lambda: soft_before.total(pe)})), (0, gather), (1, combine), (2, output),
                                          (0, at_tiles({1: lambda: soft.turn(pe), 3: lambda: soft.maximum(pe), 5: lambda: soft.total(pe)}))], straight=8)

                    @block.scalar
                    def _(act):
                        def copy_y(t, s, j):
                            act.wait_ge(y_ps, t + 1)
                            if late(t):
                                act.wait_ge(o_ps, t - 1)
                            act.copy(yT[:, s, :, :], pY[s][:, :].rearrange("p (b d) -> p b d", b=TB)).then_inc(y_sb, 1)

                        def root(t, s, j):
                            n3.root(act, t, s)

                        def apply3(t, s, j):
                            if late(t):
                                act.wait_ge(o_out[s], 16 * j)
                            n3.apply_act(act, z3[:, s, :, :], os_[:, s, :, :], t, s, o_done)
                        pipeline(act, NT, [(1, copy_y), (3, apply3), (2, root), (0, at_tiles({4: lambda: soft.exp(act)}))], straight=8)

                    @block.vector
                    def _(dve):
                        def weigh(t, s, j):
                            for c in range(EC):
                                dve.wait_ge(vg_ps, EC * t + c + 1)
                                if late(t):
                                    dve.wait_ge(y_ps, t - 1)
                                dve.tensor_tensor(pr[:, s, c, :, :].rearrange("p b (h d) -> p (b h) d", h=HEADS),
                                                  pVg[s][c][:, :].rearrange("p (r d) -> p r d", d=HD),
                                                  att[:, c, ds(t * BH, BH)].unsqueeze(2).broadcast_to([P, BH, HD]), ALU.mult).then_inc(pr_done, 1)

                        def stats3(t, s, j):
                            dve.wait_ge(o_ps, t + 1)
                            if late(t):
                                dve.wait_ge(o_done, TB * t - TB)
                            dve.tensor_tensor(z3[:, s, :, :], pZ[:, :].rearrange("p (b d) -> p b d", b=TB), XS[:, ds(t * TB, TB), :], ALU.add).then_inc(z_done, 1)
                            dve.wait_ge(z_done, t + 1)
                            n3.stats(dve, z3[:, s, :, :], t, s)

                        def shift3(t, s, j):
                            n3.shift(dve, t, s)
                        soft_before.divide(dve)
                        pipeline(dve, NT, [(0, weigh), (3, shift3), (2, stats3),
                                           (0, at_tiles({0: lambda: soft.scan(dve), 2: lambda: soft.copy(dve), 4: lambda: soft.subtract(dve), 6: lambda: soft.divide(dve)}))], straight=8)

                    @block.sync
                    def _(sp):
                        def store(t, s, j):
                            sp.wait_ge(o_done, TB * t + TB)
                            sp.dma_start(out_tiles[:, ds(t, 1), :, :].rearrange("n o b d -> n (o b) d"), os_[:, s, :, :]).then_inc(o_out[s], 16)
                        for i in range(2):
                            sp.wait_ge(s_out[i], 16 * (NT // 2))
                        soft.load(sp)
                        pipeline(sp, NT, [(0, store)])
                        for s in range(2):
                            sp.wait_ge(o_out[s], 16 * (NT // 2))
            l3.__exit__(None, None, None)


_INS = ['x', 'adj', 'L0_gnn_W1', 'L0_gnn_b1', 'L0_gnn_g1', 'L0_gnn_be1', 'L0_gnn_W2', 'L0_gnn_b2', 'L0_gnn_g2',
        'L0_gnn_be2', 'L1_gnn_W', 'L1_gnn_bias', 'L2_gnn_Wg0', 'L2_gnn_bg0', 'L2_gnn_Wg1', 'L2_gnn_bg1', 'L2_gnn_Wih',
        'L2_gnn_Whh', 'L2_gnn_bih', 'L2_gnn_bhh', 'L3_gnn_W_lin', 'L3_gnn_W_val', 'L3_gnn_a', 'L3_gnn_W_out',
        'L3_gnn_src', 'L3_gnn_dst']


def kernel(**inputs):
    import numpy as _np
    import concourse.bacc as _bacc
    from concourse import mybir as _mybir
    from concourse.bass_utils import run_bass_kernel_spmd as _run

    nc = _bacc.Bacc("TRN2", target_bir_lowering=False, num_devices=1)
    arrays, args = {}, []
    for name in _INS:
        a = _np.ascontiguousarray(inputs[name])
        arrays[f"in_{name}_dram"] = a
        args.append(nc.dram_tensor(f"in_{name}_dram", a.shape, _mybir.dt.from_np(a.dtype), kind="ExternalInput").ap())
    args.append(nc.dram_tensor("out_dram", (NB, P, P), F32, kind="ExternalOutput").ap())
    adj_resnorm_kernel(nc, *args)
    r = _run(nc, [arrays], core_ids=[0])
    return r.results[0]["out_dram"]
```
